# Optimizing a Trainium2 kernel written in Bass

```python
import numpy as np
import jax
import jax.numpy as jnp

def _softmax(x, axis=-1):
    return jax.nn.softmax(x, axis=axis)

def _gelu(x):
    return jax.nn.gelu(x, approximate=True)

def _silu(x):
    return jax.nn.silu(x)

def _sigmoid(x):
    return jax.nn.sigmoid(x)

def _layernorm(x, axis=-1, eps=1e-05):
    m = jnp.mean(x, axis=axis, keepdims=True)
    v = jnp.var(x, axis=axis, keepdims=True)
    return (x - m) / jnp.sqrt(v + eps)

def _scatter_add(tgt, idx, src, axis=0):
    return tgt.at[idx].add(src)

def _segment_sum(src, seg, n):
    return jax.ops.segment_sum(src, seg, n)
kernel_name = 'mk_sandwich_d4_jaxref_r8_cb0696'

def setup_inputs(seed: int=0):
    np.random.seed(seed)
    _w = jnp.asarray

    def _L0_attn_setup():
        import jax, jax.numpy as jnp
        import numpy as np
        N_HEADS = 16
        SCALE = 8.0
        key = jax.random.key(seed)
        k1, k2, k3, k4 = jax.random.split(key, 4)
        b, n, d_model, inner = (8, 256, 128, 128)
        x = jax.random.normal(k1, (b, n, d_model), dtype=jnp.float32)
        Wqkv = jax.random.normal(k2, (3 * inner, d_model), dtype=jnp.float32) * (1.0 / np.sqrt(d_model))
        Wproj = jax.random.normal(k3, (d_model, inner), dtype=jnp.float32) * (1.0 / np.sqrt(inner))
        bproj = jax.random.normal(k4, (d_model,), dtype=jnp.float32) * 0.01
        return {'x': x, 'Wqkv': Wqkv, 'Wproj': Wproj, 'bproj': bproj}
    _L0_attn_in = _L0_attn_setup()

    def _L0_ffn_setup():
        import jax, jax.numpy as jnp
        import numpy as np
        EPS = 1e-05

        def _layernorm(x, w, b):
            mu = jnp.mean(x, axis=-1, keepdims=True)
            var = jnp.mean((x - mu) ** 2, axis=-1, keepdims=True)
            return (x - mu) * jax.lax.rsqrt(var + EPS) * w + b

        def _rope_tables(T, D, base=10000.0):
            inv_freq = 1.0 / base ** (jnp.arange(0, D, 2, dtype=jnp.float32) / D)
            t = jnp.arange(T, dtype=jnp.float32)
            freqs = jnp.einsum('i,j->ij', t, inv_freq)
            emb = jnp.concatenate([freqs, freqs], axis=-1)
            return (jnp.cos(emb), jnp.sin(emb))

        def _rotate_half(x):
            x1, x2 = (x[..., :x.shape[-1] // 2], x[..., x.shape[-1] // 2:])
            return jnp.concatenate([-x2, x1], axis=-1)

        def _attn(x, ln_w, ln_b, conv_w, attn_w, proj_w, n_head):
            B, T, C = x.shape
            D = C // n_head
            h = _layernorm(x, ln_w, ln_b)
            hc = jnp.transpose(h, (0, 2, 1))
            hc = jnp.pad(hc, ((0, 0), (0, 0), (2, 0)))
            hc = jax.lax.conv_general_dilated(hc, conv_w, window_strides=(1,), padding='VALID', dimension_numbers=('NCH', 'OIH', 'NCH'), feature_group_count=C)
            h = jnp.transpose(hc, (0, 2, 1))
            qkv = h @ attn_w
            q, k, v = jnp.split(qkv, 3, axis=-1)
            q = q.reshape(B, T, n_head, D)
            k = k.reshape(B, T, n_head, D)
            v = v.reshape(B, T, n_head, D)
            cos, sin = _rope_tables(T, D)
            cos = cos[None, :, None, :]
            sin = sin[None, :, None, :]
            q = q * cos + _rotate_half(q) * sin
            k = k * cos + _rotate_half(k) * sin
            scores = jnp.einsum('bqhd,bkhd->bhqk', q, k) / jnp.sqrt(jnp.float32(D))
            causal = jnp.tril(jnp.ones((T, T), dtype=bool))
            scores = jnp.where(causal, scores, jnp.float32(-1e+30))
            p = jax.nn.softmax(scores, axis=-1)
            y = jnp.einsum('bhqk,bkhd->bqhd', p, v).reshape(B, T, C)
            return y @ proj_w

        def _moe(x, ln_w, ln_b, router_w, expert_wv, expert_proj):
            h = _layernorm(x, ln_w, ln_b)
            logits = h @ router_w
            expert_idx = jnp.argmax(logits, axis=-1)
            E = router_w.shape[-1]
            out = jnp.zeros_like(x)
            for e in range(E):
                gv = h @ expert_wv[e]
                gate_raw, value = jnp.split(gv, 2, axis=-1)
                y = gate_raw * jax.nn.sigmoid(gate_raw) * value @ expert_proj[e]
                out = out + jnp.where((expert_idx == e)[..., None], y, 0.0)
            return out
        C, H, E, B, T = (128, 16, 4, 4, 128)
        Dff = 4 * C
        key = jax.random.key(seed)
        ks = jax.random.split(key, 8)
        s = 0.02
        return {'x': jax.random.normal(ks[0], (B, T, C), dtype=jnp.float32), 'ln1_w': jnp.ones((C,), jnp.float32), 'ln1_b': jnp.zeros((C,), jnp.float32), 'ln2_w': jnp.ones((C,), jnp.float32), 'ln2_b': jnp.zeros((C,), jnp.float32), 'conv_w': jax.random.normal(ks[1], (C, 1, 3), dtype=jnp.float32) * 0.1, 'attn_w': jax.random.normal(ks[2], (C, 3 * C), dtype=jnp.float32) * s, 'proj_w': jax.random.normal(ks[3], (C, C), dtype=jnp.float32) * s, 'router_w': jax.random.normal(ks[4], (C, E), dtype=jnp.float32) * s, 'expert_wv': jax.random.normal(ks[5], (E, C, 2 * Dff), dtype=jnp.float32) * s, 'expert_proj': jax.random.normal(ks[6], (E, Dff, C), dtype=jnp.float32) * s}
    _L0_ffn_in = _L0_ffn_setup()

    def _L1_attn_setup():
        import jax, jax.numpy as jnp
        import numpy as np
        from jax import lax
        B, T, H = (4, 512, 128)
        K = 32

        def _causal_dw_conv(v, w, b):
            c = v.shape[1]
            k = w.shape[-1]
            y = lax.conv_general_dilated(v, w, window_strides=(1,), padding=[(k - 1, 0)], dimension_numbers=('NCH', 'OIH', 'NCH'), feature_group_count=c)
            return y + b[None, :, None]
        key = jax.random.key(seed)
        ks = jax.random.split(key, 9)
        s_in = 1.0 / np.sqrt(H)
        s_dw = 1.0 / np.sqrt(K)
        s_out = 1.0 / np.sqrt(2 * H)
        return {'x': jax.random.normal(ks[0], (B, T, H), jnp.float32), 'w_in': jax.random.normal(ks[1], (2 * H, H), jnp.float32) * s_in, 'b_in': jax.random.normal(ks[2], (2 * H,), jnp.float32) * s_in, 'w_a': jax.random.normal(ks[3], (H, 1, K), jnp.float32) * s_dw, 'b_a': jax.random.normal(ks[4], (H,), jnp.float32) * s_dw, 'w_b': jax.random.normal(ks[5], (H, 1, K), jnp.float32) * s_dw, 'b_b': jax.random.normal(ks[6], (H,), jnp.float32) * s_dw, 'w_out': jax.random.normal(ks[7], (H, 2 * H), jnp.float32) * s_out, 'b_out': jax.random.normal(ks[8], (H,), jnp.float32) * s_out}
    _L1_attn_in = _L1_attn_setup()

    def _L1_ffn_setup():
        import jax, jax.numpy as jnp
        import numpy as np
        import math
        BETA = 0.9
        THRESHOLD = 1.0
        NUM_STEPS = 5
        ALPHA = 2.0

        @jax.custom_vjp
        def spike_fn(u):
            return (u > 0).astype(u.dtype)

        def _spike_fwd(u):
            return (spike_fn(u), u)

        def _spike_bwd(u, g):
            s = jnp.pi / 2.0 * ALPHA * u
            return (g * (ALPHA / 2.0) / (1.0 + s * s),)
        spike_fn.defvjp(_spike_fwd, _spike_bwd)
        key = jax.random.key(seed)
        k1, k2, k3 = jax.random.split(key, 3)
        n_embd = 128
        x = jax.random.normal(k1, (4, 256, n_embd), dtype=jnp.float32)
        W_fc = jax.random.normal(k2, (4 * n_embd, n_embd), dtype=jnp.float32) / math.sqrt(n_embd)
        W_proj = jax.random.normal(k3, (n_embd, 4 * n_embd), dtype=jnp.float32) / math.sqrt(4 * n_embd)
        return {'x': x, 'W_fc': W_fc, 'W_proj': W_proj}
    _L1_ffn_in = _L1_ffn_setup()

    def _L2_attn_setup():
        import jax, jax.numpy as jnp
        import numpy as np
        B, T, C = (2, 256, 128)
        H = 16
        D = C // H
        HID = C // 4
        FF = 4 * C

        def _rms_norm(x):
            eps = jnp.finfo(x.dtype).eps
            return x * jax.lax.rsqrt(jnp.mean(jnp.square(x), axis=-1, keepdims=True) + eps)
        key = jax.random.key(seed)
        ks = jax.random.split(key, 11)
        s = lambda fan_in: 1.0 / np.sqrt(fan_in)
        inp = {'x': jax.random.normal(ks[0], (B, T, C), jnp.float32), 'Wq': jax.random.uniform(ks[1], (C, C), jnp.float32, -s(C), s(C)), 'Wk': jax.random.uniform(ks[2], (C, C), jnp.float32, -s(C), s(C)), 'Wv': jax.random.uniform(ks[3], (C, C), jnp.float32, -s(C), s(C)), 'Wm1': jax.random.uniform(ks[4], (HID, C), jnp.float32, -s(C), s(C)), 'bm1': jax.random.uniform(ks[5], (HID,), jnp.float32, -s(C), s(C)), 'Wm2': jax.random.uniform(ks[6], (H, HID), jnp.float32, -s(HID), s(HID)), 'bm2': jax.random.uniform(ks[7], (H,), jnp.float32, -s(HID), s(HID)), 'Wproj': jax.random.uniform(ks[8], (C, C), jnp.float32, -s(C), s(C)), 'Wfc': jax.random.uniform(ks[9], (FF, C), jnp.float32, -s(C), s(C)), 'Wcp': jax.random.uniform(ks[10], (C, FF), jnp.float32, -s(FF), s(FF))}
        return inp
    _L2_attn_in = _L2_attn_setup()

    def _L2_ffn_setup():
        import jax, jax.numpy as jnp
        import numpy as np
        DIM = 128

        def _reference_tuple_inner(x, W_r, W_k, W_v, mu_r, mu_k):
            B, T, C = x.shape
            x_prev = jnp.concatenate([jnp.zeros((B, 1, C), x.dtype), x[:, :-1, :]], axis=1)
            xr = mu_r * x + (1.0 - mu_r) * x_prev
            xk = mu_k * x + (1.0 - mu_k) * x_prev
            r = jax.nn.sigmoid(jnp.einsum('btc,dc->btd', xr, W_r))
            k = jnp.einsum('btc,dc->btd', xk, W_k)
            k_act = jnp.square(jax.nn.relu(k))
            out = r * jnp.einsum('btc,dc->btd', k_act, W_v)
            new_state = x[:, -1, :]
            return (out, new_state)
        key = jax.random.key(seed)
        ks = jax.random.split(key, 6)
        B, T, C = (8, 256, DIM)
        x = jax.random.normal(ks[0], (B, T, C), dtype=jnp.float32)
        s = 1.0 / np.sqrt(C)
        W_r = jax.random.uniform(ks[1], (C, C), jnp.float32, -s, s)
        W_k = jax.random.uniform(ks[2], (C, C), jnp.float32, -s, s)
        W_v = jax.random.uniform(ks[3], (C, C), jnp.float32, -s, s)
        mu_r = jax.random.uniform(ks[4], (C,), jnp.float32)
        mu_k = jax.random.uniform(ks[5], (C,), jnp.float32)
        return {'x': x, 'W_r': W_r, 'W_k': W_k, 'W_v': W_v, 'mu_r': mu_r, 'mu_k': mu_k}
    _L2_ffn_in = _L2_ffn_setup()

    def _L3_attn_setup():
        import jax, jax.numpy as jnp
        import numpy as np
        LR = 0.001

        def _mlp(params, h):
            W1, b1, W2, b2 = params
            return jax.nn.silu(h @ W1 + b1) @ W2 + b2
        key = jax.random.key(seed)
        ks = jax.random.split(key, 6)
        B, S, D = (8, 256, 128)
        sc = 1.0 / np.sqrt(D)
        x = jax.random.normal(ks[0], (B, S, D), dtype=jnp.float32)
        W_Q = jax.random.normal(ks[1], (D, D), dtype=jnp.float32) * sc
        W_KV = jax.random.normal(ks[2], (D, 2 * D), dtype=jnp.float32) * sc
        W1 = jax.random.normal(ks[3], (D, D), dtype=jnp.float32) * sc
        b1 = jnp.zeros((D,), dtype=jnp.float32)
        W2 = jax.random.normal(ks[4], (D, D), dtype=jnp.float32) * sc
        b2 = jnp.zeros((D,), dtype=jnp.float32)
        return {'x': x, 'W_Q': W_Q, 'W_KV': W_KV, 'W1': W1, 'b1': b1, 'W2': W2, 'b2': b2}
    _L3_attn_in = _L3_attn_setup()

    def _L3_ffn_setup():
        import jax, jax.numpy as jnp
        import numpy as np
        B, S, D = (4, 256, 128)
        N_EXPERTS, EXPERT_SIZE = (16, 32)
        WIDTH = N_EXPERTS * EXPERT_SIZE
        key = jax.random.key(seed)
        k_x, k_w1, k_w2, k_g = jax.random.split(key, 4)
        x = jax.random.normal(k_x, (B, S, D), dtype=jnp.float32)
        w1 = jax.random.normal(k_w1, (D, WIDTH), dtype=jnp.float32) / np.sqrt(D).astype(np.float32)
        b1 = jnp.zeros((WIDTH,), dtype=jnp.float32)
        w2 = jax.random.normal(k_w2, (WIDTH, D), dtype=jnp.float32) / np.sqrt(WIDTH).astype(np.float32)
        b2 = jnp.zeros((D,), dtype=jnp.float32)
        return {'x': x, 'w1': w1, 'b1': b1, 'w2': w2, 'b2': b2}
    _L3_ffn_in = _L3_ffn_setup()
    _d = {'L0_attn_x': _L0_attn_in['x'], 'L0_attn_Wqkv': _L0_attn_in['Wqkv'], 'L0_attn_Wproj': _L0_attn_in['Wproj'], 'L0_attn_bproj': _L0_attn_in['bproj'], 'L0_ffn_ln1_w': _L0_ffn_in['ln1_w'], 'L0_ffn_ln1_b': _L0_ffn_in['ln1_b'], 'L0_ffn_ln2_w': _L0_ffn_in['ln2_w'], 'L0_ffn_ln2_b': _L0_ffn_in['ln2_b'], 'L0_ffn_conv_w': _L0_ffn_in['conv_w'], 'L0_ffn_attn_w': _L0_ffn_in['attn_w'], 'L0_ffn_proj_w': _L0_ffn_in['proj_w'], 'L0_ffn_router_w': _L0_ffn_in['router_w'], 'L0_ffn_expert_wv': _L0_ffn_in['expert_wv'], 'L0_ffn_expert_proj': _L0_ffn_in['expert_proj'], 'L1_attn_w_in': _L1_attn_in['w_in'], 'L1_attn_b_in': _L1_attn_in['b_in'], 'L1_attn_w_a': _L1_attn_in['w_a'], 'L1_attn_b_a': _L1_attn_in['b_a'], 'L1_attn_w_b': _L1_attn_in['w_b'], 'L1_attn_b_b': _L1_attn_in['b_b'], 'L1_attn_w_out': _L1_attn_in['w_out'], 'L1_attn_b_out': _L1_attn_in['b_out'], 'L1_ffn_W_fc': _L1_ffn_in['W_fc'], 'L1_ffn_W_proj': _L1_ffn_in['W_proj'], 'L2_attn_Wq': _L2_attn_in['Wq'], 'L2_attn_Wk': _L2_attn_in['Wk'], 'L2_attn_Wv': _L2_attn_in['Wv'], 'L2_attn_Wm1': _L2_attn_in['Wm1'], 'L2_attn_bm1': _L2_attn_in['bm1'], 'L2_attn_Wm2': _L2_attn_in['Wm2'], 'L2_attn_bm2': _L2_attn_in['bm2'], 'L2_attn_Wproj': _L2_attn_in['Wproj'], 'L2_attn_Wfc': _L2_attn_in['Wfc'], 'L2_attn_Wcp': _L2_attn_in['Wcp'], 'L2_ffn_W_r': _L2_ffn_in['W_r'], 'L2_ffn_W_k': _L2_ffn_in['W_k'], 'L2_ffn_W_v': _L2_ffn_in['W_v'], 'L2_ffn_mu_r': _L2_ffn_in['mu_r'], 'L2_ffn_mu_k': _L2_ffn_in['mu_k'], 'L3_attn_W_Q': _L3_attn_in['W_Q'], 'L3_attn_W_KV': _L3_attn_in['W_KV'], 'L3_attn_W1': _L3_attn_in['W1'], 'L3_attn_b1': _L3_attn_in['b1'], 'L3_attn_W2': _L3_attn_in['W2'], 'L3_attn_b2': _L3_attn_in['b2'], 'L3_ffn_w1': _L3_ffn_in['w1'], 'L3_ffn_b1': _L3_ffn_in['b1'], 'L3_ffn_w2': _L3_ffn_in['w2'], 'L3_ffn_b2': _L3_ffn_in['b2']}
    _x0 = _d['L0_attn_x']
    _d['L0_attn_x'] = jax.random.normal(jax.random.fold_in(jax.random.key(seed), 1), (1, 2048, 128), dtype=_x0.dtype)
    del _x0
    return _d

def reference(L0_attn_x, L0_attn_Wqkv, L0_attn_Wproj, L0_attn_bproj, L0_ffn_ln1_w, L0_ffn_ln1_b, L0_ffn_ln2_w, L0_ffn_ln2_b, L0_ffn_conv_w, L0_ffn_attn_w, L0_ffn_proj_w, L0_ffn_router_w, L0_ffn_expert_wv, L0_ffn_expert_proj, L1_attn_w_in, L1_attn_b_in, L1_attn_w_a, L1_attn_b_a, L1_attn_w_b, L1_attn_b_b, L1_attn_w_out, L1_attn_b_out, L1_ffn_W_fc, L1_ffn_W_proj, L2_attn_Wq, L2_attn_Wk, L2_attn_Wv, L2_attn_Wm1, L2_attn_bm1, L2_attn_Wm2, L2_attn_bm2, L2_attn_Wproj, L2_attn_Wfc, L2_attn_Wcp, L2_ffn_W_r, L2_ffn_W_k, L2_ffn_W_v, L2_ffn_mu_r, L2_ffn_mu_k, L3_attn_W_Q, L3_attn_W_KV, L3_attn_W1, L3_attn_b1, L3_attn_W2, L3_attn_b2, L3_ffn_w1, L3_ffn_b1, L3_ffn_w2, L3_ffn_b2):

    def _L0_attn_ref(x, Wqkv, Wproj, bproj):
        import jax, jax.numpy as jnp
        import numpy as np
        N_HEADS = 16
        SCALE = 8.0
        b, n, _ = x.shape
        qkv = jnp.einsum('bnm,fm->bnf', x, Wqkv)
        qkv = qkv.reshape(b, n, N_HEADS, -1)
        dh = qkv.shape[3] // 3
        q, k, v = (qkv[..., :dh], qkv[..., dh:2 * dh], qkv[..., 2 * dh:])
        scores = jnp.einsum('bnhd,bngd->bnhg', q, k) / SCALE
        attn = jax.nn.softmax(scores, axis=-1)
        out = jnp.einsum('bnhg,bngd->bnhd', attn, v)
        out = out.reshape(b, n, -1)
        return jnp.einsum('bni,mi->bnm', out, Wproj) + bproj

    def _L0_ffn_ref(x, ln1_w, ln1_b, ln2_w, ln2_b, conv_w, attn_w, proj_w, router_w, expert_wv, expert_proj):
        import jax, jax.numpy as jnp
        import numpy as np
        EPS = 1e-05

        def _layernorm(x, w, b):
            mu = jnp.mean(x, axis=-1, keepdims=True)
            var = jnp.mean((x - mu) ** 2, axis=-1, keepdims=True)
            return (x - mu) * jax.lax.rsqrt(var + EPS) * w + b

        def _rope_tables(T, D, base=10000.0):
            inv_freq = 1.0 / base ** (jnp.arange(0, D, 2, dtype=jnp.float32) / D)
            t = jnp.arange(T, dtype=jnp.float32)
            freqs = jnp.einsum('i,j->ij', t, inv_freq)
            emb = jnp.concatenate([freqs, freqs], axis=-1)
            return (jnp.cos(emb), jnp.sin(emb))

        def _rotate_half(x):
            x1, x2 = (x[..., :x.shape[-1] // 2], x[..., x.shape[-1] // 2:])
            return jnp.concatenate([-x2, x1], axis=-1)

        def _attn(x, ln_w, ln_b, conv_w, attn_w, proj_w, n_head):
            B, T, C = x.shape
            D = C // n_head
            h = _layernorm(x, ln_w, ln_b)
            hc = jnp.transpose(h, (0, 2, 1))
            hc = jnp.pad(hc, ((0, 0), (0, 0), (2, 0)))
            hc = jax.lax.conv_general_dilated(hc, conv_w, window_strides=(1,), padding='VALID', dimension_numbers=('NCH', 'OIH', 'NCH'), feature_group_count=C)
            h = jnp.transpose(hc, (0, 2, 1))
            qkv = h @ attn_w
            q, k, v = jnp.split(qkv, 3, axis=-1)
            q = q.reshape(B, T, n_head, D)
            k = k.reshape(B, T, n_head, D)
            v = v.reshape(B, T, n_head, D)
            cos, sin = _rope_tables(T, D)
            cos = cos[None, :, None, :]
            sin = sin[None, :, None, :]
            q = q * cos + _rotate_half(q) * sin
            k = k * cos + _rotate_half(k) * sin
            scores = jnp.einsum('bqhd,bkhd->bhqk', q, k) / jnp.sqrt(jnp.float32(D))
            causal = jnp.tril(jnp.ones((T, T), dtype=bool))
            scores = jnp.where(causal, scores, jnp.float32(-1e+30))
            p = jax.nn.softmax(scores, axis=-1)
            y = jnp.einsum('bhqk,bkhd->bqhd', p, v).reshape(B, T, C)
            return y @ proj_w

        def _moe(x, ln_w, ln_b, router_w, expert_wv, expert_proj):
            h = _layernorm(x, ln_w, ln_b)
            logits = h @ router_w
            expert_idx = jnp.argmax(logits, axis=-1)
            E = router_w.shape[-1]
            out = jnp.zeros_like(x)
            for e in range(E):
                gv = h @ expert_wv[e]
                gate_raw, value = jnp.split(gv, 2, axis=-1)
                y = gate_raw * jax.nn.sigmoid(gate_raw) * value @ expert_proj[e]
                out = out + jnp.where((expert_idx == e)[..., None], y, 0.0)
            return out
        n_head = 16
        x = x + _attn(x, ln1_w, ln1_b, conv_w, attn_w, proj_w, n_head)
        x = x + _moe(x, ln2_w, ln2_b, router_w, expert_wv, expert_proj)
        return x

    def _L1_attn_ref(x, w_in, b_in, w_a, b_a, w_b, b_b, w_out, b_out):
        import jax, jax.numpy as jnp
        import numpy as np
        from jax import lax
        B, T, H = (4, 512, 128)
        K = 32

        def _causal_dw_conv(v, w, b):
            c = v.shape[1]
            k = w.shape[-1]
            y = lax.conv_general_dilated(v, w, window_strides=(1,), padding=[(k - 1, 0)], dimension_numbers=('NCH', 'OIH', 'NCH'), feature_group_count=c)
            return y + b[None, :, None]
        h = w_a.shape[0]
        z = jnp.einsum('bth,eh->bet', x, w_in) + b_in[None, :, None]
        za, zb = (z[:, :h, :], z[:, h:, :])
        ca = _causal_dw_conv(za, w_a, b_a)
        cb = _causal_dw_conv(zb, w_b, b_b)
        gated_a = ca * jax.nn.sigmoid(cb)
        gated_b = cb * jax.nn.sigmoid(ca)
        cat = jnp.concatenate([gated_a, gated_b], axis=1)
        return jnp.einsum('bet,he->bth', cat, w_out) + b_out[None, None, :]

    def _L1_ffn_ref(x, W_fc, W_proj):
        import jax, jax.numpy as jnp
        import numpy as np
        import math
        BETA = 0.9
        THRESHOLD = 1.0
        NUM_STEPS = 5
        ALPHA = 2.0

        @jax.custom_vjp
        def spike_fn(u):
            return (u > 0).astype(u.dtype)

        def _spike_fwd(u):
            return (spike_fn(u), u)

        def _spike_bwd(u, g):
            s = jnp.pi / 2.0 * ALPHA * u
            return (g * (ALPHA / 2.0) / (1.0 + s * s),)
        spike_fn.defvjp(_spike_fwd, _spike_bwd)
        h = jnp.square(jax.nn.relu(jnp.einsum('bsd,fd->bsf', x, W_fc)))
        y = jnp.einsum('bsf,df->bsd', h, W_proj)

        def step(mem, _):
            reset = jax.lax.stop_gradient(spike_fn(mem - THRESHOLD))
            mem_new = BETA * mem + y - reset * THRESHOLD
            spk = spike_fn(mem_new - THRESHOLD)
            return (mem_new, spk)
        mem0 = jnp.zeros_like(y)
        _, spks = jax.lax.scan(step, mem0, None, length=NUM_STEPS)
        return jnp.sum(spks, axis=0) / NUM_STEPS

    def _L2_attn_ref(x, Wq, Wk, Wv, Wm1, bm1, Wm2, bm2, Wproj, Wfc, Wcp):
        import jax, jax.numpy as jnp
        import numpy as np
        B, T, C = (2, 256, 128)
        H = 16
        D = C // H
        HID = C // 4
        FF = 4 * C

        def _rms_norm(x):
            eps = jnp.finfo(x.dtype).eps
            return x * jax.lax.rsqrt(jnp.mean(jnp.square(x), axis=-1, keepdims=True) + eps)
        b, t, c = x.shape
        h = Wm2.shape[0]
        d = c // h
        q = (x @ Wq.T).reshape(b, t, h, d)
        k = (x @ Wk.T).reshape(b, t, h, d)
        v = (x @ Wv.T).reshape(b, t, h, d)
        surprise = jax.nn.sigmoid(jnp.maximum(x @ Wm1.T + bm1, 0.0) @ Wm2.T + bm2)
        decay = 1.0 - surprise
        qT = jnp.transpose(q, (1, 0, 2, 3))
        kT = jnp.transpose(k, (1, 0, 2, 3))
        vT = jnp.transpose(v, (1, 0, 2, 3))
        dT = jnp.transpose(decay, (1, 0, 2))
        gT = jnp.transpose(surprise, (1, 0, 2))

        def step(state, inp):
            qt, kt, vt, dt, gt = inp
            state = state * dt[..., None, None] + gt[..., None, None] * (kt[..., :, None] * vt[..., None, :])
            yt = jnp.einsum('bhd,bhde->bhe', qt, state)
            return (state, yt)
        state0 = jnp.zeros((b, h, d, d), x.dtype)
        _, ys = jax.lax.scan(step, state0, (qT, kT, vT, dT, gT))
        y = jnp.transpose(ys, (1, 0, 2, 3)).reshape(b, t, c)
        y = y @ Wproj.T
        yn = _rms_norm(y)
        mlp = jnp.square(jnp.maximum(yn @ Wfc.T, 0.0)) @ Wcp.T
        return y + mlp

    def _L2_ffn_ref(x, W_r, W_k, W_v, mu_r, mu_k):
        import jax, jax.numpy as jnp
        import numpy as np
        DIM = 128

        def _reference_tuple_inner(x, W_r, W_k, W_v, mu_r, mu_k):
            B, T, C = x.shape
            x_prev = jnp.concatenate([jnp.zeros((B, 1, C), x.dtype), x[:, :-1, :]], axis=1)
            xr = mu_r * x + (1.0 - mu_r) * x_prev
            xk = mu_k * x + (1.0 - mu_k) * x_prev
            r = jax.nn.sigmoid(jnp.einsum('btc,dc->btd', xr, W_r))
            k = jnp.einsum('btc,dc->btd', xk, W_k)
            k_act = jnp.square(jax.nn.relu(k))
            out = r * jnp.einsum('btc,dc->btd', k_act, W_v)
            new_state = x[:, -1, :]
            return (out, new_state)
        return _reference_tuple_inner(x, W_r, W_k, W_v, mu_r, mu_k)[0]

    def _L3_attn_ref(x, W_Q, W_KV, W1, b1, W2, b2):
        import jax, jax.numpy as jnp
        import numpy as np
        LR = 0.001

        def _mlp(params, h):
            W1, b1, W2, b2 = params
            return jax.nn.silu(h @ W1 + b1) @ W2 + b2
        kv = x @ W_KV
        k, v = jnp.split(kv, 2, axis=-1)
        k = jnp.swapaxes(k, 0, 1)
        v = jnp.swapaxes(v, 0, 1)

        def loss_fn(params, k_t, v_t):
            return jnp.mean((_mlp(params, k_t) - v_t) ** 2)

        def step(params, kvt):
            k_t, v_t = kvt
            g = jax.grad(loss_fn)(params, k_t, v_t)
            new_params = tuple((p - LR * gp for p, gp in zip(params, g)))
            return (new_params, None)
        params, _ = jax.lax.scan(step, (W1, b1, W2, b2), (k, v))
        q = x @ W_Q
        return _mlp(params, q)

    def _L3_ffn_ref(x, w1, b1, w2, b2):
        import jax, jax.numpy as jnp
        import numpy as np
        B, S, D = (4, 256, 128)
        N_EXPERTS, EXPERT_SIZE = (16, 32)
        WIDTH = N_EXPERTS * EXPERT_SIZE
        h = jax.nn.relu(jnp.einsum('bsd,dw->bsw', x, w1) + b1)
        return jnp.einsum('bsw,wd->bsd', h, w2) + b2
    x = L0_attn_x
    x = x + _layernorm(_L0_attn_ref(_layernorm(x, axis=-1), L0_attn_Wqkv, L0_attn_Wproj, L0_attn_bproj), axis=-1)
    x = x + _layernorm(_L0_ffn_ref(_layernorm(x, axis=-1), L0_ffn_ln1_w, L0_ffn_ln1_b, L0_ffn_ln2_w, L0_ffn_ln2_b, L0_ffn_conv_w, L0_ffn_attn_w, L0_ffn_proj_w, L0_ffn_router_w, L0_ffn_expert_wv, L0_ffn_expert_proj), axis=-1)
    x = x + _layernorm(_L1_attn_ref(_layernorm(x, axis=-1), L1_attn_w_in, L1_attn_b_in, L1_attn_w_a, L1_attn_b_a, L1_attn_w_b, L1_attn_b_b, L1_attn_w_out, L1_attn_b_out), axis=-1)
    x = x + _layernorm(_L1_ffn_ref(_layernorm(x, axis=-1), L1_ffn_W_fc, L1_ffn_W_proj), axis=-1)
    x = x + _layernorm(_L2_attn_ref(_layernorm(x, axis=-1), L2_attn_Wq, L2_attn_Wk, L2_attn_Wv, L2_attn_Wm1, L2_attn_bm1, L2_attn_Wm2, L2_attn_bm2, L2_attn_Wproj, L2_attn_Wfc, L2_attn_Wcp), axis=-1)
    x = x + _layernorm(_L2_ffn_ref(_layernorm(x, axis=-1), L2_ffn_W_r, L2_ffn_W_k, L2_ffn_W_v, L2_ffn_mu_r, L2_ffn_mu_k), axis=-1)
    x = x + _layernorm(_L3_attn_ref(_layernorm(x, axis=-1), L3_attn_W_Q, L3_attn_W_KV, L3_attn_W1, L3_attn_b1, L3_attn_W2, L3_attn_b2), axis=-1)
    x = x + _layernorm(_L3_ffn_ref(_layernorm(x, axis=-1), L3_ffn_w1, L3_ffn_b1, L3_ffn_w2, L3_ffn_b2), axis=-1)
    return x

_drawn_inputs = setup_inputs


def setup_inputs(seed=0):
    import zlib

    import numpy as np

    out = dict(_drawn_inputs(seed))
    spreads = {'L0_ffn_ln1_w': (1.0, 0.6),
     'L0_ffn_ln1_b': (0.0, 0.8),
     'L0_ffn_ln2_w': (1.0, 0.6),
     'L0_ffn_ln2_b': (0.0, 0.8),
     'L3_attn_b1': (0.0, 0.292),
     'L3_attn_b2': (0.0, 0.1),
     'L3_ffn_b1': (0.0, 0.275),
     'L3_ffn_b2': (0.0, 0.1)}
    factors = {'L0_ffn_conv_w': 8.0,
     'L0_ffn_attn_w': 8.0,
     'L0_ffn_proj_w': 8.0,
     'L0_ffn_router_w': 3.893,
     'L0_ffn_expert_wv': 3.532,
     'L0_ffn_expert_proj': 3.575,
     'L2_attn_bm1': 8.0,
     'L2_attn_bm2': 3.785}
    for name, (base, spread) in spreads.items():
        noise = np.random.default_rng([zlib.crc32(name.encode()), seed]).standard_normal(out[name].shape)
        drawn = base * np.exp(spread * noise) if base else spread * noise
        out[name] = jnp.asarray(drawn.astype(out[name].dtype))
    for name, factor in factors.items():
        out[name] = (out[name] * factor).astype(out[name].dtype)
    return out
```

```python
from contextlib import ExitStack

import numpy as np
import concourse.bass as bass
from concourse import mybir

F32 = mybir.dt.float32
BF16 = mybir.dt.bfloat16
I32 = mybir.dt.int32
ALU = mybir.AluOpType
ACT = mybir.ActivationFunctionType
AX = mybir.AxisListType

P = 128
T = 2048
NT = T // P
TB = 4
BL = TB * P
NB = T // BL
H = 16
D = P // H
EPS = 1e-5
FF = 512
FC = FF // P
NE = 4
CK = 32
NEG = -1e30

PACK = [
    ("eye", P), ("l0_qkv", 3 * P), ("l0_proj", P),
    ("m_ln1w", 1), ("m_ln1b", 1), ("m_ln2w", 1), ("m_ln2b", 1), ("m_conv", 3),
    ("m_qkv", 3 * P), ("m_proj", P), ("m_router", NE), ("cos", NT * D // 2), ("sin", NT * D // 2),
    ("c_in", 2 * P), ("c_inb", 8), ("c_taps", 64), ("c_diag", 32), ("c_ba", 1), ("c_bb", 1),
    ("c_out", 2 * P), ("s_fc", FF), ("s_proj", FC * P),
    ("g_q", P), ("g_k", P), ("g_v", D * P), ("g_m1", 32), ("g_bm1", 1), ("g_m2", P), ("g_bm2", 1),
    ("g_proj", D * P), ("g_fc", FF), ("g_cp", FC * P),
    ("r_r", P), ("r_k", P), ("r_v", P), ("r_mur", 1), ("r_muk", 1),
    ("t_q", P), ("t_kv", 2 * P), ("t_w1", P), ("t_w2", P), ("t_w2t", P), ("t_b1", 1), ("t_b2", 1),
    ("t_before", P),
    ("f_w1", FF), ("f_b1", FC), ("f_w2", FC * P),
]
AT = {}
_at = 0
for _name, _n in PACK:
    AT[_name] = (_at, _n)
    _at += _n
NW = _at
WV, EPROJ = NE * 2 * FF, NE * FC * P
ROWS = ["l0_bproj", "c_bout", "f_b2"]


class Mem:
    pass


class Chain:

    def __init__(self, eng, sem, base=0):
        self.eng, self.sem, self.base, self.n = eng, sem, base, 0

    def __call__(self, ins):
        self.n += 1
        return ins.then_inc(self.sem, 1)

    def wait(self):
        self.eng.wait_ge(self.sem, self.base + self.n)


def alone(eng, M):
    eng.sem_inc(M.s_alone, 1)


class Scratch:

    def __init__(self, nc, ctx, layer):
        self.nc, self.ctx, self.layer, self.sems = nc, ctx, layer, []
        ctx.callback(self.clear)

    def clear(self):
        if self.sems:
            self.nc.clear_and_free_semaphores(self.sems)
            self.nc.all_engine_barrier()

    def sb(self, name, shape, dt=F32):
        return self.ctx.enter_context(self.nc.sbuf_tensor(f"{self.layer}_{name}", shape, dt))

    def ps(self, name, shape, dt=F32):
        return self.ctx.enter_context(self.nc.psum_tensor(f"{self.layer}_{name}", shape, dt))

    def sem(self, name):
        self.sems.append(self.nc.alloc_semaphore(f"{self.layer}_{name}"))
        return self.sems[-1]



def norm_stats(dve, M, own, src, st, mv, eps=EPS):
    for j in range(TB):
        own(dve.bn_stats(st[:, j, :], src(j)))
    own.wait()
    dve.memset(M.spare[:, 0:1], 0.0)
    for j in range(TB):
        own(dve.bn_aggr(mv[:, j, :], st[:, j, :]))
    own.wait()
    return own(dve.tensor_scalar(mv[:, :, 1], mv[:, :, 1], eps, None, ALU.add))


def norm_apply(dve, own, src, mv, rstd, dst):
    for j in range(TB):
        own(dve.tensor_scalar(dst[:, j, :], src(j), mv[:, j, 0:1], rstd[:, j:j + 1], ALU.subtract, ALU.mult))


class Norm:

    def __init__(self, S, name):
        self.st = S.sb(name + "_st", [P, TB, 6])
        self.mv = S.sb(name + "_mv", [P, TB, 2])
        self.rstd = S.sb(name + "_rstd", [P, TB])
        self.out = S.sb(name + "_out", [P, TB, P])
        self.var = S.sem(name + "_var_ready")
        self.inv = S.sem(name + "_rstd_ready")
        self.done = S.sem(name + "_normalised")

    def dve(self, dve, M, own, src, i):
        norm_stats(dve, M, own, src, self.st, self.mv)
        own.wait()
        dve.sem_inc(self.var, 1)
        dve.wait_ge(self.inv, i + 1)
        norm_apply(dve, own, src, self.mv, self.rstd, self.out)
        own.wait()

    def pool(self, pool, M, i):
        pool.wait_ge(self.var, i + 1)
        pool.tensor_tensor(self.rstd[:, :], self.mv[:, :, 1], M.mhalf[:, 0:TB], ALU.pow).then_inc(self.inv, 1)


def turn(pe, M, dst, src):
    for j in range(TB):
        last = pe.transpose(dst[:, j * P:(j + 1) * P], src[:, j, :], M.eye)
    return last


class Front:

    def __init__(self, S, pad=0, hT=None):
        self.norm = Norm(S, "front")
        self.pad = pad
        self.hT = hT if hT is not None else S.sb("hT", [P, pad + BL])
        self.bank = S.ps("front_bank", [P, BL])
        self.turned = S.sem("front_turned")
        self.ready = S.sem("front_ready")

    def dve(self, dve, M, own, i):
        self.norm.dve(dve, M, own, lambda j: M.X[:, i * TB + j, :], i)
        dve.sem_inc(self.norm.done, 1)

    def pool(self, pool, M, i):
        self.norm.pool(pool, M, i)

    def pe(self, pe, M, i):
        pe.wait_ge(self.norm.done, i + 1)
        turn(pe, M, self.bank, self.norm.out).then_inc(self.turned, 1)

    def act(self, act, i, dst=None):
        act.wait_ge(self.turned, i + 1)
        dst = self.hT[:, self.pad:self.pad + BL] if dst is None else dst
        act.copy(dst, self.bank[:, :]).then_inc(self.ready, 1)


class Tail:

    def __init__(self, S):
        self.norm = Norm(S, "tail")
        self.y = S.sem("y_ready")

    def dve(self, dve, M, own, y, i):
        dve.wait_ge(self.y, i + 1)
        self.norm.dve(dve, M, own, y, i)
        own(dve.tensor_tensor(M.X[:, bass.ts(i, TB), :], M.X[:, bass.ts(i, TB), :], self.norm.out[:, :, :], ALU.add))
        own.wait()
        dve.sem_inc(self.norm.done, 1)

    def pool(self, pool, M, i):
        self.norm.pool(pool, M, i)



def load(nc, M, x, w, rows, causal):
    ctx = M.ctx
    M.W = ctx.enter_context(nc.sbuf_tensor("weights", [P, NW], F32))
    M.X = ctx.enter_context(nc.sbuf_tensor("x", [P, NT, P], F32))
    M.rows = ctx.enter_context(nc.sbuf_tensor("rows", [1, len(ROWS) * P], F32))
    M.ones = ctx.enter_context(nc.sbuf_tensor("ones", [1, P], F32))
    M.eyeb = ctx.enter_context(nc.sbuf_tensor("eyeb", [P, P], BF16))
    M.mhalf = ctx.enter_context(nc.sbuf_tensor("mhalf", [P, NT], F32))
    M.causal = ctx.enter_context(nc.sbuf_tensor("causal", [P, P], BF16))
    M.spare = ctx.enter_context(nc.sbuf_tensor("spare", [P, 1], F32))
    M.s_load = ctx.enter_context(nc.semaphore("loaded"))
    M.s_alone = ctx.enter_context(nc.semaphore("waits_passed"))
    s_const = ctx.enter_context(nc.semaphore("constants"))
    M.w = lambda name, a=0, n=None: M.W[:, AT[name][0] + a:AT[name][0] + (AT[name][1] if n is None else a + n)]
    M.row = lambda name: M.rows[0:1, ROWS.index(name) * P:(ROWS.index(name) + 1) * P]
    M.eye = M.w("eye")
    cuts = [0, AT["m_ln1w"][0], AT["c_in"][0], AT["t_q"][0], NW]
    M.N_LOAD = 16 * (3 + len(cuts) - 1)
    with nc.Block() as block:
        @block.sync
        def _(sp):
            sp.dma_start(M.X[:, :, :], x.rearrange("(t p) f -> p t f", p=P)).then_inc(M.s_load, 16)
            for a, b in zip(cuts[:-1], cuts[1:]):
                sp.dma_start(M.W[:, a:b], w[:, a:b]).then_inc(M.s_load, 16)
            sp.dma_start(M.rows[:, :], rows).then_inc(M.s_load, 16)
            sp.dma_start(M.causal[:, :], causal).then_inc(M.s_load, 16)
            sp.wait_ge(M.s_load, M.N_LOAD)

        @block.vector
        def _(dve):
            dve.memset(M.ones[:, :], 1.0)
            dve.memset(M.mhalf[:, :], -0.5).then_inc(s_const, 1)
            dve.wait_ge(M.s_load, M.N_LOAD)
            dve.tensor_copy(M.eyeb[:, :], M.eye).then_inc(s_const, 1)
            dve.wait_ge(s_const, 2)


def store(nc, M, out):
    s_out = M.ctx.enter_context(nc.semaphore("stored"))
    with nc.Block() as block:
        @block.sync
        def _(sp):
            sp.dma_start(out.rearrange("(t p) f -> p t f", p=P), M.X[:, :, :]).then_inc(s_out, 16)
            sp.wait_ge(s_out, 16)



def head_mix(nc, M):
    with ExitStack() as ctx:
        S = Scratch(nc, ctx, "l0")
        front, tail = Front(S), Tail(S)
        qkvP = [S.ps(f"qkvP{k}", [P, 3 * P]) for k in range(2)]
        oP = S.ps("oP", [P, BL])
        yP = S.ps("yP", [P, TB, P])
        qkv = S.sb("qkv", [P, 2, 3 * P])
        prod = S.sb("prod", [P, H * H * D])
        prod2 = S.sb("prod2", [P, H * H * D])
        sc = S.sb("sc", [P, 2, H * H])
        pr = S.sb("pr", [P, 2, H * H])
        mx = S.sb("mx", [P, H])
        den = S.sb("den", [P, 2, H])
        o = S.sb("o", [P, TB, P])
        oT = S.sb("oT", [P, BL])
        s_qkvP = S.sem("qkv_in_psum")
        s_qkv = S.sem("qkv_ready")
        s_sc = S.sem("scores_ready")
        s_pr = S.sem("exp_ready")
        s_pv = S.sem("weighted_values")
        s_o = S.sem("o_ready")
        s_oP = S.sem("o_turned")
        s_oT = S.sem("oT_ready")
        s_red = S.sem("sums_taken")
        own_dve = S.sem("own_dve")
        PER = 59
        with nc.Block() as block:
            @block.tensor
            def _(pe):
                with pe.Fori(0, NB) as i:
                    front.pe(pe, M, i)
                    pe.wait_ge(front.ready, i + 1)
                    for j in range(TB):
                        if j >= 2:
                            pe.wait_ge(s_qkv, i * TB + j - 1)
                        pe.matmul(qkvP[j % 2][:, :], front.hT[:, j * P:(j + 1) * P], M.w("l0_qkv"),
                                  start=True, stop=True).then_inc(s_qkvP, 1)
                    pe.wait_ge(s_o, i + 1)
                    turn(pe, M, oP, o).then_inc(s_oP, 1)
                    pe.wait_ge(s_oT, i + 1)
                    for j in range(TB):
                        pe.matmul(yP[:, j, :], oT[:, j * P:(j + 1) * P], M.w("l0_proj"), start=True, stop=False)
                        last = pe.matmul(yP[:, j, :], M.ones[0:1, :], M.row("l0_bproj"), start=False, stop=True)
                    last.then_inc(tail.y, 1)

            @block.scalar
            def _(act):
                with act.Fori(0, NB) as i:
                    front.act(act, i)

                    def evacuate(j):
                        act.wait_ge(s_qkvP, i * TB + j + 1)
                        act.copy(qkv[:, j % 2, :], qkvP[j % 2][:, :]).then_inc(s_qkv, 1)

                    evacuate(0)
                    for j in range(TB):
                        act.wait_ge(s_sc, i * TB + j + 1)
                        act.activation(pr[:, j % 2, :], sc[:, j % 2, :], ACT.Exp, scale=1.0 / 8.0).then_inc(s_pr, 1)
                        if j + 1 < TB:
                            if j >= 1:
                                act.wait_ge(s_pv, i * TB + j)
                            evacuate(j + 1)
                    act.wait_ge(s_oP, i + 1)
                    act.copy(oT[:, :], oP[:, :]).then_inc(s_oT, 1)

            @block.gpsimd
            def _(pool):
                with pool.Fori(0, NB) as i:
                    front.pool(pool, M, i)
                    for j in range(TB):
                        pool.wait_ge(s_pr, i * TB + j + 1)
                        if j > 0:
                            pool.wait_ge(s_red, i * TB + j)
                        v = qkv[:, j % 2, :].rearrange("p (g c d) -> p c d g", c=3, d=D)[:, 2, :, :]
                        pool.tensor_tensor(
                            prod2[:, :].rearrange("p (h d g) -> p h d g", h=H, d=D),
                            pr[:, j % 2, :].rearrange("p (h a g) -> p h a g", h=H, a=1).broadcast_to([P, H, D, H]),
                            v.rearrange("p (a d) g -> p a d g", a=1).broadcast_to([P, H, D, H]),
                            ALU.mult).then_inc(s_pv, 1)
                    tail.pool(pool, M, i)

            @block.vector
            def _(dve):
                with dve.Fori(0, NB) as i:
                    own = Chain(dve, own_dve, i * PER)
                    front.dve(dve, M, own, i)

                    def scores(j):
                        dve.wait_ge(s_qkv, i * TB + j + 1)
                        t = qkv[:, j % 2, :].rearrange("p (g c d) -> p g c d", c=3, d=D)
                        s3 = sc[:, j % 2, :].rearrange("p (h g) -> p h g", h=H)
                        own(dve.tensor_tensor(
                            prod[:, :].rearrange("p (h g d) -> p h g d", h=H, g=H),
                            t[:, :, 0:1, :].broadcast_to([P, H, H, D]),
                            t[:, :, 1, :].rearrange("p (a g) d -> p a g d", a=1).broadcast_to([P, H, H, D]), ALU.mult))
                        own.wait()
                        own(dve.tensor_reduce(sc[:, j % 2, :], prod[:, :].rearrange("p (n d) -> p n d", d=D), AX.X, ALU.add))
                        own.wait()
                        own(dve.tensor_reduce(mx[:, :], s3, AX.X, ALU.max))
                        own.wait()
                        own(dve.tensor_tensor(s3, s3, mx[:, :].rearrange("p (h a) -> p h a", a=1).broadcast_to([P, H, H]), ALU.subtract))
                        own.wait()
                        dve.sem_inc(s_sc, 1)

                    def values(j):
                        dve.wait_ge(s_pr, i * TB + j + 1)
                        own(dve.tensor_reduce(den[:, 0, :], pr[:, j % 2, :].rearrange("p (h g) -> p h g", h=H), AX.X, ALU.add))
                        own.wait()
                        own(dve.reciprocal(den[:, 1, :], den[:, 0, :]))
                        dve.wait_ge(s_pv, i * TB + j + 1)
                        own(dve.tensor_reduce(o[:, j, :], prod2[:, :].rearrange("p (n g) -> p n g", g=H), AX.X, ALU.add))
                        own.wait()
                        dve.sem_inc(s_red, 1)
                        o3 = o[:, j, :].rearrange("p (h d) -> p h d", h=H)
                        own(dve.tensor_tensor(o3, o3, den[:, 1, :].rearrange("p (h a) -> p h a", a=1).broadcast_to([P, H, D]), ALU.mult))
                        own.wait()

                    scores(0)
                    for j in range(1, TB):
                        scores(j)
                        values(j - 1)
                    values(TB - 1)
                    dve.sem_inc(s_o, 1)
                    tail.dve(dve, M, own, lambda j: yP[:, j, :], i)
                    assert own.n == PER, own.n




GH = 4
NG = H // GH
SLOT = 64
TERMS = [(0, 0), (0, 1), (0, 2), (1, 0), (1, 1), (2, 0)]
NTERM = len(TERMS) * D
ROWSB = NTERM + 3
PARTS = 3


def causal_moe(nc, M):
    with ExitStack() as ctx:
        S = Scratch(nc, ctx, "l1")
        M.U = S.sb("u", [P, NT, P])
        with ExitStack() as actx:
            A = Scratch(nc, actx, "l1")
            M.V = A.sb("v", [P, NT, H, D])
            M.Y = A.sb("heads_out", [P, NT, H, D])
            with ExitStack() as bctx:
                B = Scratch(nc, bctx, "l1")
                M.Qs = B.sb("q_split", [P, NT, H, SLOT], BF16)
                M.Ks = B.sb("k_split", [P, NT, H, SLOT], BF16)
                rotary_qkv(nc, M)
                attention(nc, M)
            M.E = A.sb("expert_weights", [P, WV + EPROJ])
            project(nc, M)
            experts(nc, M)


def rotary_qkv(nc, M):
    with ExitStack() as ctx:
        S = Scratch(nc, ctx, "l1a")
        outer, inner = Norm(S, "outer"), Norm(S, "inner")
        turnP = S.ps("turnP", [P, BL])
        qkvP = [S.ps(f"qkvP{k}", [P, 3 * P]) for k in range(2)]
        hT = S.sb("hT", [P, 2 + BL])
        c = S.sb("conv", [P, 3, BL])
        qk = S.sb("qk", [P, 2, 2 * P])
        t1 = S.sb("times_cos", [P, 2 * P])
        t2 = S.sb("times_sin", [P, 2 * P])
        rot = S.sb("turned_qk", [P, 3, 2 * P])
        part = S.sb("parts", [P, 2, PARTS, 2 * P], BF16)
        s_turned = S.sem("h_turned")
        s_hT = S.sem("hT_ready")
        s_c = S.sem("conv_ready")
        s_qkvP = S.sem("qkv_in_psum")
        s_qk = S.sem("qk_ready")
        s_sin = S.sem("sin_products")
        s_part = S.sem("parts_ready")
        s_put = S.sem("q_slots_written")
        s_putk = S.sem("k_slots_written")
        own_dve = S.sem("own_dve")
        own_pool = S.sem("own_pool")
        s_rot = S.sem("sin_used")
        PER = 63
        with nc.Block() as block:
            @block.tensor
            def _(pe):
                with pe.Fori(0, NB) as i:
                    pe.wait_ge(inner.done, i + 1)
                    turn(pe, M, turnP, inner.out).then_inc(s_turned, 1)
                    pe.wait_ge(s_c, i + 1)
                    for j in range(TB):
                        if j >= 2:
                            pe.wait_ge(s_qk, i * TB + j - 1)
                        pe.matmul(qkvP[j % 2][:, :], c[:, 2, j * P:(j + 1) * P], M.w("m_qkv"), start=True, stop=True).then_inc(s_qkvP, 1)

            @block.scalar
            def _(act):
                with act.Fori(0, NB) as i:
                    act.wait_ge(s_turned, i + 1)
                    act.activation(hT[:, 2:2 + BL], turnP[:, :], ACT.Identity, scale=M.w("m_ln1w"), bias=M.w("m_ln1b")).then_inc(s_hT, 1)

                    def slots(j):
                        act.wait_ge(s_part, i * TB + j + 1)
                        p4 = part[:, j % 2, :, P:2 * P].rearrange("p n (h d) -> p h n d", h=H)
                        k4 = M.Ks[:, i * TB + j, :, 0:NTERM].rearrange("p h (n d) -> p h n d", d=D)
                        act.copy(k4[:, :, 0:3, :], p4)
                        act.copy(k4[:, :, 3:5, :], p4[:, :, 0:2, :])
                        act.copy(k4[:, :, 5:6, :], p4[:, :, 0:1, :]).then_inc(s_putk, 1)

                    for j in range(TB):
                        act.wait_ge(s_qkvP, i * TB + j + 1)
                        if j >= 2:
                            act.wait_ge(s_rot, i * TB + j - 1)
                        act.copy(M.V[:, i * TB + j, :, :], qkvP[j % 2][:, 2 * P:3 * P].rearrange("p (h d) -> p h d", h=H))
                        act.copy(qk[:, j % 2, :], qkvP[j % 2][:, 0:2 * P]).then_inc(s_qk, 1)
                        if j >= 1:
                            slots(j - 1)
                    slots(TB - 1)

            @block.gpsimd
            def _(pool):
                pool.memset(M.Qs[:, :, :, NTERM:SLOT], 0.0).then_inc(own_pool, 1)
                pool.memset(M.Ks[:, :, :, ROWSB:SLOT], 0.0).then_inc(own_pool, 1)
                pool.memset(M.Ks[:, :, :, NTERM:ROWSB], 1.0).then_inc(own_pool, 1)
                pool.wait_ge(own_pool, 3)
                with pool.Fori(0, NB) as i:
                    outer.pool(pool, M, i)
                    inner.pool(pool, M, i)

                    def slots(j):
                        pool.wait_ge(s_part, i * TB + j + 1)
                        alone(pool, M)
                        p4 = part[:, j % 2, :, 0:P].rearrange("p n (h d) -> p h n d", h=H)
                        q4 = M.Qs[:, i * TB + j, :, 0:NTERM].rearrange("p h (n d) -> p h n d", d=D)
                        pool.tensor_copy(q4[:, :, 0:3, :], p4[:, :, 0:1, :].broadcast_to([P, H, 3, D]))
                        pool.tensor_copy(q4[:, :, 3:5, :], p4[:, :, 1:2, :].broadcast_to([P, H, 2, D]))
                        pool.tensor_copy(q4[:, :, 5:6, :], p4[:, :, 2:3, :]).then_inc(s_put, 1)

                    for j in range(TB):
                        pool.wait_ge(s_qk, i * TB + j + 1)
                        if j >= 1:
                            pool.wait_ge(s_rot, i * TB + j)
                        x4 = qk[:, j % 2, :].rearrange("p (h a d) -> p h a d", a=2, d=D // 2)
                        t4 = t2[:, :].rearrange("p (h a d) -> p h a d", a=2, d=D // 2)
                        sin = M.w("sin").rearrange("p (t d) -> p t d", t=NT)[:, bass.ds(i * TB + j, 1), :].broadcast_to([P, 2 * H, D // 2])
                        pool.tensor_tensor(t4[:, :, 0, :], x4[:, :, 1, :], sin, ALU.mult)
                        pool.tensor_tensor(t4[:, :, 1, :], x4[:, :, 0, :], sin, ALU.mult).then_inc(s_sin, 1)
                        if j >= 1:
                            slots(j - 1)
                    slots(TB - 1)

            @block.vector
            def _(dve):
                first = Chain(dve, own_dve)
                first(dve.memset(hT[:, 0:2], 0.0))
                first.wait()
                with dve.Fori(0, NB) as i:
                    own = Chain(dve, own_dve, i * PER + 1)
                    outer.dve(dve, M, own, lambda j: M.X[:, i * TB + j, :], i)
                    own(dve.tensor_copy(M.U[:, bass.ts(i, TB), :], outer.out[:, :, :]))
                    inner.dve(dve, M, own, lambda j: outer.out[:, j, :], i)
                    dve.sem_inc(inner.done, 1)
                    dve.wait_ge(s_hT, i + 1)
                    w = M.w("m_conv")
                    own(dve.tensor_scalar(c[:, 0, :], hT[:, 0:BL], w[:, 0:1], None, ALU.mult))
                    own.wait()
                    own(dve.scalar_tensor_tensor(c[:, 1, :], hT[:, 1:1 + BL], w[:, 1:2], c[:, 0, :], ALU.mult, ALU.add))
                    own.wait()
                    own(dve.scalar_tensor_tensor(c[:, 2, :], hT[:, 2:2 + BL], w[:, 2:3], c[:, 1, :], ALU.mult, ALU.add))
                    own.wait()
                    dve.sem_inc(s_c, 1)
                    own(dve.tensor_copy(hT[:, 0:2], hT[:, BL:BL + 2]))
                    for j in range(TB):
                        dve.wait_ge(s_qk, i * TB + j + 1)
                        x4 = qk[:, j % 2, :].rearrange("p (h a d) -> p h a d", a=2, d=D // 2)
                        t14 = t1[:, :].rearrange("p (h a d) -> p h a d", a=2, d=D // 2)
                        t24 = t2[:, :].rearrange("p (h a d) -> p h a d", a=2, d=D // 2)
                        r4 = rot[:, 0, :].rearrange("p (h a d) -> p h a d", a=2, d=D // 2)
                        cos = M.w("cos").rearrange("p (t d) -> p t d", t=NT)[:, bass.ds(i * TB + j, 1), :].broadcast_to([P, 2 * H, D // 2])
                        own(dve.tensor_tensor(t14[:, :, 0, :], x4[:, :, 0, :], cos, ALU.mult))
                        own(dve.tensor_tensor(t14[:, :, 1, :], x4[:, :, 1, :], cos, ALU.mult))
                        own.wait()
                        dve.wait_ge(s_sin, i * TB + j + 1)
                        own(dve.tensor_tensor(r4[:, :, 0, :], t14[:, :, 0, :], t24[:, :, 0, :], ALU.subtract))
                        own(dve.tensor_tensor(r4[:, :, 1, :], t14[:, :, 1, :], t24[:, :, 1, :], ALU.add))
                        own.wait()
                        dve.sem_inc(s_rot, 1)
                        pj = part[:, j % 2, :, :]
                        if j >= 2:
                            dve.wait_ge(s_put, i * TB + j - 1)
                            dve.wait_ge(s_putk, i * TB + j - 1)
                        own(dve.tensor_copy(pj[:, 0, :], rot[:, 0, :]))
                        own.wait()
                        own(dve.tensor_tensor(rot[:, 1, :], rot[:, 0, :], pj[:, 0, :], ALU.subtract))
                        own.wait()
                        own(dve.tensor_copy(pj[:, 1, :], rot[:, 1, :]))
                        own.wait()
                        own(dve.tensor_tensor(pj[:, 2, :], rot[:, 1, :], pj[:, 1, :], ALU.subtract))
                        own.wait()
                        dve.sem_inc(s_part, 1)
                    dve.wait_ge(s_put, i * TB + TB)
                    dve.wait_ge(s_putk, i * TB + TB)
                    assert own.n == PER, own.n


def attention(nc, M):
    T_, Q_, U_, E_, F_, N_ = "turn", "turn_q", "max", "exp", "weigh", "norm"
    firsts = [(T_, 0)]
    for t in range(NT):
        if t + 1 < NT:
            firsts.append((T_, t + 1))
        for p in range(2):
            for c in range(t // TB + 1):
                for e in range(2):
                    firsts.append((U_, t, 2 * p + e, c))
    seconds = []
    for qc in range(NB):
        seconds += [(Q_, 2 * qc), (Q_, 2 * qc + 1)]
        for kt in range(TB * qc + TB):
            seconds += [(E_, qc, kt, 0), (E_, qc, kt, 1)]
            if kt > 0:
                seconds.append((F_, qc, kt - 1))
        seconds += [(F_, qc, TB * qc + TB - 1), (N_, qc)]
    width = lambda t, c: min(BL, (t + 1) * P - c * BL)

    def cost(it):
        if it[0] == U_:
            return 130 + width(it[1], it[3])
        if it[0] in (E_, F_):
            return (2 if it[0] == E_ else 4) * (BL - P * max(0, it[2] - TB * it[1]))
        return 60

    def merged(a, b):
        ta, tb = sum(map(cost, a)) or 1, sum(map(cost, b)) or 1
        out, x, y, ca, cb = [], 0, 0, 0.0, 0.0
        while x < len(a) or y < len(b):
            if y >= len(b) or (x < len(a) and ca / ta <= cb / tb):
                out.append(a[x])
                ca += cost(a[x])
                x += 1
            else:
                out.append(b[y])
                cb += cost(b[y])
                y += 1
        return out

    NU = sum(1 for it in firsts if it[0] == U_)
    NEX = sum(1 for it in seconds if it[0] == F_)
    TURNS_A, TURNS_B = NT, NT // 2 + NB
    RING = 3

    def ring(items):
        users = [it for it in items if it[0] in (T_, Q_, U_, N_)]
        return {it: (k % RING, users[k - RING] if k >= RING else None) for k, it in enumerate(users)}

    with ExitStack() as ctx:
        S = Scratch(nc, ctx, "l1b")
        bank = [S.ps(f"ring{k}", [P, BL]) for k in range(RING)]
        stP = [S.ps(f"stP{p}", [P, 2, BL]) for p in range(2)]
        oP = S.ps("oP", [P, BL])
        KTn = S.sb("kT_next", [P, 2, T], BF16)
        KTc = S.sb("kT", [P, 2, T], BF16)
        QTn = S.sb("qT_tile", [P, 2, 2, 2, P], BF16)
        QTf = S.sb("qT", [P, 2, 2, T], BF16)
        mx = S.sb("max_parts", [P, NB, NT, GH])
        nm = S.sb("neg_max", [P, 3, NT, GH])
        PT = S.sb("probs", [P, 2, GH, BL])
        Vg = S.sb("v_ones", [P, NT, GH, 32])
        OT = S.sb("o_rows", [P, BL])
        OK = S.sb("o_tokens", [P, TB, GH, 32])
        rec = S.sb("reciprocal", [P, TB, GH, 1])
        s_tfull = S.sem("turned")
        s_tfree = S.sem("turned_out")
        s_sc = S.sem("scores_in_psum")
        s_max = S.sem("max_taken")
        s_neg = S.sem("neg_max_in_q")
        s_zero = S.sem("q_zeroed")
        s_kc = S.sem("kT_moved")
        s_vg = S.sem("values_ready")
        s_st = S.sem("scoresT_in_psum")
        s_exp = S.sem("exp_ready")
        s_pv = S.sem("pv_done")
        s_oT = S.sem("o_rows_ready")
        s_y = S.sem("o_normalised")
        own_dve = S.sem("own_dve")
        own_pool = S.sem("own_pool")

        def diag(qc, kt):
            return max(0, kt - TB * qc)

        def tensor_step(pe, s, g, base):
            items = merged(firsts if s is not None else [], seconds if g is not None else [])
            banks, count = ring(items), {}
            k, n, u, e, f = 0, 0, 0, 0, 0

            def take(it):
                b, before = banks[it]
                if before is not None:
                    pe.wait_ge(s_max if before[0] == U_ else s_tfree, count[before])
                return bank[b]

            if g is not None:
                pe.wait_ge(s_kc, g + 1)
                pe.wait_ge(s_vg, g + 1)
                pe.wait_ge(s_tfree, base)
                if not (isinstance(g, int) and g == NG - 1):
                    pe.wait_ge(s_max, s * NU)
                pe.wait_ge(s_neg, g + 1)
            for it in items:
                if it[0] == T_:
                    t = it[1]
                    tP = take(it)
                    for w in range(4):
                        src = (M.Ks if w < 2 else M.Qs)[:, t, bass.ds(s * GH + 2 * (w % 2), 2), :]
                        last = pe.matmul(tP[:, w * P:(w + 1) * P], src.rearrange("p h r -> p (h r)"), M.eyeb[:, :], start=True, stop=True)
                    last.then_inc(s_tfull, 1)
                    k += 1
                    count[it] = base + k
                elif it[0] == Q_:
                    tP = take(it)
                    for w in range(4):
                        src = M.Qs[:, 2 * it[1] + w % 2, bass.ds(g * GH + 2 * (w // 2), 2), :]
                        last = pe.matmul(tP[:, w * P:(w + 1) * P], src.rearrange("p h r -> p (h r)"), M.eyeb[:, :], start=True, stop=True)
                    last.then_inc(s_tfull, 1)
                    k += 1
                    count[it] = base + k
                elif it[0] == U_:
                    _, t, h, c = it
                    if h == 0 and c == 0:
                        pe.wait_ge(s_tfree, count[(T_, t)])
                    scP = take(it)
                    w = width(t, c)
                    last_c = c == t // TB
                    last = pe.matmul(scP[:, 0:w], QTn[:, h // 2, h % 2, t % 2, :],
                                     KTn[:, h // 2, c * BL:c * BL + w], start=True, stop=not last_c)
                    if last_c:
                        last = pe.matmul(scP[:, w - P:w], M.eyeb[:, :], M.causal[:, :], start=False, stop=True)
                    last.then_inc(s_sc, 1)
                    u += 1
                    count[it] = s * NU + u
                elif it[0] == E_:
                    _, qc, kt, p = it
                    r = diag(qc, kt)
                    if kt == 0 and p == 0:
                        pe.wait_ge(s_tfree, count[(Q_, 2 * qc + 1)])
                    if e >= 1:
                        pe.wait_ge(s_exp, (g * NEX + e) * 2 + p - 1)
                    for h in range(2):
                        last = pe.matmul(stP[p][:, h, r * P:BL], KTc[:, p, kt * P:(kt + 1) * P],
                                         QTf[:, p, h, qc * BL + r * P:(qc + 1) * BL], start=True, stop=kt < TB * qc)
                    if kt >= TB * qc:
                        for h in range(2):
                            last = pe.matmul(stP[p][:, h, r * P:(r + 1) * P], M.causal[:, :], M.eyeb[:, :], start=False, stop=True)
                    last.then_inc(s_st, 1)
                    e += p
                elif it[0] == F_:
                    _, qc, kt = it
                    r = diag(qc, kt)
                    pe.wait_ge(s_exp, (g * NEX + f) * 2 + 2)
                    for j in range(GH):
                        last = pe.matmul(oP[32 * j:32 * j + 32, r * P:BL], Vg[:, kt, j, :], PT[:, f % 2, j, r * P:BL],
                                         start=(kt == 0), stop=(kt == TB * qc + TB - 1), skip_group_check=True)
                    last.then_inc(s_pv, 1)
                    f += 1
                else:
                    tP = take(it)
                    pe.wait_ge(s_oT, g * NB + n + 1)
                    for j in range(TB):
                        last = pe.transpose(tP[:, j * P:(j + 1) * P], OT[:, j * P:(j + 1) * P], M.eye)
                    last.then_inc(s_tfull, 1)
                    k += 1
                    count[it] = base + k
                    n += 1
            assert k == (TURNS_A if s is not None else 0) + (TURNS_B if g is not None else 0)

        def scalar_step(act, s, g, base):
            items = merged(firsts if s is not None else [], seconds if g is not None else [])
            banks = ring(items)
            k, n, e = 0, 0, 0
            for it in items:
                if it[0] == T_:
                    t = it[1]
                    if t == 0 and g is not None:
                        act.wait_ge(s_kc, s)
                    act.wait_ge(s_tfull, base + k + 1)
                    tP = bank[banks[it][0]]
                    act.copy(KTn[:, :, t * P:(t + 1) * P], tP[:, 0:2 * P].rearrange("p (a q) -> p a q", a=2))
                    for h in range(2):
                        half = slice(SLOT * h, SLOT * h + SLOT)
                        last = act.copy(QTn[half, :, h, t % 2, :], tP[half, 2 * P:4 * P].rearrange("p (a q) -> p a q", a=2))
                    last.then_inc(s_tfree, 1)
                    k += 1
                elif it[0] == Q_:
                    act.wait_ge(s_tfull, base + k + 1)
                    tP = bank[banks[it][0]]
                    for h in range(2):
                        half = slice(SLOT * h, SLOT * h + SLOT)
                        last = act.copy(QTf[half, :, h, 2 * it[1] * P:(2 * it[1] + 2) * P], tP[half, :].rearrange("p (a q) -> p a q", a=2))
                    last.then_inc(s_tfree, 1)
                    k += 1
                elif it[0] == E_:
                    _, qc, kt, p = it
                    r = diag(qc, kt)
                    if e >= 2:
                        act.wait_ge(s_pv, g * NEX + e - 1)
                    act.wait_ge(s_st, (g * NEX + e) * 2 + p + 1)
                    act.activation(PT[:, e % 2, 2 * p:2 * p + 2, r * P:BL], stP[p][:, :, r * P:BL], ACT.Exp,
                                   scale=float(1.0 / np.sqrt(np.float32(D)))).then_inc(s_exp, 1)
                    e += p
                elif it[0] == N_:
                    act.wait_ge(s_pv, g * NEX + e)
                    act.copy(OT[:, :], oP[:, :]).then_inc(s_oT, 1)
                    act.wait_ge(s_y, g * NB + n + 1)
                    act.wait_ge(s_tfull, base + k + 1)
                    tP = bank[banks[it][0]]
                    act.copy(OK[:, :, :, :], tP[:, :].rearrange("p (t h r) -> p t h r", t=TB, h=GH)).then_inc(s_tfree, 1)
                    k += 1
                    n += 1

        OWN = 6
        base_of = lambda s: TURNS_A + (s - 1) * (TURNS_A + TURNS_B)

        def vector_step(dve, s, g, base, ownbase):
            items = merged(firsts if s is not None else [], seconds if g is not None else [])
            banks = ring(items)
            k, n, u = 0, 0, 0
            own = Chain(dve, own_dve, ownbase)
            for it in items:
                if it[0] in (T_, Q_):
                    k += 1
                elif it[0] == U_:
                    _, t, h, c = it
                    dve.wait_ge(s_sc, s * NU + u + 1)
                    dve.tensor_reduce(mx[:, c, t, h:h + 1], bank[banks[it][0]][:, 0:width(t, c)], AX.X, ALU.max).then_inc(s_max, 1)
                    u += 1
                elif it[0] == N_:
                    dve.wait_ge(s_tfree, base + k + 1)
                    own(dve.reciprocal(rec[:, :, :, :], OK[:, :, :, D:D + 1]))
                    own.wait()
                    dve.tensor_tensor(M.Y[:, TB * it[1]:TB * it[1] + TB, bass.ds(g * GH, GH), :], OK[:, :, :, 0:D],
                                      rec[:, :, :, :].broadcast_to([P, TB, GH, D]), ALU.mult).then_inc(s_y, 1)
                    k += 1
                    n += 1
            if s is not None:
                dve.wait_ge(s_max, s * NU + NU)
                slot = lambda m: M.Qs[:, :, bass.ds(s * GH, GH), NTERM + m]
                own(dve.tensor_reduce(nm[:, 0, :, :], mx[:, :, :, :].rearrange("p c t h -> p t h c"), AX.X, ALU.max, negate=True))
                own.wait()
                own(dve.tensor_copy(slot(0), nm[:, 0, :, :]))
                own.wait()
                own(dve.tensor_tensor(nm[:, 1, :, :], nm[:, 0, :, :], slot(0), ALU.subtract))
                own.wait()
                own(dve.tensor_copy(slot(1), nm[:, 1, :, :]))
                own.wait()
                own(dve.tensor_tensor(nm[:, 2, :, :], nm[:, 1, :, :], slot(1), ALU.subtract))
                own.wait()
                own(dve.tensor_copy(slot(2), nm[:, 2, :, :]))
                own.wait()
                dve.sem_inc(s_neg, 1)
                if g is not None:
                    dve.wait_ge(s_pv, s * NEX)
                dve.tensor_copy(KTc[:, :, :], KTn[:, :, :]).then_inc(s_kc, 1)
            return own.n

        def pool_step(pool, s, g):
            if s is not None:
                if g is not None:
                    pool.wait_ge(s_pv, s * NEX)
                    alone(pool, M)
                pool.tensor_copy(Vg[:, :, :, 0:D], M.V[:, :, bass.ds(s * GH, GH), :]).then_inc(s_vg, 1)

        with nc.Block() as block:
            @block.tensor
            def _(pe):
                tensor_step(pe, 0, None, 0)
                with pe.Fori(1, NG) as s:
                    tensor_step(pe, s, s - 1, base_of(s))
                tensor_step(pe, None, NG - 1, base_of(NG))

            @block.scalar
            def _(act):
                act.wait_ge(s_zero, 1)
                scalar_step(act, 0, None, 0)
                act.wait_ge(s_zero, 2)
                with act.Fori(1, NG) as s:
                    scalar_step(act, s, s - 1, base_of(s))
                scalar_step(act, None, NG - 1, base_of(NG))

            @block.vector
            def _(dve):
                dve.memset(mx[:, :, :, :], -3.0e38).then_inc(own_dve, 1)
                dve.sem_inc(s_y, 1)
                dve.wait_ge(own_dve, 1)
                n = 1 + vector_step(dve, 0, None, 0, 1)
                PER = OWN + NB
                with dve.Fori(1, NG) as s:
                    assert vector_step(dve, s, s - 1, base_of(s), n + (s - 1) * PER) == PER
                vector_step(dve, None, NG - 1, base_of(NG), n + (NG - 1) * PER)

            @block.gpsimd
            def _(pool):
                pool.memset(QTn[:, :, :, :, :], 0.0).then_inc(s_zero, 1)
                pool.memset(Vg[:, :, :, :], 0.0).then_inc(own_pool, 1)
                pool.wait_ge(own_pool, 1)
                pool.memset(Vg[:, :, :, D:D + 1], 1.0).then_inc(own_pool, 1)
                pool.wait_ge(own_pool, 2)
                pool.memset(QTf[:, :, :, :], 0.0).then_inc(s_zero, 1)
                pool_step(pool, 0, None)
                with pool.Fori(1, NG) as s:
                    pool_step(pool, s, s - 1)


def project(nc, M):
    with ExitStack() as ctx:
        S = Scratch(nc, ctx, "l1c")
        tP = [S.ps(f"tP{k}", [P, BL]) for k in range(2)]
        yP = [S.ps(f"yP{k}", [P, TB, P]) for k in range(2)]
        hT = S.sb("headsT", [P, BL])
        hS = S.sb("heads", [P, TB, P])
        s_h = S.sem("heads_copied")
        s_t = S.sem("heads_turned")
        s_hT = S.sem("headsT_ready")
        s_y = S.sem("product_in_psum")
        s_u = S.sem("u_updated")
        s_e = S.sem("expert_weights_loaded")
        with nc.Block() as block:
            @block.sync
            def _(sp):
                sp.dma_start(M.E[:, 0:WV], M.experts_w[:, 0:WV]).then_inc(s_e, 16)
                sp.dma_start(M.E[:, WV:WV + EPROJ], M.experts_w[:, WV:WV + EPROJ]).then_inc(s_e, 16)
                sp.wait_ge(s_e, 32)

            @block.gpsimd
            def _(pool):
                with pool.Fori(0, NB) as i:
                    pool.tensor_copy(hS[:, :, :], M.Y[:, bass.ts(i, TB), :, :].rearrange("p t h d -> p t (h d)")).then_inc(s_h, 1)
                    pool.wait_ge(s_t, i + 1)

            @block.tensor
            def _(pe):
                with pe.Fori(0, NB) as i:
                    pe.wait_ge(s_h, i + 1)
                    turn(pe, M, tP[0], hS).then_inc(s_t, 1)
                    pe.wait_ge(s_hT, i + 1)
                    for j in range(TB):
                        last = pe.matmul(yP[0][:, j, :], hT[:, j * P:(j + 1) * P], M.w("m_proj"), start=True, stop=True)
                    last.then_inc(s_y, 1)
                    pe.wait_ge(s_u, i + 1)

            @block.scalar
            def _(act):
                with act.Fori(0, NB) as i:
                    act.wait_ge(s_t, i + 1)
                    act.copy(hT[:, :], tP[0][:, :]).then_inc(s_hT, 1)

            @block.vector
            def _(dve):
                with dve.Fori(0, NB) as i:
                    dve.wait_ge(s_y, i + 1)
                    u = M.U[:, bass.ts(i, TB), :]
                    dve.tensor_tensor(u, u, yP[0][:, :, :], ALU.add).then_inc(s_u, 1)


def experts(nc, M):
    with ExitStack() as ctx:
        S = Scratch(nc, ctx, "l1d")
        inner, tail = Norm(S, "inner"), Tail(S)
        turnP = S.ps("turnP", [P, BL])
        gP = [S.ps(f"gP{k}", [P, BL]) for k in range(2)]
        vP = [S.ps(f"vP{k}", [P, BL]) for k in range(2)]
        yP = [S.ps(f"yP{k}", [P, TB, P]) for k in range(2)]
        hT = S.sb("hT", [P, BL])
        lg = S.sb("logits", [P, TB, NE])
        best = S.sb("best", [P, TB, 1])
        hit = S.sb("hit", [P, TB, NE])
        left = S.sb("left", [P, 2, TB])
        pick = S.sb("pick", [P, TB, NE])
        sg = S.sb("silu", [P, 2, BL])
        a = S.sb("act", [P, 2, FC, BL])
        acc = S.sb("acc", [P, TB, P])
        s_turned = S.sem("h_turned")
        s_hT = S.sem("hT_ready")
        s_lg = S.sem("logits_in_psum")
        s_lgo = S.sem("logits_out")
        s_gP = S.sem("gate_in_psum")
        s_sg = S.sem("silu_ready")
        s_a = S.sem("act_ready")
        s_y = S.sem("expert_in_psum")
        s_acc = S.sem("expert_added")
        own_dve = S.sem("own_dve")
        PER = 54
        wv = lambda n: M.E[:, n:n + P]
        with nc.Block() as block:
            @block.tensor
            def _(pe):
                with pe.Fori(0, NB) as i:
                    pe.wait_ge(inner.done, i + 1)
                    turn(pe, M, turnP, inner.out).then_inc(s_turned, 1)
                    pe.wait_ge(s_hT, i + 1)
                    for j in range(TB):
                        last = pe.matmul(turnP[:, j * NE:(j + 1) * NE], hT[:, j * P:(j + 1) * P], M.w("m_router"), start=True, stop=True)
                    last.then_inc(s_lg, 1)

                    def down(e):
                        pe.wait_ge(s_a, (i * NE + e) * FC + FC)
                        if e >= 2:
                            pe.wait_ge(s_acc, i * NE + e - 1)
                        for j in range(TB):
                            for c in range(FC):
                                last = pe.matmul(yP[e % 2][:, j, :], a[:, e % 2, c, j * P:(j + 1) * P],
                                                 M.E[:, WV + (e * FC + c) * P:WV + (e * FC + c + 1) * P], start=(c == 0), stop=(c == FC - 1))
                        last.then_inc(s_y, 1)

                    for e in range(NE):
                        for c in range(FC):
                            n = e * FC + c
                            if n >= 2:
                                pe.wait_ge(s_a, i * NE * FC + n - 1)
                            pe.matmul(gP[n % 2][:, :], wv(e * 2 * FF + c * P), hT[:, :], start=True, stop=True)
                            pe.matmul(vP[n % 2][:, :], wv(e * 2 * FF + FF + c * P), hT[:, :], start=True, stop=True).then_inc(s_gP, 1)
                        if e >= 1:
                            down(e - 1)
                    down(NE - 1)
                    pe.wait_ge(s_lgo, i + 1)

            @block.scalar
            def _(act):
                with act.Fori(0, NB) as i:
                    act.wait_ge(s_turned, i + 1)
                    act.activation(hT[:, :], turnP[:, :], ACT.Identity, scale=M.w("m_ln2w"), bias=M.w("m_ln2b")).then_inc(s_hT, 1)
                    for n in range(NE * FC):
                        act.wait_ge(s_gP, i * NE * FC + n + 1)
                        if n >= 2:
                            act.wait_ge(s_a, i * NE * FC + n - 1)
                        act.activation(sg[:, n % 2, :], gP[n % 2][:, :], ACT.Silu).then_inc(s_sg, 1)

            @block.gpsimd
            def _(pool):
                with pool.Fori(0, NB) as i:
                    inner.pool(pool, M, i)
                    tail.pool(pool, M, i)

            @block.vector
            def _(dve):
                with dve.Fori(0, NB) as i:
                    own = Chain(dve, own_dve, i * PER)
                    inner.dve(dve, M, own, lambda j: M.U[:, i * TB + j, :], i)
                    dve.sem_inc(inner.done, 1)
                    own(dve.tensor_copy(acc[:, :, :], M.U[:, bass.ts(i, TB), :]))
                    dve.wait_ge(s_lg, i + 1)
                    own(dve.tensor_copy(lg[:, :, :], turnP[:, 0:TB * NE].rearrange("p (t e) -> p t e", e=NE)))
                    own.wait()
                    dve.sem_inc(s_lgo, 1)
                    own(dve.tensor_reduce(best[:, :, 0], lg[:, :, :], AX.X, ALU.max))
                    own.wait()
                    own(dve.tensor_tensor(hit[:, :, :], lg[:, :, :], best[:, :, :].broadcast_to([P, TB, NE]), ALU.is_equal))
                    own.wait()
                    own(dve.tensor_copy(pick[:, :, 0], hit[:, :, 0]))
                    own(dve.tensor_scalar(left[:, 0, :], hit[:, :, 0], -1.0, 1.0, ALU.mult, ALU.add))
                    own.wait()
                    for e in range(1, NE):
                        own(dve.tensor_tensor(pick[:, :, e], hit[:, :, e], left[:, (e - 1) % 2, :], ALU.mult))
                        own.wait()
                        if e + 1 < NE:
                            own(dve.tensor_tensor(left[:, e % 2, :], left[:, (e - 1) % 2, :], pick[:, :, e], ALU.subtract))
                            own.wait()

                    def add(e):
                        dve.wait_ge(s_y, i * NE + e + 1)
                        for j in range(TB):
                            own(dve.scalar_tensor_tensor(acc[:, j, :], yP[e % 2][:, j, :], pick[:, j, e:e + 1], acc[:, j, :], ALU.mult, ALU.add))
                        own.wait()
                        dve.sem_inc(s_acc, 1)

                    for e in range(NE):
                        for c in range(FC):
                            n = e * FC + c
                            dve.wait_ge(s_sg, i * NE * FC + n + 1)
                            if e >= 2 and c == 0:
                                dve.wait_ge(s_y, i * NE + e - 1)
                            dve.tensor_tensor(a[:, e % 2, c, :], sg[:, n % 2, :], vP[n % 2][:, :], ALU.mult).then_inc(s_a, 1)
                        if e >= 1:
                            add(e - 1)
                    add(NE - 1)
                    dve.sem_inc(tail.y, 1)
                    tail.dve(dve, M, own, lambda j: acc[:, j, :], i)
                    assert own.n == PER, own.n



def long_conv(nc, M):
    G = 8
    PADW = CK - 4
    with ExitStack() as ctx:
        S = Scratch(nc, ctx, "l2")
        front, tail = Front(S, pad=3), Tail(S)
        zP = [S.ps(f"zP{k}", [P, BL]) for k in range(2)]
        cP = [S.ps(f"cP{k}", [P, BL]) for k in range(2)]
        yP = S.ps("yP", [P, TB, P])
        taps = S.sb("taps", [P, 2 * 4 * 8, 32])
        z = S.sb("z", [P, G, PADW + BL])
        hb = S.sb("half_bias", [P, 2])
        th = S.sb("tanh", [P, 2, BL])
        sg = S.sb("sigmoid", [P, 2, BL])
        ga = S.sb("gated", [P, 2, BL])
        s_zP = S.sem("z_in_psum")
        s_z = S.sem("z_ready")
        edge = S.sb("edge", [P, 1, 3])
        s_edge = S.sem("edge_cleared")
        s_keep = S.sem("history_kept")
        s_cP = S.sem("conv_in_psum")
        s_th = S.sem("tanh_ready")
        s_ga = S.sem("gated_ready")
        s_set = S.sem("set_up")
        s_hist = S.sem("hT_history")
        s_pool = S.sem("own_pool")
        own_dve = S.sem("own_dve")
        PER = 29
        with nc.Block() as block:
            @block.tensor
            def _(pe):
                pe.wait_ge(s_set, 5)
                with pe.Fori(0, NB) as i:
                    front.pe(pe, M, i)
                    pe.wait_ge(front.ready, i + 1)
                    for n in range(G):
                        if n >= 2:
                            pe.wait_ge(s_z, i * G + n - 1)
                        for a in range(4):
                            last = pe.matmul(zP[n % 2][32 * a:32 * a + 32, :], M.w("c_in", 32 * n, 32),
                                             front.hT[:, 3 - a:3 - a + BL], start=True, stop=True)
                        last.then_inc(s_zP, 1)
                    pe.wait_ge(s_edge, i + 1)
                    for half in range(2):
                        for m in range(8):
                            for n in range(4):
                                last = pe.matmul(cP[half][32 * n:32 * n + 32, :], taps[:, (half * 4 + n) * 8 + m, :],
                                                 z[:, half * 4 + n, PADW - 4 * m:PADW - 4 * m + BL],
                                                 start=(m == 0), stop=(m == 7), skip_group_check=True)
                        last.then_inc(s_cP, 1)
                    pe.wait_ge(s_ga, i * 2 + 2)
                    for j in range(TB):
                        for half in range(2):
                            pe.matmul(yP[:, j, :], ga[:, half, j * P:(j + 1) * P], M.w("c_out", half * P, P),
                                      start=(half == 0), stop=False)
                        last = pe.matmul(yP[:, j, :], M.ones[0:1, :], M.row("c_bout"), start=False, stop=True)
                    last.then_inc(tail.y, 1)

            @block.scalar
            def _(act):
                act.activation(hb[:, 0:1], M.w("c_ba"), ACT.Copy, scale=0.5).then_inc(s_set, 1)
                act.activation(hb[:, 1:2], M.w("c_bb"), ACT.Copy, scale=0.5).then_inc(s_set, 1)
                act.wait_ge(s_set, 5)
                with act.Fori(0, NB) as i:
                    front.act(act, i)
                    for n in range(G):
                        act.wait_ge(s_zP, i * G + n + 1)
                        act.activation(z[:, n, PADW:PADW + BL], zP[n % 2][:, :], ACT.Identity,
                                       bias=M.w("c_inb", n, 1)).then_inc(s_z, 1)
                    for half in range(2):
                        act.wait_ge(s_cP, i * 2 + half + 1)
                        act.activation(th[:, half, :], cP[half][:, :], ACT.Tanh, scale=0.5, bias=hb[:, half:half + 1]).then_inc(s_th, 1)
                    act.wait_ge(s_hist, i + 1)
                    act.wait_ge(s_keep, i + 2)

            @block.gpsimd
            def _(pool):
                pool.memset(z[:, :, 0:PADW], 0.0).then_inc(s_set, 1)
                pool.memset(front.hT[:, 0:3], 0.0).then_inc(s_set, 1)
                pool.memset(edge[:, :, :], 1.0).then_inc(s_pool, 1)
                pool.wait_ge(s_pool, 1)
                for a in range(1, 4):
                    pool.memset(edge[32 * a:32 * a + 32, :, 0:a], 0.0).then_inc(s_pool, 1)
                pool.wait_ge(s_pool, 4)
                pool.sem_inc(s_keep, 1)
                with pool.Fori(0, NB) as i:
                    front.pool(pool, M, i)
                    pool.wait_ge(s_zP, i * G + G)
                    alone(pool, M)
                    pool.tensor_copy(front.hT[:, 0:3], front.hT[:, BL:BL + 3]).then_inc(s_hist, 1)
                    pool.wait_ge(s_z, i * G + G)
                    pool.tensor_tensor(z[:, :, PADW:PADW + 3], z[:, :, PADW:PADW + 3],
                                       edge[:, :, :].broadcast_to([P, G, 3]), ALU.mult).then_inc(s_edge, 1)
                    pool.wait_ge(s_edge, i + 1)
                    alone(pool, M)
                    pool.memset(edge[:, :, :], 1.0).then_inc(s_pool, 1)
                    pool.wait_ge(s_pool, i + 5)
                    pool.wait_ge(s_cP, i * 2 + 2)
                    alone(pool, M)
                    pool.tensor_copy(z[:, :, 0:PADW], z[:, :, BL:BL + PADW]).then_inc(s_keep, 1)
                    tail.pool(pool, M, i)

            @block.vector
            def _(dve):
                diag = M.w("c_diag").rearrange("p (a c) -> p a c", a=1).broadcast_to([P, 64, 32])
                dve.tensor_tensor(taps[:, :, :], M.w("c_taps").rearrange("p (n a) -> p n a", a=1).broadcast_to([P, 64, 32]),
                                  diag, ALU.mult).then_inc(s_set, 1)
                with dve.Fori(0, NB) as i:
                    own = Chain(dve, own_dve, i * PER)
                    front.dve(dve, M, own, i)
                    for half in range(2):
                        dve.wait_ge(s_th, i * 2 + half + 1)
                        own(dve.tensor_scalar(sg[:, half, :], th[:, half, :], 0.5, 0.5, ALU.mult, ALU.add))
                    own.wait()
                    for half, b in ((0, "c_ba"), (1, "c_bb")):
                        dve.scalar_tensor_tensor(ga[:, half, :], cP[half][:, :], M.w(b), sg[:, 1 - half, :],
                                                 ALU.add, ALU.mult).then_inc(s_ga, 1)
                    tail.dve(dve, M, own, lambda j: yP[:, j, :], i)
                    assert own.n == PER, own.n



STEPS = 5


def feed_forward(nc, M, layer, w_in, w_out, spiking):
    with ExitStack() as ctx:
        S = Scratch(nc, ctx, layer)
        front, tail = Front(S), Tail(S)
        hP = [S.ps(f"hP{k}", [P, BL]) for k in range(2)]
        yP = S.ps("yP", [P, TB, P])
        r = S.sb("relu", [P, 2, BL])
        a = S.sb("act", [P, FC, BL])
        cur = S.sb("current", [P, BL])
        mem = S.sb("membrane", [P, 2, BL])
        spk = S.sb("spike", [P, BL])
        cnt = S.sb("count", [P, 2, TB, P])
        s_hP = S.sem("hidden_in_psum")
        s_r = S.sem("relu_ready")
        s_a = S.sem("act_ready")
        s_y = S.sem("product_in_psum")
        own_dve = S.sem("own_dve")
        PER = 47 if spiking else 27
        with nc.Block() as block:
            @block.tensor
            def _(pe):
                with pe.Fori(0, NB) as i:
                    front.pe(pe, M, i)
                    pe.wait_ge(front.ready, i + 1)
                    for c in range(FC):
                        if c >= 2:
                            pe.wait_ge(s_a, i * FC + c - 1)
                        pe.matmul(hP[c % 2][:, :], M.w(w_in, c * P, P), front.hT[:, :], start=True, stop=True).then_inc(s_hP, 1)
                    pe.wait_ge(s_a, i * FC + FC)
                    for j in range(TB):
                        for c in range(FC):
                            last = pe.matmul(yP[:, j, :], a[:, c, j * P:(j + 1) * P], M.w(w_out, c * P, P),
                                             start=(c == 0), stop=(spiking and c == FC - 1))
                        if not spiking:
                            last = pe.matmul(yP[:, j, :], M.ones[0:1, :], M.row("f_b2"), start=False, stop=True)
                    last.then_inc(s_y if spiking else tail.y, 1)

            @block.scalar
            def _(act):
                with act.Fori(0, NB) as i:
                    front.act(act, i)
                    for c in range(FC):
                        act.wait_ge(s_hP, i * FC + c + 1)
                        if spiking:
                            if c >= 2:
                                act.wait_ge(s_a, i * FC + c - 1)
                            act.activation(r[:, c % 2, :], hP[c % 2][:, :], ACT.Relu).then_inc(s_r, 1)
                        else:
                            act.activation(a[:, c, :], hP[c % 2][:, :], ACT.Relu, bias=M.w("f_b1", c, 1)).then_inc(s_a, 1)

            @block.gpsimd
            def _(pool):
                with pool.Fori(0, NB) as i:
                    front.pool(pool, M, i)
                    tail.pool(pool, M, i)

            @block.vector
            def _(dve):
                with dve.Fori(0, NB) as i:
                    own = Chain(dve, own_dve, i * PER)
                    front.dve(dve, M, own, i)
                    if spiking:
                        for c in range(FC):
                            dve.wait_ge(s_r, i * FC + c + 1)
                            dve.tensor_tensor(a[:, c, :], r[:, c % 2, :], hP[c % 2][:, :], ALU.mult).then_inc(s_a, 1)
                        dve.wait_ge(s_y, i + 1)
                        y = yP[:, :, :].rearrange("p j f -> p (j f)")
                        c2 = [cnt[:, k, :, :].rearrange("p j f -> p (j f)") for k in range(2)]
                        own(dve.tensor_copy(cur[:, :], y))
                        own(dve.tensor_copy(mem[:, 0, :], y))
                        own.wait()
                        own(dve.tensor_scalar(c2[0], mem[:, 0, :], 1.0, None, ALU.is_gt))
                        own.wait()
                        for n in range(1, STEPS):
                            s = c2[0] if n == 1 else spk[:, :]
                            own(dve.scalar_tensor_tensor(mem[:, 1, :], mem[:, 0, :], 0.9, cur[:, :], ALU.mult, ALU.add))
                            own.wait()
                            own(dve.tensor_tensor(mem[:, 0, :], mem[:, 1, :], s, ALU.subtract))
                            own.wait()
                            own(dve.tensor_scalar(spk[:, :], mem[:, 0, :], 1.0, None, ALU.is_gt))
                            own.wait()
                            own(dve.tensor_tensor(c2[n % 2], c2[(n - 1) % 2], spk[:, :], ALU.add))
                        own.wait()
                        own(dve.tensor_scalar(c2[1], c2[(STEPS - 1) % 2], 1.0 / STEPS, None, ALU.mult))
                        own.wait()
                        dve.sem_inc(tail.y, 1)
                        tail.dve(dve, M, own, lambda j: cnt[:, 1, j, :], i)
                    else:
                        tail.dve(dve, M, own, lambda j: yP[:, j, :], i)
                    assert own.n == PER, own.n


def spiking_layer(nc, M):
    feed_forward(nc, M, "l3", "s_fc", "s_proj", True)


def last_layer(nc, M):
    feed_forward(nc, M, "l7", "f_w1", "f_w2", False)



def surprise_memory(nc, M):
    with ExitStack() as ctx:
        S = Scratch(nc, ctx, "l4")
        front, tail = Front(S), Tail(S)
        bank = [S.ps(f"bank{k}", [P, BL]) for k in range(3)]
        yP = S.ps("yP", [P, TB, P])
        q, k_, g, dec = (S.sb(n, [P, BL]) for n in ("q", "k", "surprise", "decay"))
        half = S.sb("tanh_half", [P, BL])
        m1 = S.sb("m1", [32, BL])
        hb = S.sb("half_bias", [P, 1])
        u = S.sb("u", [P, 2, BL])
        st = S.sb("state", [P, 2, BL])
        last_state = S.sb("last_state", [P, D])
        prod = S.sb("prod", [P, D, BL])
        y = S.sb("y", [P, TB, P])
        sq = S.sb("squares", [P, P])
        ms = S.sb("mean_square", [P, 2, TB])
        rms = S.sb("rms", [P, TB])
        yn = S.sb("yn", [P, TB, P])
        ynT = S.sb("ynT", [P, BL])
        r = S.sb("relu", [P, 2, BL])
        a = S.sb("act", [P, FC, BL])
        out = S.sb("out", [P, TB, P])
        s_m1P = S.sem("m1_in_psum")
        s_m1 = S.sem("m1_ready")
        s_gP = S.sem("surprise_in_psum")
        s_g = S.sem("tanh_ready")
        s_qP = S.sem("q_in_psum")
        s_q = S.sem("q_ready")
        s_kP = S.sem("k_in_psum")
        s_k = S.sem("gated_k_ready")
        s_vP = S.sem("v_in_psum")
        s_u = S.sem("v_bank_used")
        s_st = S.sem("state_ready")
        s_prod = S.sem("q_times_state")
        s_yP = S.sem("y_in_psum")
        s_y = S.sem("y_in_sbuf")
        s_ms = S.sem("mean_square_ready")
        s_rms = S.sem("rms_ready")
        s_yn = S.sem("yn_ready")
        s_ynP = S.sem("yn_turned")
        s_ynT = S.sem("ynT_ready")
        s_hP = S.sem("hidden_in_psum")
        s_r = S.sem("relu_ready")
        s_a = S.sem("act_ready")
        s_mlp = S.sem("mlp_in_psum")
        own_dve = S.sem("own_dve")
        own_act = S.sem("own_act")
        FIRST, PER = 2, 64
        with nc.Block() as block:
            @block.tensor
            def _(pe):
                with pe.Fori(0, NB) as i:
                    front.pe(pe, M, i)
                    pe.wait_ge(front.ready, i + 1)
                    hT = front.hT[:, :]
                    pe.matmul(bank[0][0:32, :], M.w("g_m1"), hT, start=True, stop=True).then_inc(s_m1P, 1)
                    pe.matmul(bank[1][:, :], M.w("g_k"), hT, start=True, stop=True).then_inc(s_kP, 1)
                    pe.matmul(bank[2][:, :], M.w("g_q"), hT, start=True, stop=True).then_inc(s_qP, 1)
                    pe.wait_ge(s_m1, i + 1)
                    pe.matmul(bank[0][:, :], M.w("g_m2")[0:32, :], m1[:, :], start=True, stop=True).then_inc(s_gP, 1)
                    pe.wait_ge(s_k, i + 1)
                    pe.wait_ge(s_q, i + 1)
                    for j in range(D):
                        if j >= 2:
                            pe.wait_ge(s_u, i * D + j - 1)
                        pe.matmul(bank[1 + j % 2][:, :], M.w("g_v", j * P, P), hT, start=True, stop=True).then_inc(s_vP, 1)
                    pe.wait_ge(s_prod, i * D + D)
                    for t in range(TB):
                        for j in range(D):
                            last = pe.matmul(yP[:, t, :], prod[:, j, t * P:(t + 1) * P], M.w("g_proj", j * P, P),
                                             start=(j == 0), stop=(j == D - 1))
                    last.then_inc(s_yP, 1)
                    pe.wait_ge(s_yn, i + 1)
                    turn(pe, M, bank[0], yn).then_inc(s_ynP, 1)
                    pe.wait_ge(s_ynT, i + 1)
                    for c in range(FC):
                        if c >= 2:
                            pe.wait_ge(s_a, i * FC + c - 1)
                        pe.matmul(bank[1 + c % 2][:, :], M.w("g_fc", c * P, P), ynT[:, :], start=True, stop=True).then_inc(s_hP, 1)
                    pe.wait_ge(s_a, i * FC + FC)
                    for t in range(TB):
                        for c in range(FC):
                            last = pe.matmul(yP[:, t, :], a[:, c, t * P:(t + 1) * P], M.w("g_cp", c * P, P),
                                             start=(c == 0), stop=(c == FC - 1))
                    last.then_inc(s_mlp, 1)

            @block.scalar
            def _(act):
                act.activation(hb[:, :], M.w("g_bm2"), ACT.Copy, scale=0.5).then_inc(own_act, 1)
                act.wait_ge(own_act, 1)
                with act.Fori(0, NB) as i:
                    front.act(act, i)
                    act.wait_ge(s_m1P, i + 1)
                    act.activation(m1[:, :], bank[0][0:32, :], ACT.Relu, bias=M.w("g_bm1")[0:32, :]).then_inc(s_m1, 1)
                    act.wait_ge(s_qP, i + 1)
                    act.copy(q[:, :], bank[2][:, :]).then_inc(s_q, 1)
                    act.wait_ge(s_gP, i + 1)
                    act.activation(half[:, :], bank[0][:, :], ACT.Tanh, scale=0.5, bias=hb[:, :]).then_inc(s_g, 1)
                    act.wait_ge(s_yP, i + 1)
                    act.copy(y[:, :, :], yP[:, :, :]).then_inc(s_y, 1)
                    act.wait_ge(s_ynP, i + 1)
                    act.copy(ynT[:, :], bank[0][:, :]).then_inc(s_ynT, 1)
                    for c in range(FC):
                        act.wait_ge(s_hP, i * FC + c + 1)
                        if c >= 2:
                            act.wait_ge(s_a, i * FC + c - 1)
                        act.activation(r[:, c % 2, :], bank[1 + c % 2][:, :], ACT.Relu).then_inc(s_r, 1)

            @block.gpsimd
            def _(pool):
                with pool.Fori(0, NB) as i:
                    front.pool(pool, M, i)
                    for j in range(D):
                        pool.wait_ge(s_st, i * D + j + 1)
                        pool.tensor_tensor(prod[:, j, :], q[:, :], st[:, j % 2, :], ALU.mult).then_inc(s_prod, 1)
                    pool.wait_ge(s_ms, i + 1)
                    pool.tensor_tensor(rms[:, :], ms[:, 1, :], M.mhalf[:, 0:TB], ALU.pow).then_inc(s_rms, 1)
                    tail.pool(pool, M, i)

            @block.vector
            def _(dve):
                first = Chain(dve, own_dve)
                first(dve.memset(last_state[:, :], 0.0))
                first(dve.memset(ms[:, :, :], 0.0))
                first.wait()
                assert first.n == FIRST
                with dve.Fori(0, NB) as i:
                    own = Chain(dve, own_dve, i * PER + FIRST)
                    front.dve(dve, M, own, i)
                    dve.wait_ge(s_g, i + 1)
                    own(dve.tensor_scalar(g[:, :], half[:, :], 0.5, 0.5, ALU.mult, ALU.add))
                    own.wait()
                    own(dve.tensor_scalar(dec[:, :], g[:, :], -1.0, 1.0, ALU.mult, ALU.add))
                    dve.wait_ge(s_kP, i + 1)
                    own(dve.tensor_tensor(k_[:, :], g[:, :], bank[1][:, :], ALU.mult))
                    own.wait()
                    dve.sem_inc(s_k, 1)
                    dve.wait_ge(s_q, i + 1)
                    for j in range(D):
                        dve.wait_ge(s_vP, i * D + j + 1)
                        own(dve.tensor_tensor(u[:, j % 2, :], k_[:, :], bank[1 + j % 2][:, :], ALU.mult))
                        own.wait()
                        dve.sem_inc(s_u, 1)
                        if j >= 2:
                            dve.wait_ge(s_prod, i * D + j - 1)
                        own(dve.tensor_tensor_scan(st[:, j % 2, :], dec[:, :], u[:, j % 2, :], last_state[:, j:j + 1], ALU.mult, ALU.add))
                        own.wait()
                        dve.sem_inc(s_st, 1)
                        own(dve.tensor_copy(last_state[:, j:j + 1], st[:, j % 2, BL - 1:BL]))
                    dve.wait_ge(s_y, i + 1)
                    for t in range(TB):
                        own(dve.tensor_tensor_reduce(out=sq[:, :], in0=y[:, t, :], in1=y[:, t, :], scale=1.0, scalar=0.0,
                                                     op0=ALU.mult, op1=ALU.add, accum_out=ms[:, 0, t:t + 1]))
                        own.wait()
                    own(dve.tensor_scalar(ms[:, 1, :], ms[:, 0, :], 1.0 / P, float(np.finfo(np.float32).eps), ALU.mult, ALU.add))
                    own.wait()
                    dve.sem_inc(s_ms, 1)
                    dve.wait_ge(s_rms, i + 1)
                    for t in range(TB):
                        own(dve.tensor_scalar(yn[:, t, :], y[:, t, :], rms[:, t:t + 1], None, ALU.mult))
                    own.wait()
                    dve.sem_inc(s_yn, 1)
                    for c in range(FC):
                        dve.wait_ge(s_r, i * FC + c + 1)
                        dve.tensor_tensor(a[:, c, :], r[:, c % 2, :], bank[1 + c % 2][:, :], ALU.mult).then_inc(s_a, 1)
                    dve.wait_ge(s_mlp, i + 1)
                    own(dve.tensor_tensor(out[:, :, :], y[:, :, :], yP[:, :, :], ALU.add))
                    own.wait()
                    dve.sem_inc(tail.y, 1)
                    tail.dve(dve, M, own, lambda j: out[:, j, :], i)
                    assert own.n == PER, own.n



def channel_mix(nc, M):
    with ExitStack() as ctx:
        S = Scratch(nc, ctx, "l5")
        front, tail = Front(S, pad=1), Tail(S)
        kP = S.ps("kP", [P, BL])
        rP = S.ps("rP", [P, TB, P])
        vP = S.ps("vP", [P, TB, P])
        rest = S.sb("one_minus_mu", [P, 2])
        now = S.sb("now", [P, 2, BL])
        xr = S.sb("xr", [P, BL])
        xk = S.sb("xk", [P, BL])
        relu = S.sb("relu", [P, BL])
        ka = S.sb("k_act", [P, BL])
        half = S.sb("tanh_half", [P, TB, P])
        r = S.sb("r", [P, TB, P])
        y = S.sb("y", [P, TB, P])
        s_mix = S.sem("mixed")
        s_kP = S.sem("k_in_psum")
        s_rP = S.sem("r_in_psum")
        s_relu = S.sem("relu_ready")
        s_ka = S.sem("k_act_ready")
        s_r = S.sem("tanh_ready")
        s_vP = S.sem("v_in_psum")
        own_dve = S.sem("own_dve")
        FIRST, PER = 3, 34
        with nc.Block() as block:
            @block.tensor
            def _(pe):
                with pe.Fori(0, NB) as i:
                    front.pe(pe, M, i)
                    pe.wait_ge(s_mix, i + 1)
                    pe.matmul(kP[:, :], M.w("r_k"), xk[:, :], start=True, stop=True).then_inc(s_kP, 1)
                    for j in range(TB):
                        last = pe.matmul(rP[:, j, :], xr[:, j * P:(j + 1) * P], M.w("r_r"), start=True, stop=True)
                    last.then_inc(s_rP, 1)
                    pe.wait_ge(s_ka, i + 1)
                    for j in range(TB):
                        last = pe.matmul(vP[:, j, :], ka[:, j * P:(j + 1) * P], M.w("r_v"), start=True, stop=True)
                    last.then_inc(s_vP, 1)

            @block.scalar
            def _(act):
                with act.Fori(0, NB) as i:
                    front.act(act, i)
                    act.wait_ge(s_kP, i + 1)
                    act.activation(relu[:, :], kP[:, :], ACT.Relu).then_inc(s_relu, 1)
                    act.wait_ge(s_rP, i + 1)
                    act.activation(half[:, :, :], rP[:, :, :], ACT.Tanh, scale=0.5).then_inc(s_r, 1)

            @block.gpsimd
            def _(pool):
                with pool.Fori(0, NB) as i:
                    front.pool(pool, M, i)
                    tail.pool(pool, M, i)

            @block.vector
            def _(dve):
                first = Chain(dve, own_dve)
                mu = [M.w("r_mur"), M.w("r_muk")]
                for k in range(2):
                    first(dve.tensor_scalar(rest[:, k:k + 1], mu[k], -1.0, 1.0, ALU.mult, ALU.add))
                first(dve.memset(front.hT[:, 0:1], 0.0))
                first.wait()
                assert first.n == FIRST
                with dve.Fori(0, NB) as i:
                    own = Chain(dve, own_dve, i * PER + FIRST)
                    front.dve(dve, M, own, i)
                    dve.wait_ge(front.ready, i + 1)
                    for k, dst in ((0, xr), (1, xk)):
                        own(dve.tensor_scalar(now[:, k, :], front.hT[:, 1:1 + BL], mu[k], None, ALU.mult))
                        own.wait()
                        own(dve.scalar_tensor_tensor(dst[:, :], front.hT[:, 0:BL], rest[:, k:k + 1], now[:, k, :], ALU.mult, ALU.add))
                    own.wait()
                    dve.sem_inc(s_mix, 1)
                    own(dve.tensor_copy(front.hT[:, 0:1], front.hT[:, BL:BL + 1]))
                    dve.wait_ge(s_relu, i + 1)
                    dve.tensor_tensor(ka[:, :], relu[:, :], kP[:, :], ALU.mult).then_inc(s_ka, 1)
                    dve.wait_ge(s_r, i + 1)
                    own(dve.tensor_scalar(r[:, :, :], half[:, :, :], 0.5, 0.5, ALU.mult, ALU.add))
                    own.wait()
                    dve.wait_ge(s_vP, i + 1)
                    own(dve.tensor_tensor(y[:, :, :], r[:, :, :], vP[:, :, :], ALU.mult))
                    own.wait()
                    dve.sem_inc(tail.y, 1)
                    tail.dve(dve, M, own, lambda j: y[:, j, :], i)
                    assert own.n == PER, own.n



LR = 1e-3
NCH = NT
GS = 2.0 / P
QUICK = 6
TOL_A, TOL_E = 2.0 ** -20, 2.0 ** -18


def test_time_mlp(nc, M):
    with ExitStack() as ctx:
        S = Scratch(nc, ctx, "l6")
        M.hT = S.sb("hT_all", [P, T])
        M.kT = S.sb("kT_all", [P, T])
        M.vT = S.sb("vT_all", [P, T])
        M.M1 = S.sb("M1_all", [P, T])
        M.Kt = S.sb("K_all", [P, T])
        M.W1, M.W2h, M.W2T = (S.sb(n, [P, P]) for n in ("W1", "W2_half", "W2T"))
        M.before4, M.before2 = S.sb("before4", [P, P]), S.sb("before2", [P, P])
        M.b1, M.b2 = S.sb("b1", [P, 1]), S.sb("b2", [P, 1])
        keys_and_values(nc, M)
        learn(nc, M)
        answer(nc, M)


def keys_and_values(nc, M):
    with ExitStack() as ctx:
        S = Scratch(nc, ctx, "l6a")
        front = Front(S)
        kvP = [S.ps(f"kvP{k}", [P, BL]) for k in range(2)]
        gramP = S.ps("gramP", [P, TB, P])
        keyP = S.ps("keyP", [P, BL])
        k4 = S.sb("k_block", [P, BL])
        s_kvP = S.sem("kv_in_psum")
        s_k = S.sem("k_ready")
        s_gram = S.sem("gram_in_psum")
        s_m1 = S.sem("gram_masked")
        s_keyP = S.sem("keys_turned")
        s_key = S.sem("keys_ready")
        own_dve = S.sem("own_dve")
        PER = 13
        with nc.Block() as block:
            @block.tensor
            def _(pe):
                with pe.Fori(0, NB) as i:
                    front.pe(pe, M, i)
                    pe.wait_ge(front.ready, i + 1)
                    for n in range(2):
                        last = pe.matmul(kvP[n][:, :], M.w("t_kv", n * P, P), front.hT[:, :], start=True, stop=True)
                    last.then_inc(s_kvP, 1)
                    pe.wait_ge(s_k, i + 1)
                    for j in range(TB):
                        kj = k4[:, j * P:(j + 1) * P]
                        last = pe.matmul(gramP[:, j, :], kj, kj, start=True, stop=True)
                    last.then_inc(s_gram, 1)
                    for j in range(TB):
                        last = pe.transpose(keyP[:, j * P:(j + 1) * P], k4[:, j * P:(j + 1) * P], M.eye)
                    last.then_inc(s_keyP, 1)
                    pe.wait_ge(s_key, i + 1)
                    pe.wait_ge(s_m1, i + 1)

            @block.scalar
            def _(act):
                with act.Fori(0, NB) as i:
                    front.act(act, i)
                    act.copy(M.hT[:, bass.ts(i, BL)], front.bank[:, :])
                    act.wait_ge(s_kvP, i + 1)
                    act.copy(k4[:, :], kvP[0][:, :]).then_inc(s_k, 1)
                    act.copy(M.kT[:, bass.ts(i, BL)], kvP[0][:, :])
                    act.copy(M.vT[:, bass.ts(i, BL)], kvP[1][:, :])
                    act.wait_ge(s_keyP, i + 1)
                    act.copy(M.Kt[:, bass.ts(i, BL)], keyP[:, :]).then_inc(s_key, 1)

            @block.gpsimd
            def _(pool):
                with pool.Fori(0, NB) as i:
                    front.pool(pool, M, i)

            @block.vector
            def _(dve):
                own = Chain(dve, own_dve)
                own(dve.tensor_scalar(M.before4[:, :], M.w("t_before"), -LR / 4, None, ALU.mult))
                own(dve.tensor_scalar(M.before2[:, :], M.w("t_before"), -LR / 2, None, ALU.mult))
                own.wait()
                with dve.Fori(0, NB) as i:
                    own = Chain(dve, own_dve, i * PER + 2)
                    front.dve(dve, M, own, i)
                    dve.wait_ge(s_gram, i + 1)
                    dve.scalar_tensor_tensor(M.M1[:, bass.ts(i, BL)].rearrange("p (t q) -> p t q", t=TB), gramP[:, :, :], 1.0,
                                             M.before4[:, :].rearrange("p (a q) -> p a q", a=1).broadcast_to([P, TB, P]),
                                             ALU.add, ALU.mult).then_inc(s_m1, 1)
                    assert own.n == PER, own.n


def learn(nc, M):
    with ExitStack() as ctx:
        S = Scratch(nc, ctx, "l6b")
        hTP, hP, oP, gP, aaP, eeP, etP, dP = (S.ps(n, [P, BL]) for n in ("hTP", "hP", "oP", "gP", "aaP", "eeP", "etP", "dP"))
        b_ = lambda x: x[:, 0:P]
        names = ("M1", "Kt", "hb", "hbt", "ht", "tT", "tt", "w", "z", "bv", "M2", "M3", "E", "G4")
        M1, Kt, hb, hbt, ht, tT, tt, w, z, bv, M2, M3, E, G4 = (S.sb(n, [P, P]) for n in names)
        A2 = S.sb("A2", [P, 2, P])
        ae = [S.sb(n, [P, 2, P]) for n in ("ae_before", "ae_last")]
        diff, square, changes, sizes = (S.sb(n, [P, 2, P]) for n in ("diff", "square", "changes", "sizes"))
        red = S.sb("reduced", [P, 2, 2])
        bad = S.sb("not_settled", [P, 2])
        total = S.sb("total", [P, 1])
        allones = S.sb("all_ones", [P, P])
        flag = S.sb("flag", [P, 1], I32)
        sem = lambda n: S.sem(n)
        s_hT = sem("hT_in_psum")
        s_tT = sem("tanhT_ready")
        s_aT = sem("aT_ready")
        s_hP = sem("h_in_psum")
        s_ht = sem("h_ready")
        s_tt = sem("tanh_ready")
        s_A = sem("A_ready")
        s_w = sem("w_ready")
        s_z = sem("derivative_ready")
        s_o = sem("o_in_psum")
        s_aa = sem("aa_in_psum")
        s_M2 = sem("M2_ready")
        s_e = sem("eT_ready")
        s_g = sem("g_in_psum")
        s_G = sem("G_ready")
        s_ee = sem("ee_in_psum")
        s_M3 = sem("M3_ready")
        s_et = sem("e_turned")
        s_E = sem("E_ready")
        own_pool = sem("own_pool")
        s_h0 = sem("start_h_in_psum")
        s_hb = sem("start_h_ready")
        s_bv = sem("bv_ready")
        s_m1 = sem("gram_copied")
        s_d1 = sem("w1_update_in_psum")
        s_d2 = sem("w2_update_in_psum")
        s_w1 = sem("w1_updated")
        s_w2 = sem("w2_updated")
        s_diff = sem("change_taken")
        own_w = sem("own_dve_updates")
        s_set = sem("pass_set_up")
        s_all = sem("pass_checked")
        s_bad = sem("not_settled_ready")
        s_sum = sem("not_settled_summed")
        s_flag = sem("flag_ready")
        own_set = sem("own_dve_set_up")
        N_SET, N_CHECK, POOL_CH = 8, 8, 5

        def set_up(dve, first):
            own = Chain(dve, own_set, 1 if first else 1 + N_SET + N_CHECK)
            own(dve.tensor_copy(M.W1[:, :], M.w("t_w1")))
            own(dve.tensor_scalar(M.W2h[:, :], M.w("t_w2"), 0.5, None, ALU.mult))
            own(dve.tensor_copy(M.W2T[:, :], M.w("t_w2t")))
            own(dve.tensor_copy(M.b1[:, :], M.w("t_b1")))
            own(dve.tensor_copy(M.b2[:, :], M.w("t_b2")))
            own(dve.memset(changes[:, :, :], 0.0))
            own(dve.memset(sizes[:, :, :], 0.0))
            own.wait()
            own(dve.memset(bad[:, :], 0.0))
            own.wait()
            assert own.n == N_SET
            dve.sem_inc(s_set, 1)

        class Step:

            def __init__(self, c, it, NI, n0, k0, q0, p, first=False, last=False):
                self.n = n0 + c * NI + it
                self.k = k0 + c * (NI - 1) + it
                self.q = q0 + c * (NI - 1) + it - 1
                self.p, self.first, self.last = p, first, last
                self.ae = ae[1 if last else 0]

        def steps(eng, c, NI, n0, k0, q0, body):
            body(Step(c, 0, NI, n0, k0, q0, 0, first=True))
            with eng.Fori(0, (NI - 2) // 2) as m:
                for r in range(2):
                    body(Step(c, m * 2 + (r + 1), NI, n0, k0, q0, (r + 1) % 2))
            body(Step(c, NI - 1, NI, n0, k0, q0, (NI - 1) % 2, last=True))

        def tensor_pass(pe, NI, n0, k0, q0, c0):
            def body(s, c=None):
                if s.first:
                    pe.transpose(b_(hP), hb[:, :], M.eye).then_inc(s_hP, 1)
                else:
                    pe.wait_ge(s_G, s.n)
                    pe.matmul(b_(hTP), G4[:, :], M1[:, :], start=False, stop=True).then_inc(s_hT, 1)
                    pe.matmul(b_(hP), M1[:, :], G4[:, :], start=True, stop=True).then_inc(s_hP, 1)
                    pe.wait_ge(s_E, s.n)
                    pe.wait_ge(s_M2, s.k)
                    pe.matmul(b_(oP), E[:, :], M2[:, :], start=True, stop=False)
                pe.wait_ge(s_aT, s.n + 1)
                pe.matmul(b_(oP), M.W2h[:, :], s.ae[:, 0, :], start=s.first, stop=True).then_inc(s_o, 1)
                if not s.last:
                    pe.matmul(b_(aaP), s.ae[:, 0, :], s.ae[:, 0, :], start=True, stop=True).then_inc(s_aa, 1)
                    pe.matmul(b_(hTP), M.eye, hb[:, :], start=True, stop=False)
                if not s.first:
                    pe.wait_ge(s_M3, s.k)
                    pe.matmul(b_(gP), M3[:, :], A2[:, 1 - s.p, :], start=True, stop=False)
                pe.wait_ge(s_e, s.n + 1)
                pe.matmul(b_(gP), s.ae[:, 1, :], M.W2T[:, :], start=s.first, stop=True).then_inc(s_g, 1)
                pe.transpose(b_(etP), s.ae[:, 1, :], M.eye).then_inc(s_et, 1)
                if not s.last:
                    pe.matmul(b_(eeP), s.ae[:, 1, :], s.ae[:, 1, :], start=True, stop=True).then_inc(s_ee, 1)
                pe.wait_ge(s_ht, s.n + 1)
                if s.first:
                    alone(pe, M)
                    pe.wait_ge(s_m1, c0 + c + 1)
                    alone(pe, M)

            pe.wait_ge(s_set, 1 if n0 == 0 else 2)
            with pe.Fori(0, NCH) as c:
                pe.wait_ge(s_w1, c0 + c + 1)
                pe.matmul(b_(hTP), M.W1[:, :], M.kT[:, bass.ts(c, P)], start=True, stop=True).then_inc(s_h0, 1)
                pe.wait_ge(s_w2, c0 + c + 1)
                pe.wait_ge(s_hb, c0 + c + 1)
                steps(pe, c, NI, n0, k0, q0, lambda s: body(s, c))
                pe.wait_ge(s_G, n0 + c * NI + NI)
                pe.matmul(b_(hTP), Kt[:, :], G4[:, :], start=True, stop=True)
                pe.matmul(hTP[:, P:P + 1], G4[:, :], allones[:, 0:1], start=True, stop=True).then_inc(s_d1, 1)
                pe.wait_ge(s_E, n0 + c * NI + NI)
                AL = A2[:, (NI - 1) % 2, :]
                pe.matmul(b_(dP), AL, E[:, :], start=True, stop=True)
                pe.matmul(dP[:, P:2 * P], E[:, :], AL, start=True, stop=True)
                pe.matmul(dP[:, 2 * P:2 * P + 1], E[:, :], allones[:, 0:1], start=True, stop=True).then_inc(s_d2, 1)

        def scalar_pass(act, NI, n0, k0, q0, c0):
            def body(s, c=None):
                if s.first:
                    act.wait_ge(s_hb, c0 + c + 1)
                    act.activation(tT[:, :], hb[:, :], ACT.Tanh, scale=0.5).then_inc(s_tT, 1)
                else:
                    act.wait_ge(s_hT, s.q + 1)
                    act.activation(tT[:, :], b_(hTP), ACT.Tanh, scale=0.5).then_inc(s_tT, 1)
                act.wait_ge(s_ht, s.n + 1)
                act.activation(tt[:, :], hbt[:, :] if s.first else ht[:, :], ACT.Tanh, scale=0.5).then_inc(s_tt, 1)
                if s.first:
                    act.wait_ge(s_d1, c0 + c + 1)
                    act.copy(M1[:, :], M.M1[:, bass.ts(c, P)])
                    act.copy(Kt[:, :], M.Kt[:, bass.ts(c, P)]).then_inc(s_m1, 1)
                act.wait_ge(s_et, s.n + 1)
                act.copy(E[:, :], b_(etP)).then_inc(s_E, 1)

            act.wait_ge(s_set, 1 if n0 == 0 else 2)
            with act.Fori(0, NCH) as c:
                steps(act, c, NI, n0, k0, q0, lambda s: body(s, c))

        def vector_pass(dve, NI, n0, k0, q0, c0):
            def body(s, c=None):
                aT, eT = s.ae[:, 0, :], s.ae[:, 1, :]
                if s.first:
                    dve.wait_ge(s_h0, c0 + c + 1)
                    dve.tensor_scalar(hb[:, :], b_(hTP), M.b1[:, :], None, ALU.add).then_inc(s_hb, 1)
                    dve.tensor_scalar(bv[:, :], M.vT[:, bass.ts(c, P)], M.b2[:, :], -GS, ALU.subtract, ALU.mult).then_inc(s_bv, 1)
                    dve.wait_ge(s_hP, s.n + 1)
                    dve.tensor_copy(hbt[:, :], b_(hP)).then_inc(s_ht, 1)
                    dve.wait_ge(s_diff, c0 + c + 1)
                dve.wait_ge(s_tT, s.n + 1)
                dve.scalar_tensor_tensor(aT, tT[:, :], 1.0, hb[:, :] if s.first else b_(hTP), ALU.add, ALU.mult).then_inc(s_aT, 1)
                if not s.first:
                    dve.wait_ge(s_hP, s.n + 1)
                    dve.tensor_tensor(ht[:, :], b_(hP), hbt[:, :], ALU.add).then_inc(s_ht, 1)
                dve.wait_ge(s_tt, s.n + 1)
                dve.scalar_tensor_tensor(A2[:, s.p, :], tt[:, :], 1.0, hbt[:, :] if s.first else ht[:, :], ALU.add, ALU.mult).then_inc(s_A, 1)
                dve.wait_ge(s_A, s.n + 1)
                dve.scalar_tensor_tensor(w[:, :], tt[:, :], 1.0, A2[:, s.p, :], ALU.subtract, ALU.mult).then_inc(s_w, 1)
                dve.wait_ge(s_o, s.n + 1)
                if s.first:
                    dve.wait_ge(s_bv, c0 + c + 1)
                dve.scalar_tensor_tensor(eT, b_(oP), GS, bv[:, :], ALU.mult, ALU.add).then_inc(s_e, 1)
                dve.wait_ge(s_w, s.n + 1)
                dve.scalar_tensor_tensor(z[:, :], tt[:, :], 2.0, w[:, :], ALU.mult, ALU.subtract).then_inc(s_z, 1)
                if not s.last:
                    dve.wait_ge(s_aa, s.k + 1)
                    dve.scalar_tensor_tensor(M2[:, :], b_(aaP), 4.0, M.before4[:, :], ALU.add, ALU.mult).then_inc(s_M2, 1)
                dve.wait_ge(s_g, s.n + 1)
                dve.wait_ge(s_z, s.n + 1)
                dve.scalar_tensor_tensor(G4[:, :], z[:, :], 2.0, b_(gP), ALU.add, ALU.mult).then_inc(s_G, 1)
                if not s.last:
                    dve.wait_ge(s_ee, s.k + 1)
                    dve.tensor_tensor(M3[:, :], b_(eeP), M.before2[:, :], ALU.mult).then_inc(s_M3, 1)

            with dve.Fori(0, NCH) as c:
                steps(dve, c, NI, n0, k0, q0, lambda s: body(s, c))
                dve.wait_ge(s_d1, c0 + c + 2)
                dve.scalar_tensor_tensor(M.W1[:, :], b_(hTP), -LR / 4, M.W1[:, :], ALU.mult, ALU.add)
                dve.scalar_tensor_tensor(M.b1[:, :], hTP[:, P:P + 1], -LR / 4, M.b1[:, :], ALU.mult, ALU.add).then_inc(s_w1, 1)
                dve.wait_ge(s_d2, c0 + c + 1)
                dve.scalar_tensor_tensor(M.b2[:, :], dP[:, 2 * P:2 * P + 1], -LR, M.b2[:, :], ALU.mult, ALU.add)
                dve.scalar_tensor_tensor(M.W2h[:, :], b_(dP), -LR / 4, M.W2h[:, :], ALU.mult, ALU.add)
                dve.scalar_tensor_tensor(M.W2T[:, :], dP[:, P:2 * P], -LR / 2, M.W2T[:, :], ALU.mult, ALU.add).then_inc(s_w2, 1)
                dve.wait_ge(s_w1, c0 + c + 2)
                dve.wait_ge(s_w2, c0 + c + 2)

        def pool_pass(pool, NI, n0, k0, q0, c0):
            pool.wait_ge(s_set, 1 if n0 == 0 else 2)
            with pool.Fori(0, NCH) as c:
                own = (c0 + c) * POOL_CH
                pool.wait_ge(s_e, n0 + c * NI + NI)
                pool.tensor_tensor(diff[:, :, :], ae[1][:, :, :], ae[0][:, :, :], ALU.subtract).then_inc(own_pool, 1)
                pool.tensor_tensor(square[:, :, :], ae[1][:, :, :], ae[1][:, :, :], ALU.mult).then_inc(own_pool, 1)
                pool.wait_ge(own_pool, own + 2)
                pool.sem_inc(s_diff, 1)
                pool.tensor_tensor(diff[:, :, :], diff[:, :, :], diff[:, :, :], ALU.mult).then_inc(own_pool, 1)
                pool.wait_ge(own_pool, own + 3)
                pool.tensor_tensor(changes[:, :, :], changes[:, :, :], diff[:, :, :], ALU.add).then_inc(own_pool, 1)
                pool.tensor_tensor(sizes[:, :, :], sizes[:, :, :], square[:, :, :], ALU.add).then_inc(own_pool, 1)
                pool.wait_ge(own_pool, own + 5)
            pool.sem_inc(s_all, 1)

        NQ = NCH * QUICK
        quick = (QUICK, 0, 0, 0, 0)
        full = (P, NQ, NQ - NCH, NQ - NCH, NCH)
        with nc.Block() as block:
            @block.tensor
            def _(pe):
                pe.sem_inc(s_d1, 1)
                tensor_pass(pe, *quick)
                pe.wait_ge(s_bad, 1)
                pe.matmul(dP[:, 0:2], allones[:, :], bad[:, :], start=True, stop=True).then_inc(s_sum, 1)
                pe.wait_ge(s_flag, 1)
                again = pe.value_load(flag[0:1, 0:1], min_val=0, max_val=1)
                with pe.If(again > 0):
                    tensor_pass(pe, *full)
                    pe.wait_ge(s_w2, 2 * NCH + 1)
                pe.nop()

            @block.scalar
            def _(act):
                scalar_pass(act, *quick)
                act.wait_ge(s_flag, 1)
                again = act.value_load(flag[0:1, 0:1], min_val=0, max_val=1)
                with act.If(again > 0):
                    scalar_pass(act, *full)
                    act.wait_ge(s_w2, 2 * NCH + 1)
                act.nop()

            @block.gpsimd
            def _(pool):
                pool.sem_inc(s_diff, 1)
                pool_pass(pool, *quick)
                pool.wait_ge(s_flag, 1)
                again = pool.value_load(flag[0:1, 0:1], min_val=0, max_val=1)
                with pool.If(again > 0):
                    pool_pass(pool, *full)
                    pool.wait_ge(s_w2, 2 * NCH + 1)
                pool.nop()

            @block.vector
            def _(dve):
                dve.memset(allones[:, :], 1.0).then_inc(own_set, 1)
                dve.wait_ge(own_set, 1)
                set_up(dve, True)
                dve.sem_inc(s_w1, 1)
                dve.sem_inc(s_w2, 1)
                vector_pass(dve, *quick)
                own = Chain(dve, own_set, 1 + N_SET)
                dve.wait_ge(s_all, 1)
                own(dve.tensor_reduce(red[:, 0, :], changes[:, :, :], AX.X, ALU.max))
                own(dve.tensor_reduce(red[:, 1, :], sizes[:, :, :], AX.X, ALU.max))
                own.wait()
                own(dve.tensor_scalar(red[:, 1, 0:1], red[:, 1, 0:1], TOL_A ** 2 / NCH, None, ALU.mult))
                own(dve.tensor_scalar(red[:, 1, 1:2], red[:, 1, 1:2], TOL_E ** 2 / NCH, None, ALU.mult))
                own.wait()
                own(dve.tensor_tensor(bad[:, :], red[:, 0, :], red[:, 1, :], ALU.is_gt))
                own.wait()
                dve.sem_inc(s_bad, 1)
                dve.wait_ge(s_sum, 1)
                own(dve.tensor_reduce(total[:, :], dP[:, 0:2], AX.X, ALU.add))
                own.wait()
                own(dve.tensor_scalar(flag[:, :], total[:, :], 0.5, None, ALU.is_gt))
                own.wait()
                own(dve.memset(M.spare[:, 0:1], 0.0))
                assert own.n == N_CHECK, own.n
                dve.sem_inc(s_flag, 1)
                again = dve.value_load(flag[0:1, 0:1], min_val=0, max_val=1)
                with dve.If(again > 0):
                    set_up(dve, False)
                    vector_pass(dve, *full)
                dve.nop()


def answer(nc, M):
    with ExitStack() as ctx:
        S = Scratch(nc, ctx, "l6c")
        tail = Tail(S)
        qP, hP, oP = (S.ps(n, [P, BL]) for n in ("qP", "hP", "oP"))
        yP = S.ps("yP", [P, TB, P])
        q, hs, yT = (S.sb(n, [P, BL]) for n in ("q", "hidden", "yT"))
        s_qP = S.sem("q_in_psum")
        s_q = S.sem("q_ready")
        s_hP = S.sem("hidden_in_psum")
        s_h = S.sem("hidden_ready")
        s_oP = S.sem("o_in_psum")
        s_yT = S.sem("yT_ready")
        own_dve = S.sem("own_dve")
        PER = 14
        with nc.Block() as block:
            @block.tensor
            def _(pe):
                with pe.Fori(0, NB) as i:
                    pe.matmul(qP[:, :], M.w("t_q"), M.hT[:, bass.ts(i, BL)], start=True, stop=True).then_inc(s_qP, 1)
                    pe.wait_ge(s_q, i + 1)
                    pe.matmul(hP[:, :], M.W1[:, :], q[:, :], start=True, stop=True).then_inc(s_hP, 1)
                    pe.wait_ge(s_h, i + 1)
                    pe.matmul(oP[:, :], M.W2h[:, :], hs[:, :], start=True, stop=True).then_inc(s_oP, 1)
                    pe.wait_ge(s_yT, i + 1)
                    for j in range(TB):
                        last = pe.transpose(yP[:, j, :], yT[:, j * P:(j + 1) * P], M.eye)
                    last.then_inc(tail.y, 1)
                    pe.wait_ge(tail.norm.done, i + 1)

            @block.scalar
            def _(act):
                with act.Fori(0, NB) as i:
                    act.wait_ge(s_qP, i + 1)
                    act.copy(q[:, :], qP[:, :]).then_inc(s_q, 1)
                    act.wait_ge(s_hP, i + 1)
                    act.activation(hs[:, :], hP[:, :], ACT.Silu, bias=M.b1[:, :]).then_inc(s_h, 1)
                    act.wait_ge(s_oP, i + 1)
                    act.activation(yT[:, :], oP[:, :], ACT.Identity, scale=2.0, bias=M.b2[:, :]).then_inc(s_yT, 1)

            @block.gpsimd
            def _(pool):
                with pool.Fori(0, NB) as i:
                    tail.pool(pool, M, i)

            @block.vector
            def _(dve):
                with dve.Fori(0, NB) as i:
                    own = Chain(dve, own_dve, i * PER)
                    tail.dve(dve, M, own, lambda j: yP[:, j, :], i)
                    assert own.n == PER, own.n


def build(nc, x, w, experts_w, rows, causal, out, layers=range(8)):
    with ExitStack() as ctx:
        M = Mem()
        M.ctx = ctx
        M.experts_w = experts_w
        load(nc, M, x, w, rows, causal)
        for n in layers:
            LAYERS[n](nc, M)
        store(nc, M, out)


LAYERS = [head_mix, causal_moe, long_conv, spiking_layer, surprise_memory, channel_mix, test_time_mlp, last_layer]


def host_layout(i):
    f = np.float32
    a = {k: np.asarray(v) for k, v in i.items()}
    part = {}
    part["eye"] = np.eye(P, dtype=f)
    part["l0_qkv"] = a["L0_attn_Wqkv"].T
    part["l0_proj"] = a["L0_attn_Wproj"].T
    for k, n in (("m_ln1w", "L0_ffn_ln1_w"), ("m_ln1b", "L0_ffn_ln1_b"), ("m_ln2w", "L0_ffn_ln2_w"),
                 ("m_ln2b", "L0_ffn_ln2_b"), ("c_ba", "L1_attn_b_a"), ("c_bb", "L1_attn_b_b"),
                 ("r_mur", "L2_ffn_mu_r"), ("r_muk", "L2_ffn_mu_k"), ("t_b1", "L3_attn_b1"), ("t_b2", "L3_attn_b2")):
        part[k] = a[n].reshape(P, 1)
    part["m_conv"] = a["L0_ffn_conv_w"].reshape(P, 3)
    part["m_qkv"] = a["L0_ffn_attn_w"]
    part["m_proj"] = a["L0_ffn_proj_w"]
    part["m_router"] = a["L0_ffn_router_w"]
    inv = (f(1.0) / np.power(f(10000.0), np.arange(0, D, 2, dtype=f) / f(D))).astype(f)
    ang = np.arange(T, dtype=f)[:, None] * inv[None, :]
    for k, fn in (("cos", np.cos), ("sin", np.sin)):
        part[k] = fn(ang).astype(f).reshape(NT, P, D // 2).transpose(1, 0, 2).reshape(P, -1)
    wv = a["L0_ffn_expert_wv"].transpose(1, 0, 2).reshape(P, -1)
    ep = a["L0_ffn_expert_proj"].reshape(NE, FC, P, P).transpose(2, 0, 1, 3).reshape(P, -1)
    experts_w = np.concatenate([wv, ep], axis=1)
    part["c_in"] = a["L1_attn_w_in"].T
    bi = a["L1_attn_b_in"].reshape(8, 1, 32)
    part["c_inb"] = np.concatenate([bi] * 4, axis=1).reshape(8, P).T
    taps = np.stack([a["L1_attn_w_a"].reshape(P, CK), a["L1_attn_w_b"].reshape(P, CK)])[:, :, ::-1]
    part["c_taps"] = taps.reshape(2, 4, 32, 8, 4).transpose(4, 2, 0, 1, 3).reshape(P, 64)
    part["c_diag"] = np.concatenate([np.eye(32, dtype=f)] * 4, axis=0)
    part["c_out"] = a["L1_attn_w_out"].T.reshape(2, P, P).transpose(1, 0, 2).reshape(P, -1)
    part["s_fc"] = a["L1_ffn_W_fc"].T
    part["s_proj"] = a["L1_ffn_W_proj"].T.reshape(FC, P, P).transpose(1, 0, 2).reshape(P, -1)
    part["g_q"], part["g_k"] = a["L2_attn_Wq"].T, a["L2_attn_Wk"].T
    wv = a["L2_attn_Wv"].T.reshape(P, H, D)
    part["g_v"] = np.stack([np.stack([wv[:, :, j]] * D, axis=2) for j in range(D)], axis=1).reshape(P, -1)
    part["g_m1"] = a["L2_attn_Wm1"].T
    z = lambda m: np.concatenate([m, np.zeros((P - m.shape[0], m.shape[1]), f)], axis=0)
    part["g_bm1"] = z(a["L2_attn_bm1"].reshape(32, 1))
    part["g_m2"] = z(np.stack([a["L2_attn_Wm2"].T] * D, axis=2).reshape(32, P))
    part["g_bm2"] = np.stack([a["L2_attn_bm2"]] * D, axis=1).reshape(P, 1)
    wp = a["L2_attn_Wproj"].T.reshape(H, D, P)
    part["g_proj"] = np.stack([np.stack([wp[:, j]] * D, axis=1).reshape(P, P) for j in range(D)], axis=1).reshape(P, -1)
    part["g_fc"] = a["L2_attn_Wfc"].T
    part["g_cp"] = a["L2_attn_Wcp"].T.reshape(FC, P, P).transpose(1, 0, 2).reshape(P, -1)
    part["r_r"], part["r_k"], part["r_v"] = a["L2_ffn_W_r"].T, a["L2_ffn_W_k"].T, a["L2_ffn_W_v"].T
    part["t_q"], part["t_kv"] = a["L3_attn_W_Q"], a["L3_attn_W_KV"]
    part["t_w1"], part["t_w2"], part["t_w2t"] = a["L3_attn_W1"], a["L3_attn_W2"], a["L3_attn_W2"].T
    part["t_before"] = np.triu(np.ones((P, P), f), 1)
    part["f_w1"] = a["L3_ffn_w1"]
    part["f_b1"] = a["L3_ffn_b1"].reshape(FC, P).T
    part["f_w2"] = a["L3_ffn_w2"].reshape(FC, P, P).transpose(1, 0, 2).reshape(P, -1)
    w = np.concatenate([part[n] for n, _ in PACK], axis=1)
    rows = np.concatenate([a["L0_attn_bproj"], a["L1_attn_b_out"], a["L3_ffn_b2"]]).reshape(1, -1)
    x = a["L0_attn_x"].reshape(T, P)
    return {"x": x, "w": w, "experts_w": experts_w, "rows": rows}


def kernel(**inputs):
    import concourse.bacc as _bacc
    from concourse.bass_utils import run_bass_kernel_spmd as _run

    arrays = host_layout(inputs)
    arrays["causal"] = np.triu(np.full((P, P), NEG, np.float32), 1).astype(mybir.dt.np(BF16))
    nc = _bacc.Bacc("TRN2", target_bir_lowering=False, num_devices=1)
    arrays = {f"in_{k}_dram": np.ascontiguousarray(v) for k, v in arrays.items()}
    args = [nc.dram_tensor(k, v.shape, mybir.dt.from_np(v.dtype), kind="ExternalInput").ap() for k, v in arrays.items()]
    out = nc.dram_tensor("out_0_dram", (T, P), F32, kind="ExternalOutput").ap()
    build(nc, *args, out)
    r = _run(nc, [arrays], core_ids=[0])
    return r.results[0]["out_0_dram"].reshape(1, T, P)
```

```python
from contextlib import ExitStack

import numpy as np
import concourse.bass as bass
from concourse import mybir

F32 = mybir.dt.float32
BF16 = mybir.dt.bfloat16
I32 = mybir.dt.int32
ALU = mybir.AluOpType
ACT = mybir.ActivationFunctionType
AX = mybir.AxisListType

P = 128
T = 2048
NT = T // P
TB = 4
BL = TB * P
NB = T // BL
H = 16
D = P // H
EPS = 1e-5
FF = 512
FC = FF // P
NE = 4
CK = 32
NEG = -1e30

PACK = [
    ("eye", P), ("l0_qkv", 3 * P), ("l0_proj", P),
    ("m_ln1w", 1), ("m_ln1b", 1), ("m_ln2w", 1), ("m_ln2b", 1), ("m_conv", 3),
    ("m_qkv", 3 * P), ("m_proj", P), ("m_router", NE), ("cos", NT * D // 2), ("sin", NT * D // 2),
    ("c_in", 2 * P), ("c_inb", 8), ("c_taps", 64), ("c_diag", 32), ("c_ba", 1), ("c_bb", 1),
    ("c_out", 2 * P), ("s_fc", FF), ("s_proj", FC * P),
    ("g_q", P), ("g_k", P), ("g_v", D * P), ("g_m1", 32), ("g_bm1", 1), ("g_m2", P), ("g_bm2", 1),
    ("g_proj", D * P), ("g_fc", FF), ("g_cp", FC * P),
    ("r_r", P), ("r_k", P), ("r_v", P), ("r_mur", 1), ("r_muk", 1),
    ("t_q", P), ("t_kv", 2 * P), ("t_w1", P), ("t_w2", P), ("t_w2t", P), ("t_b1", 1), ("t_b2", 1),
    ("t_before", P),
    ("f_w1", FF), ("f_b1", FC), ("f_w2", FC * P),
]
AT = {}
_at = 0
for _name, _n in PACK:
    AT[_name] = (_at, _n)
    _at += _n
NW = _at
WV, EPROJ = NE * 2 * FF, NE * FC * P
ROWS = ["l0_bproj", "c_bout", "f_b2"]


class Mem:
    pass


class Chain:

    def __init__(self, eng, sem, base=0):
        self.eng, self.sem, self.base, self.n = eng, sem, base, 0

    def __call__(self, ins):
        self.n += 1
        return ins.then_inc(self.sem, 1)

    def wait(self):
        self.eng.wait_ge(self.sem, self.base + self.n)


def alone(eng, M):
    eng.sem_inc(M.s_alone, 1)


class Scratch:

    def __init__(self, nc, ctx, layer):
        self.nc, self.ctx, self.layer, self.sems = nc, ctx, layer, []
        ctx.callback(self.clear)

    def clear(self):
        if self.sems:
            self.nc.clear_and_free_semaphores(self.sems)
            self.nc.all_engine_barrier()

    def sb(self, name, shape, dt=F32):
        return self.ctx.enter_context(self.nc.sbuf_tensor(f"{self.layer}_{name}", shape, dt))

    def ps(self, name, shape, dt=F32):
        return self.ctx.enter_context(self.nc.psum_tensor(f"{self.layer}_{name}", shape, dt))

    def sem(self, name):
        self.sems.append(self.nc.alloc_semaphore(f"{self.layer}_{name}"))
        return self.sems[-1]



def norm_stats(dve, M, own, src, st, mv, eps=EPS):
    for j in range(TB):
        own(dve.bn_stats(st[:, j, :], src(j)))
    own.wait()
    dve.memset(M.spare[:, 0:1], 0.0)
    for j in range(TB):
        own(dve.bn_aggr(mv[:, j, :], st[:, j, :]))
    own.wait()
    return own(dve.tensor_scalar(mv[:, :, 1], mv[:, :, 1], eps, None, ALU.add))


def norm_apply(dve, own, src, mv, rstd, dst):
    for j in range(TB):
        own(dve.tensor_scalar(dst[:, j, :], src(j), mv[:, j, 0:1], rstd[:, j:j + 1], ALU.subtract, ALU.mult))


class Norm:

    def __init__(self, S, name, eps=EPS):
        self.eps = eps
        self.st = S.sb(name + "_st", [P, TB, 6])
        self.mv = S.sb(name + "_mv", [P, TB, 2])
        self.rstd = S.sb(name + "_rstd", [P, TB])
        self.out = S.sb(name + "_out", [P, TB, P])
        self.var = S.sem(name + "_var_ready")
        self.inv = S.sem(name + "_rstd_ready")
        self.done = S.sem(name + "_normalised")

    def stats(self, dve, M, own, src):
        norm_stats(dve, M, own, src, self.st, self.mv, self.eps)
        own.wait()
        dve.sem_inc(self.var, 1)

    def apply(self, dve, own, src, i):
        dve.wait_ge(self.inv, i + 1)
        norm_apply(dve, own, src, self.mv, self.rstd, self.out)
        own.wait()

    def dve(self, dve, M, own, src, i):
        self.stats(dve, M, own, src)
        self.apply(dve, own, src, i)

    def pool(self, pool, M, i):
        pool.wait_ge(self.var, i + 1)
        pool.tensor_tensor(self.rstd[:, :], self.mv[:, :, 1], M.mhalf[:, 0:TB], ALU.pow).then_inc(self.inv, 1)


def turn(pe, M, dst, src):
    for j in range(TB):
        last = pe.transpose(dst[:, j * P:(j + 1) * P], src[:, j, :], M.eye)
    return last


class Front:

    def __init__(self, S, pad=0, hT=None):
        self.norm = Norm(S, "front")
        self.pad = pad
        self.hT = hT if hT is not None else S.sb("hT", [P, pad + BL])
        self.bank = S.ps("front_bank", [P, BL])
        self.turned = S.sem("front_turned")
        self.ready = S.sem("front_ready")

    def stats(self, dve, M, own, i):
        self.norm.stats(dve, M, own, lambda j: M.X[:, i * TB + j, :])

    def apply(self, dve, M, own, i, after=None):
        if after is not None:
            dve.wait_ge(self.turned, after)
        self.norm.apply(dve, own, lambda j: M.X[:, i * TB + j, :], i)
        dve.sem_inc(self.norm.done, 1)

    def dve(self, dve, M, own, i):
        self.stats(dve, M, own, i)
        self.apply(dve, M, own, i)

    def pool(self, pool, M, i):
        self.norm.pool(pool, M, i)

    def pe(self, pe, M, i):
        pe.wait_ge(self.norm.done, i + 1)
        turn(pe, M, self.bank, self.norm.out).then_inc(self.turned, 1)

    def act(self, act, i, dst=None):
        act.wait_ge(self.turned, i + 1)
        dst = self.hT[:, self.pad:self.pad + BL] if dst is None else dst
        act.copy(dst, self.bank[:, :]).then_inc(self.ready, 1)


class Tail:

    def __init__(self, S, eps=EPS):
        self.norm = Norm(S, "tail", eps)
        self.y = S.sem("y_ready")

    def stats(self, dve, M, own, y, i):
        dve.wait_ge(self.y, i + 1)
        self.norm.stats(dve, M, own, y)

    def apply(self, dve, M, own, y, i):
        self.norm.apply(dve, own, y, i)
        own(dve.tensor_tensor(M.X[:, bass.ts(i, TB), :], M.X[:, bass.ts(i, TB), :], self.norm.out[:, :, :], ALU.add))
        own.wait()
        dve.sem_inc(self.norm.done, 1)

    def dve(self, dve, M, own, y, i):
        self.stats(dve, M, own, y, i)
        self.apply(dve, M, own, y, i)

    def pool(self, pool, M, i):
        self.norm.pool(pool, M, i)


def blocks(eng, body, last=NB):
    with eng.Fori(0, last - 1) as i:
        body(i, True)
    body(last - 1, False)


def norms(pool, M, front, tail, between=None):
    front.pool(pool, M, 0)

    def body(i, more):
        if more:
            front.pool(pool, M, i + 1)
        if between is not None:
            between(i)
        tail.pool(pool, M, i)
    blocks(pool, body)



def load(nc, M, x, w, rows, causal):
    ctx = M.ctx
    M.W = ctx.enter_context(nc.sbuf_tensor("weights", [P, NW], F32))
    M.X = ctx.enter_context(nc.sbuf_tensor("x", [P, NT, P], F32))
    M.rows = ctx.enter_context(nc.sbuf_tensor("rows", [1, len(ROWS) * P], F32))
    M.ones = ctx.enter_context(nc.sbuf_tensor("ones", [1, P], F32))
    M.eyeb = ctx.enter_context(nc.sbuf_tensor("eyeb", [P, P], BF16))
    M.mhalf = ctx.enter_context(nc.sbuf_tensor("mhalf", [P, NT], F32))
    M.causal = ctx.enter_context(nc.sbuf_tensor("causal", [P, P], BF16))
    M.spare = ctx.enter_context(nc.sbuf_tensor("spare", [P, 1], F32))
    M.s_first = ctx.enter_context(nc.semaphore("first_loads"))
    M.s_rest = ctx.enter_context(nc.semaphore("other_loads"))
    M.s_alone = ctx.enter_context(nc.semaphore("waits_passed"))
    s_const = ctx.enter_context(nc.semaphore("constants"))
    M.w = lambda name, a=0, n=None: M.W[:, AT[name][0] + a:AT[name][0] + (AT[name][1] if n is None else a + n)]
    M.row = lambda name: M.rows[0:1, ROWS.index(name) * P:(ROWS.index(name) + 1) * P]
    M.eye = M.w("eye")
    cuts = [0, AT["m_ln1w"][0], AT["c_in"][0], AT["t_q"][0], NW]
    N_FIRST = 16 * 3
    M.N_REST = 16 * (2 + len(cuts) - 2)
    xt = x.rearrange("(t p) f -> p t f", p=P)
    with nc.Block() as block:
        @block.sync
        def _(sp):
            sp.dma_start(M.X[:, 0:TB, :], xt[:, 0:TB, :]).then_inc(M.s_first, 16)
            sp.dma_start(M.W[:, 0:cuts[1]], w[:, 0:cuts[1]]).then_inc(M.s_first, 16)
            sp.dma_start(M.rows[:, :], rows).then_inc(M.s_first, 16)
            sp.dma_start(M.X[:, TB:NT, :], xt[:, TB:NT, :]).then_inc(M.s_rest, 16)
            sp.dma_start(M.causal[:, :], causal).then_inc(M.s_rest, 16)
            for a, b in zip(cuts[1:-1], cuts[2:]):
                sp.dma_start(M.W[:, a:b], w[:, a:b]).then_inc(M.s_rest, 16)
            sp.wait_ge(M.s_first, N_FIRST)

        @block.vector
        def _(dve):
            dve.memset(M.ones[:, :], 1.0)
            dve.memset(M.mhalf[:, :], -0.5).then_inc(s_const, 1)
            dve.wait_ge(M.s_first, N_FIRST)
            dve.tensor_copy(M.eyeb[:, :], M.eye).then_inc(s_const, 1)
            dve.wait_ge(s_const, 2)


def store(nc, M, out):
    s_out = M.ctx.enter_context(nc.semaphore("stored"))
    with nc.Block() as block:
        @block.sync
        def _(sp):
            sp.dma_start(out.rearrange("(t p) f -> p t f", p=P), M.X[:, :, :]).then_inc(s_out, 16)
            sp.wait_ge(s_out, 16)



def head_mix(nc, M):
    with ExitStack() as ctx:
        S = Scratch(nc, ctx, "l0")
        front, tail = Front(S), Tail(S)
        qkvP = [S.ps(f"qkvP{k}", [P, 3 * P]) for k in range(2)]
        oP = S.ps("oP", [P, BL])
        yP = S.ps("yP", [P, TB, P])
        qkv = S.sb("qkv", [P, 2, 3 * P])
        prod = S.sb("prod", [P, H * H * D])
        prod2 = S.sb("prod2", [P, H * H * D])
        sc = S.sb("sc", [P, 2, H * H])
        pr = S.sb("pr", [P, 2, H * H])
        mx = S.sb("mx", [P, H])
        den = S.sb("den", [P, 2, H])
        o = S.sb("o", [P, TB, P])
        oT = S.sb("oT", [P, BL])
        s_qkvP = S.sem("qkv_in_psum")
        s_qkv = S.sem("qkv_ready")
        s_sc = S.sem("scores_ready")
        s_pr = S.sem("exp_ready")
        s_pv = S.sem("weighted_values")
        s_o = S.sem("o_ready")
        s_oP = S.sem("o_turned")
        s_oT = S.sem("oT_ready")
        s_red = S.sem("sums_taken")
        own_dve = S.sem("own_dve")
        PER = 59
        with nc.Block() as block:
            @block.sync
            def _(sp):
                sp.wait_ge(M.s_rest, M.N_REST)

            @block.tensor
            def _(pe):
                def products(i, tiles):
                    for j in tiles:
                        if not (isinstance(i, int) and i * TB + j < 2):
                            pe.wait_ge(s_qkv, i * TB + j - 1)
                        pe.matmul(qkvP[j % 2][:, :], front.hT[:, j * P:(j + 1) * P], M.w("l0_qkv"),
                                  start=True, stop=True).then_inc(s_qkvP, 1)

                def begin(i):
                    front.pe(pe, M, i)
                    pe.wait_ge(front.ready, i + 1)
                    products(i, (0, 1))

                def body(i, more):
                    products(i, (2, 3))
                    if more:
                        begin(i + 1)
                    pe.wait_ge(s_o, i + 1)
                    turn(pe, M, oP, o).then_inc(s_oP, 1)
                    pe.wait_ge(s_oT, i + 1)
                    for j in range(TB):
                        pe.matmul(yP[:, j, :], oT[:, j * P:(j + 1) * P], M.w("l0_proj"), start=True, stop=False)
                        last = pe.matmul(yP[:, j, :], M.ones[0:1, :], M.row("l0_bproj"), start=False, stop=True)
                    last.then_inc(tail.y, 1)

                begin(0)
                blocks(pe, body)

            @block.scalar
            def _(act):
                def evacuate(i, j):
                    if not (isinstance(i, int) and i * TB + j < 2):
                        act.wait_ge(s_pv, i * TB + j - 1)
                    act.wait_ge(s_qkvP, i * TB + j + 1)
                    act.copy(qkv[:, j % 2, :], qkvP[j % 2][:, :]).then_inc(s_qkv, 1)

                def exp(i, j):
                    act.wait_ge(s_sc, i * TB + j + 1)
                    act.activation(pr[:, j % 2, :], sc[:, j % 2, :], ACT.Exp, scale=1.0 / 8.0).then_inc(s_pr, 1)

                def begin(i):
                    front.act(act, i)
                    evacuate(i, 0)
                    evacuate(i, 1)

                def body(i, more):
                    exp(i, 0)
                    evacuate(i, 2)
                    exp(i, 1)
                    evacuate(i, 3)
                    exp(i, 2)
                    exp(i, 3)
                    if more:
                        begin(i + 1)
                    act.wait_ge(s_oP, i + 1)
                    act.copy(oT[:, :], oP[:, :]).then_inc(s_oT, 1)

                begin(0)
                blocks(act, body)

            @block.gpsimd
            def _(pool):
                def body(i, first, more):
                    for j in range(TB):
                        if j == 1 and not first:
                            tail.pool(pool, M, i - 1)
                        if j == 3 and more:
                            front.pool(pool, M, i + 1)
                        pool.wait_ge(s_pr, i * TB + j + 1)
                        if j > 0 or not first:
                            pool.wait_ge(s_red, i * TB + j)
                        v = qkv[:, j % 2, :].rearrange("p (g c d) -> p c d g", c=3, d=D)[:, 2, :, :]
                        pool.tensor_tensor(
                            prod2[:, :].rearrange("p (h d g) -> p h d g", h=H, d=D),
                            pr[:, j % 2, :].rearrange("p (h a g) -> p h a g", h=H, a=1).broadcast_to([P, H, D, H]),
                            v.rearrange("p (a d) g -> p a d g", a=1).broadcast_to([P, H, D, H]),
                            ALU.mult).then_inc(s_pv, 1)

                front.pool(pool, M, 0)
                body(0, True, True)
                with pool.Fori(1, NB - 1) as i:
                    body(i, False, True)
                body(NB - 1, False, False)
                tail.pool(pool, M, NB - 1)

            @block.vector
            def _(dve):
                def scores(own, i, j):
                    dve.wait_ge(s_qkv, i * TB + j + 1)
                    t = qkv[:, j % 2, :].rearrange("p (g c d) -> p g c d", c=3, d=D)
                    s3 = sc[:, j % 2, :].rearrange("p (h g) -> p h g", h=H)
                    own(dve.tensor_tensor(
                        prod[:, :].rearrange("p (h g d) -> p h g d", h=H, g=H),
                        t[:, :, 0:1, :].broadcast_to([P, H, H, D]),
                        t[:, :, 1, :].rearrange("p (a g) d -> p a g d", a=1).broadcast_to([P, H, H, D]), ALU.mult))
                    own.wait()
                    own(dve.tensor_reduce(sc[:, j % 2, :], prod[:, :].rearrange("p (n d) -> p n d", d=D), AX.X, ALU.add))
                    own.wait()
                    own(dve.tensor_reduce(mx[:, :], s3, AX.X, ALU.max))
                    own.wait()
                    own(dve.tensor_tensor(s3, s3, mx[:, :].rearrange("p (h a) -> p h a", a=1).broadcast_to([P, H, H]), ALU.subtract))
                    own.wait()
                    dve.sem_inc(s_sc, 1)

                def values(own, i, j):
                    dve.wait_ge(s_pr, i * TB + j + 1)
                    own(dve.tensor_reduce(den[:, 0, :], pr[:, j % 2, :].rearrange("p (h g) -> p h g", h=H), AX.X, ALU.add))
                    own.wait()
                    own(dve.reciprocal(den[:, 1, :], den[:, 0, :]))
                    dve.wait_ge(s_pv, i * TB + j + 1)
                    own(dve.tensor_reduce(o[:, j, :], prod2[:, :].rearrange("p (n g) -> p n g", g=H), AX.X, ALU.add))
                    own.wait()
                    dve.sem_inc(s_red, 1)
                    o3 = o[:, j, :].rearrange("p (h d) -> p h d", h=H)
                    own(dve.tensor_tensor(o3, o3, den[:, 1, :].rearrange("p (h a) -> p h a", a=1).broadcast_to([P, H, D]), ALU.mult))
                    own.wait()

                y = lambda j: yP[:, j, :]

                def body(i, first, more, base):
                    own = Chain(dve, own_dve, base)
                    scores(own, i, 0)
                    if not first:
                        tail.stats(dve, M, own, y, i - 1)
                    scores(own, i, 1)
                    values(own, i, 0)
                    scores(own, i, 2)
                    if first:
                        dve.wait_ge(M.s_rest, M.N_REST)
                    if more:
                        front.stats(dve, M, own, i + 1)
                    values(own, i, 1)
                    scores(own, i, 3)
                    values(own, i, 2)
                    if more:
                        front.apply(dve, M, own, i + 1, after=i + 1)
                    if not first:
                        tail.apply(dve, M, own, y, i - 1)
                    values(own, i, 3)
                    dve.sem_inc(s_o, 1)
                    return own.n

                own = Chain(dve, own_dve)
                front.dve(dve, M, own, 0)
                n = own.n
                n += body(0, True, True, n)
                with dve.Fori(1, NB - 1) as i:
                    assert body(i, False, True, n + (i - 1) * PER) == PER
                n += (NB - 2) * PER
                n += body(NB - 1, False, False, n)
                tail.dve(dve, M, Chain(dve, own_dve, n), y, NB - 1)




GH = 4
NG = H // GH
SLOT = 64
TERMS = [(0, 0), (0, 1), (0, 2), (1, 0), (1, 1), (2, 0)]
NTERM = len(TERMS) * D
ROWSB = NTERM + 3
PARTS = 3


def causal_moe(nc, M):
    with ExitStack() as ctx:
        S = Scratch(nc, ctx, "l1")
        M.U = S.sb("u", [P, NT, P])
        with ExitStack() as actx:
            A = Scratch(nc, actx, "l1")
            M.V = A.sb("v", [P, NT, H, D])
            M.Y = A.sb("heads_out", [P, NT, H, D])
            with ExitStack() as bctx:
                B = Scratch(nc, bctx, "l1")
                M.Qs = B.sb("q_split", [P, NT, H, SLOT], BF16)
                M.Ks = B.sb("k_split", [P, NT, H, SLOT], BF16)
                rotary_qkv(nc, M)
                attention(nc, M)
            M.E = A.sb("expert_weights", [P, WV + EPROJ])
            project(nc, M)
            experts(nc, M)


def rotary_qkv(nc, M):
    with ExitStack() as ctx:
        S = Scratch(nc, ctx, "l1a")
        outer, inner = Norm(S, "outer"), Norm(S, "inner")
        turnP = S.ps("turnP", [P, BL])
        qkvP = [S.ps(f"qkvP{k}", [P, 3 * P]) for k in range(2)]
        hT = S.sb("hT", [P, 2 + BL])
        c = S.sb("conv", [P, 3, BL])
        qk = S.sb("qk", [P, 2, 2 * P])
        t1 = S.sb("times_cos", [P, 2 * P])
        t2 = S.sb("times_sin", [P, 2, 2 * P])
        rot = S.sb("turned_qk", [P, 3, 2 * P])
        part = S.sb("parts", [P, 2, PARTS, 2 * P], BF16)
        s_turned = S.sem("h_turned")
        s_hT = S.sem("hT_ready")
        s_c = S.sem("conv_ready")
        s_qkvP = S.sem("qkv_in_psum")
        s_qk = S.sem("qk_ready")
        s_sin = S.sem("sin_products")
        s_part = S.sem("parts_ready")
        s_put = S.sem("q_slots_written")
        s_putk = S.sem("k_slots_written")
        own_dve = S.sem("own_dve")
        own_pool = S.sem("own_pool")
        s_rot = S.sem("sin_used")
        s_hist = S.sem("history_kept")
        PER = 63
        with nc.Block() as block:
            @block.tensor
            def _(pe):
                def begin(i):
                    pe.wait_ge(inner.done, i + 1)
                    turn(pe, M, turnP, inner.out).then_inc(s_turned, 1)

                def body(i, first, more):
                    pe.wait_ge(s_c, i + 1)
                    for j in range(TB):
                        if j >= 2 or not first:
                            pe.wait_ge(s_qk, i * TB + j - 1)
                        pe.matmul(qkvP[j % 2][:, :], c[:, 2, j * P:(j + 1) * P], M.w("m_qkv"), start=True, stop=True).then_inc(s_qkvP, 1)
                    if more:
                        begin(i + 1)

                begin(0)
                body(0, True, True)
                with pe.Fori(1, NB - 1) as i:
                    body(i, False, True)
                body(NB - 1, False, False)

            @block.scalar
            def _(act):
                def begin(i):
                    act.wait_ge(s_hist, i + 1)
                    act.wait_ge(s_turned, i + 1)
                    act.activation(hT[:, 2:2 + BL], turnP[:, :], ACT.Identity, scale=M.w("m_ln1w"), bias=M.w("m_ln1b")).then_inc(s_hT, 1)

                def body(i, first, more):
                    def slots(j):
                        act.wait_ge(s_part, i * TB + j + 1)
                        p4 = part[:, j % 2, :, P:2 * P].rearrange("p n (h d) -> p h n d", h=H)
                        k4 = M.Ks[:, i * TB + j, :, 0:NTERM].rearrange("p h (n d) -> p h n d", d=D)
                        act.copy(k4[:, :, 0:3, :], p4)
                        act.copy(k4[:, :, 3:5, :], p4[:, :, 0:2, :])
                        act.copy(k4[:, :, 5:6, :], p4[:, :, 0:1, :]).then_inc(s_putk, 1)

                    for j in range(TB):
                        act.wait_ge(s_qkvP, i * TB + j + 1)
                        if j >= 2 or not first:
                            act.wait_ge(s_rot, i * TB + j - 1)
                        act.copy(M.V[:, i * TB + j, :, :], qkvP[j % 2][:, 2 * P:3 * P].rearrange("p (h d) -> p h d", h=H))
                        act.copy(qk[:, j % 2, :], qkvP[j % 2][:, 0:2 * P]).then_inc(s_qk, 1)
                        if j >= 1:
                            slots(j - 1)
                    if more:
                        begin(i + 1)
                    slots(TB - 1)

                begin(0)
                body(0, True, True)
                with act.Fori(1, NB - 1) as i:
                    body(i, False, True)
                body(NB - 1, False, False)

            @block.gpsimd
            def _(pool):
                def body(i, first, more):
                    def slots(j):
                        pool.wait_ge(s_part, i * TB + j + 1)
                        alone(pool, M)
                        p4 = part[:, j % 2, :, 0:P].rearrange("p n (h d) -> p h n d", h=H)
                        q4 = M.Qs[:, i * TB + j, :, 0:NTERM].rearrange("p h (n d) -> p h n d", d=D)
                        pool.tensor_copy(q4[:, :, 0:3, :], p4[:, :, 0:1, :].broadcast_to([P, H, 3, D]))
                        pool.tensor_copy(q4[:, :, 3:5, :], p4[:, :, 1:2, :].broadcast_to([P, H, 2, D]))
                        pool.tensor_copy(q4[:, :, 5:6, :], p4[:, :, 2:3, :]).then_inc(s_put, 1)

                    for j in range(TB):
                        pool.wait_ge(s_qk, i * TB + j + 1)
                        if j >= 2 or not first:
                            pool.wait_ge(s_rot, i * TB + j - 1)
                        x4 = qk[:, j % 2, :].rearrange("p (h a d) -> p h a d", a=2, d=D // 2)
                        t4 = t2[:, j % 2, :].rearrange("p (h a d) -> p h a d", a=2, d=D // 2)
                        sin = M.w("sin").rearrange("p (t d) -> p t d", t=NT)[:, bass.ds(i * TB + j, 1), :].broadcast_to([P, 2 * H, D // 2])
                        pool.tensor_tensor(t4[:, :, 0, :], x4[:, :, 1, :], sin, ALU.mult)
                        pool.tensor_tensor(t4[:, :, 1, :], x4[:, :, 0, :], sin, ALU.mult).then_inc(s_sin, 1)
                        if j == 0 and more:
                            outer.pool(pool, M, i + 1)
                        if j == 2 and more:
                            inner.pool(pool, M, i + 1)
                        if j >= 1:
                            slots(j - 1)
                    slots(TB - 1)

                outer.pool(pool, M, 0)
                inner.pool(pool, M, 0)
                pool.memset(M.Qs[:, :, :, NTERM:SLOT], 0.0).then_inc(own_pool, 1)
                pool.memset(M.Ks[:, :, :, ROWSB:SLOT], 0.0).then_inc(own_pool, 1)
                pool.memset(M.Ks[:, :, :, NTERM:ROWSB], 1.0).then_inc(own_pool, 1)
                pool.wait_ge(own_pool, 3)
                body(0, True, True)
                with pool.Fori(1, NB - 1) as i:
                    body(i, False, True)
                body(NB - 1, False, False)

            @block.vector
            def _(dve):
                x_tile = lambda i: lambda j: M.X[:, i * TB + j, :]
                outer_tile = lambda j: outer.out[:, j, :]

                def between(own, i):
                    outer.apply(dve, own, x_tile(i), i)
                    own(dve.tensor_copy(M.U[:, bass.ts(i, TB), :] if not isinstance(i, int) else M.U[:, i * TB:i * TB + TB, :], outer.out[:, :, :]))
                    inner.stats(dve, M, own, outer_tile)

                def finish(own, i, after=None):
                    if after is not None:
                        dve.wait_ge(s_turned, after)
                    inner.apply(dve, own, outer_tile, i)
                    dve.sem_inc(inner.done, 1)

                def tile(own, i, j, first):
                    dve.wait_ge(s_qk, i * TB + j + 1)
                    x4 = qk[:, j % 2, :].rearrange("p (h a d) -> p h a d", a=2, d=D // 2)
                    t14 = t1[:, :].rearrange("p (h a d) -> p h a d", a=2, d=D // 2)
                    t24 = t2[:, j % 2, :].rearrange("p (h a d) -> p h a d", a=2, d=D // 2)
                    r4 = rot[:, 0, :].rearrange("p (h a d) -> p h a d", a=2, d=D // 2)
                    cos = M.w("cos").rearrange("p (t d) -> p t d", t=NT)[:, bass.ds(i * TB + j, 1), :].broadcast_to([P, 2 * H, D // 2])
                    own(dve.tensor_tensor(t14[:, :, 0, :], x4[:, :, 0, :], cos, ALU.mult))
                    own(dve.tensor_tensor(t14[:, :, 1, :], x4[:, :, 1, :], cos, ALU.mult))
                    own.wait()
                    dve.wait_ge(s_sin, i * TB + j + 1)
                    own(dve.tensor_tensor(r4[:, :, 0, :], t14[:, :, 0, :], t24[:, :, 0, :], ALU.subtract))
                    own(dve.tensor_tensor(r4[:, :, 1, :], t14[:, :, 1, :], t24[:, :, 1, :], ALU.add))
                    own.wait()
                    dve.sem_inc(s_rot, 1)
                    pj = part[:, j % 2, :, :]
                    if j >= 2 or not first:
                        dve.wait_ge(s_put, i * TB + j - 1)
                        dve.wait_ge(s_putk, i * TB + j - 1)
                    own(dve.tensor_copy(pj[:, 0, :], rot[:, 0, :]))
                    own.wait()
                    own(dve.tensor_tensor(rot[:, 1, :], rot[:, 0, :], pj[:, 0, :], ALU.subtract))
                    own.wait()
                    own(dve.tensor_copy(pj[:, 1, :], rot[:, 1, :]))
                    own.wait()
                    own(dve.tensor_tensor(pj[:, 2, :], rot[:, 1, :], pj[:, 1, :], ALU.subtract))
                    own.wait()
                    dve.sem_inc(s_part, 1)

                def body(i, first, more, base):
                    own = Chain(dve, own_dve, base)
                    dve.wait_ge(s_hT, i + 1)
                    w = M.w("m_conv")
                    own(dve.tensor_scalar(c[:, 0, :], hT[:, 0:BL], w[:, 0:1], None, ALU.mult))
                    own.wait()
                    own(dve.scalar_tensor_tensor(c[:, 1, :], hT[:, 1:1 + BL], w[:, 1:2], c[:, 0, :], ALU.mult, ALU.add))
                    own.wait()
                    own(dve.scalar_tensor_tensor(c[:, 2, :], hT[:, 2:2 + BL], w[:, 2:3], c[:, 1, :], ALU.mult, ALU.add))
                    own.wait()
                    dve.sem_inc(s_c, 1)
                    own(dve.tensor_copy(hT[:, 0:2], hT[:, BL:BL + 2]))
                    own.wait()
                    dve.sem_inc(s_hist, 1)
                    if more:
                        outer.stats(dve, M, own, x_tile(i + 1))
                    tile(own, i, 0, first)
                    tile(own, i, 1, first)
                    if more:
                        between(own, i + 1)
                    tile(own, i, 2, first)
                    if more:
                        finish(own, i + 1, after=i + 1)
                    tile(own, i, 3, first)
                    return own.n

                own = Chain(dve, own_dve)
                own(dve.memset(hT[:, 0:2], 0.0))
                own.wait()
                dve.sem_inc(s_hist, 1)
                outer.stats(dve, M, own, x_tile(0))
                between(own, 0)
                finish(own, 0)
                n = own.n
                n += body(0, True, True, n)
                with dve.Fori(1, NB - 1) as i:
                    assert body(i, False, True, n + (i - 1) * PER) == PER
                n += (NB - 2) * PER
                n += body(NB - 1, False, False, n)


def attention(nc, M):
    T_, Q_, U_, E_, F_, R_, N_ = "turn", "turn_q", "max", "exp", "weigh", "rows", "norm"
    firsts = [(T_, 0)]
    for t in range(NT):
        if t + 1 < NT:
            firsts.append((T_, t + 1))
        for p in range(2):
            for c in range(t // TB + 1):
                for e in range(2):
                    firsts.append((U_, t, 2 * p + e, c))
    seconds = []
    for qc in range(NB):
        seconds += [(Q_, 2 * qc), (Q_, 2 * qc + 1)]
        for kt in range(TB * qc + TB):
            seconds += [(E_, qc, kt, 0), (E_, qc, kt, 1)]
            if kt > 0:
                seconds.append((F_, qc, kt - 1))
            elif qc > 0:
                seconds.append((N_, qc - 1))
        seconds += [(F_, qc, TB * qc + TB - 1), (R_, qc)]
    seconds.append((N_, NB - 1))
    width = lambda t, c: min(BL, (t + 1) * P - c * BL)

    C_U, C_E, C_T, C_Q = 130, 0, 400, 400

    def cost(it):
        if it[0] == U_:
            return C_U + width(it[1], it[3])
        if it[0] in (E_, F_):
            return C_E + (2 if it[0] == E_ else 4) * (BL - P * max(0, it[2] - TB * it[1]))
        return {T_: C_T, Q_: C_Q, R_: 0, N_: C_Q}[it[0]]

    def merged(a, b):
        ta, tb = sum(map(cost, a)) or 1, sum(map(cost, b)) or 1
        out, x, y, ca, cb = [], 0, 0, 0.0, 0.0
        while x < len(a) or y < len(b):
            if y >= len(b) or (x < len(a) and ca / ta <= cb / tb):
                out.append(a[x])
                ca += cost(a[x])
                x += 1
            else:
                out.append(b[y])
                cb += cost(b[y])
                y += 1
        return out

    NU = sum(1 for it in firsts if it[0] == U_)
    NEX = sum(1 for it in seconds if it[0] == F_)
    TURNS_A, TURNS_B = NT, NT // 2 + NB
    RING = 3

    def ring(items):
        users = [it for it in items if it[0] in (T_, Q_, U_, N_)]
        return {it: (k % RING, users[k - RING] if k >= RING else None) for k, it in enumerate(users)}

    with ExitStack() as ctx:
        S = Scratch(nc, ctx, "l1b")
        bank = [S.ps(f"ring{k}", [P, BL]) for k in range(RING)]
        stP = [S.ps(f"stP{p}", [P, 2, BL]) for p in range(2)]
        oP = S.ps("oP", [P, BL])
        KTn = S.sb("kT_next", [P, 2, T], BF16)
        KTc = S.sb("kT", [P, 2, T], BF16)
        QTn = S.sb("qT_tile", [P, 2, 2, 2, P], BF16)
        QTf = S.sb("qT", [P, 2, 2, T], BF16)
        mx = S.sb("max_parts", [P, NB, NT, GH])
        nm = S.sb("neg_max", [P, 3, NT, GH])
        PT = S.sb("probs", [P, 2, GH, BL])
        Vg = S.sb("v_ones", [P, NT, GH, 32])
        OT = S.sb("o_rows", [P, BL])
        OK = S.sb("o_tokens", [P, TB, GH, 32])
        rec = S.sb("reciprocal", [P, TB, GH, 1])
        s_tfull = S.sem("turned")
        s_tfree = S.sem("turned_out")
        s_sc = S.sem("scores_in_psum")
        s_max = S.sem("max_taken")
        s_neg = S.sem("neg_max_in_q")
        s_zero = S.sem("q_zeroed")
        s_kc = S.sem("kT_moved")
        s_vg = S.sem("values_ready")
        s_st = S.sem("scoresT_in_psum")
        s_exp = S.sem("exp_ready")
        s_pv = S.sem("pv_done")
        s_oT = S.sem("o_rows_ready")
        s_y = S.sem("o_normalised")
        own_dve = S.sem("own_dve")
        own_pool = S.sem("own_pool")

        def diag(qc, kt):
            return max(0, kt - TB * qc)

        def tensor_step(pe, s, g, base):
            items = merged(firsts if s is not None else [], seconds if g is not None else [])
            banks, count = ring(items), {}
            k, n, u, e, f = 0, 0, 0, 0, 0

            def take(it):
                b, before = banks[it]
                if before is not None:
                    pe.wait_ge(s_max if before[0] == U_ else s_tfree, count[before])
                return bank[b]

            if g is not None:
                pe.wait_ge(s_tfree, base)
                pe.wait_ge(s_max, (g + 1) * NU)
            for it in items:
                if it[0] == T_:
                    t = it[1]
                    tP = take(it)
                    for w in range(4):
                        src = (M.Ks if w < 2 else M.Qs)[:, t, bass.ds(s * GH + 2 * (w % 2), 2), :]
                        last = pe.matmul(tP[:, w * P:(w + 1) * P], src.rearrange("p h r -> p (h r)"), M.eyeb[:, :], start=True, stop=True)
                    last.then_inc(s_tfull, 1)
                    k += 1
                    count[it] = base + k
                elif it[0] == Q_:
                    tP = take(it)
                    if it[1] == 0:
                        pe.wait_ge(s_neg, g + 1)
                    for w in range(4):
                        src = M.Qs[:, 2 * it[1] + w % 2, bass.ds(g * GH + 2 * (w // 2), 2), :]
                        last = pe.matmul(tP[:, w * P:(w + 1) * P], src.rearrange("p h r -> p (h r)"), M.eyeb[:, :], start=True, stop=True)
                    last.then_inc(s_tfull, 1)
                    k += 1
                    count[it] = base + k
                elif it[0] == U_:
                    _, t, h, c = it
                    if h == 0 and c == 0:
                        pe.wait_ge(s_tfree, count[(T_, t)])
                    scP = take(it)
                    w = width(t, c)
                    last_c = c == t // TB
                    last = pe.matmul(scP[:, 0:w], QTn[:, h // 2, h % 2, t % 2, :],
                                     KTn[:, h // 2, c * BL:c * BL + w], start=True, stop=not last_c)
                    if last_c:
                        last = pe.matmul(scP[:, w - P:w], M.eyeb[:, :], M.causal[:, :], start=False, stop=True)
                    last.then_inc(s_sc, 1)
                    u += 1
                    count[it] = s * NU + u
                elif it[0] == E_:
                    _, qc, kt, p = it
                    r = diag(qc, kt)
                    if e == 0 and p == 0:
                        pe.wait_ge(s_kc, g + 1)
                        pe.wait_ge(s_vg, g + 1)
                    if kt == 0 and p == 0:
                        pe.wait_ge(s_tfree, count[(Q_, 2 * qc + 1)])
                    if e >= 1:
                        pe.wait_ge(s_exp, (g * NEX + e) * 2 + p - 1)
                    for h in range(2):
                        last = pe.matmul(stP[p][:, h, r * P:BL], KTc[:, p, kt * P:(kt + 1) * P],
                                         QTf[:, p, h, qc * BL + r * P:(qc + 1) * BL], start=True, stop=kt < TB * qc)
                    if kt >= TB * qc:
                        for h in range(2):
                            last = pe.matmul(stP[p][:, h, r * P:(r + 1) * P], M.causal[:, :], M.eyeb[:, :], start=False, stop=True)
                    last.then_inc(s_st, 1)
                    e += p
                elif it[0] == F_:
                    _, qc, kt = it
                    r = diag(qc, kt)
                    if kt == 0 and qc > 0:
                        pe.wait_ge(s_oT, g * NB + qc)
                    pe.wait_ge(s_exp, (g * NEX + f) * 2 + 2)
                    for j in range(GH):
                        last = pe.matmul(oP[32 * j:32 * j + 32, r * P:BL], Vg[:, kt, j, :], PT[:, f % 2, j, r * P:BL],
                                         start=(kt == 0), stop=(kt == TB * qc + TB - 1), skip_group_check=True)
                    last.then_inc(s_pv, 1)
                    f += 1
                elif it[0] == N_:
                    tP = take(it)
                    pe.wait_ge(s_oT, g * NB + n + 1)
                    for j in range(TB):
                        last = pe.transpose(tP[:, j * P:(j + 1) * P], OT[:, j * P:(j + 1) * P], M.eye)
                    last.then_inc(s_tfull, 1)
                    k += 1
                    count[it] = base + k
                    n += 1
            assert k == (TURNS_A if s is not None else 0) + (TURNS_B if g is not None else 0)

        def scalar_step(act, s, g, base):
            items = merged(firsts if s is not None else [], seconds if g is not None else [])
            banks = ring(items)
            k, n, e = 0, 0, 0
            for it in items:
                if it[0] == T_:
                    t = it[1]
                    if t == 0 and g is not None:
                        act.wait_ge(s_kc, s)
                    act.wait_ge(s_tfull, base + k + 1)
                    tP = bank[banks[it][0]]
                    act.copy(KTn[:, :, t * P:(t + 1) * P], tP[:, 0:2 * P].rearrange("p (a q) -> p a q", a=2))
                    for h in range(2):
                        half = slice(SLOT * h, SLOT * h + SLOT)
                        last = act.copy(QTn[half, :, h, t % 2, :], tP[half, 2 * P:4 * P].rearrange("p (a q) -> p a q", a=2))
                    last.then_inc(s_tfree, 1)
                    k += 1
                elif it[0] == Q_:
                    act.wait_ge(s_tfull, base + k + 1)
                    tP = bank[banks[it][0]]
                    for h in range(2):
                        half = slice(SLOT * h, SLOT * h + SLOT)
                        last = act.copy(QTf[half, :, h, 2 * it[1] * P:(2 * it[1] + 2) * P], tP[half, :].rearrange("p (a q) -> p a q", a=2))
                    last.then_inc(s_tfree, 1)
                    k += 1
                elif it[0] == E_:
                    _, qc, kt, p = it
                    r = diag(qc, kt)
                    if e >= 2:
                        act.wait_ge(s_pv, g * NEX + e - 1)
                    act.wait_ge(s_st, (g * NEX + e) * 2 + p + 1)
                    act.activation(PT[:, e % 2, 2 * p:2 * p + 2, r * P:BL], stP[p][:, :, r * P:BL], ACT.Exp,
                                   scale=float(1.0 / np.sqrt(np.float32(D)))).then_inc(s_exp, 1)
                    e += p
                elif it[0] == R_:
                    act.wait_ge(s_pv, g * NEX + e)
                    act.copy(OT[:, :], oP[:, :]).then_inc(s_oT, 1)
                elif it[0] == N_:
                    act.wait_ge(s_y, g * NB + n + 1)
                    act.wait_ge(s_tfull, base + k + 1)
                    tP = bank[banks[it][0]]
                    act.copy(OK[:, :, :, :], tP[:, :].rearrange("p (t h r) -> p t h r", t=TB, h=GH)).then_inc(s_tfree, 1)
                    k += 1
                    n += 1

        OWN = 6
        base_of = lambda s: TURNS_A + (s - 1) * (TURNS_A + TURNS_B)

        def vector_step(dve, s, g, base, ownbase):
            items = merged(firsts if s is not None else [], seconds if g is not None else [])
            banks = ring(items)
            k, n, u = 0, 0, 0
            own = Chain(dve, own_dve, ownbase)
            late = []

            def normalise(qc, turns, _):
                dve.wait_ge(s_tfree, turns)
                own(dve.reciprocal(rec[:, :, :, :], OK[:, :, :, D:D + 1]))
                own.wait()
                dve.tensor_tensor(M.Y[:, TB * qc:TB * qc + TB, bass.ds(g * GH, GH), :], OK[:, :, :, 0:D],
                                  rec[:, :, :, :].broadcast_to([P, TB, GH, D]), ALU.mult).then_inc(s_y, 1)
            for it in items:
                if it[0] in (T_, Q_):
                    k += 1
                elif it[0] == U_:
                    _, t, h, c = it
                    dve.wait_ge(s_sc, s * NU + u + 1)
                    dve.tensor_reduce(mx[:, c, t, h:h + 1], bank[banks[it][0]][:, 0:width(t, c)], AX.X, ALU.max).then_inc(s_max, 1)
                    u += 1
                    if late and u >= late[0][2] + 4:
                        normalise(*late.pop(0))
                elif it[0] == N_:
                    k += 1
                    late.append((it[1], base + k, u))
                    n += 1
                if s is None and late:
                    normalise(*late.pop(0))
            if s is not None:
                if g is not None:
                    dve.wait_ge(s_pv, s * NEX)
                dve.tensor_copy(KTc[:, :, :], KTn[:, :, :]).then_inc(s_kc, 1)
                dve.wait_ge(s_max, s * NU + NU)
                slot = lambda m: M.Qs[:, :, bass.ds(s * GH, GH), NTERM + m]
                own(dve.tensor_reduce(nm[:, 0, :, :], mx[:, :, :, :].rearrange("p c t h -> p t h c"), AX.X, ALU.max, negate=True))
                own.wait()
                own(dve.tensor_copy(slot(0), nm[:, 0, :, :]))
                own.wait()
                own(dve.tensor_tensor(nm[:, 1, :, :], nm[:, 0, :, :], slot(0), ALU.subtract))
                own.wait()
                own(dve.tensor_copy(slot(1), nm[:, 1, :, :]))
                own.wait()
                own(dve.tensor_tensor(nm[:, 2, :, :], nm[:, 1, :, :], slot(1), ALU.subtract))
                own.wait()
                own(dve.tensor_copy(slot(2), nm[:, 2, :, :]))
                own.wait()
                dve.sem_inc(s_neg, 1)
            for x in late:
                normalise(*x)
            return own.n

        def pool_step(pool, s, g):
            if s is not None:
                if g is not None:
                    pool.wait_ge(s_pv, s * NEX)
                    alone(pool, M)
                pool.tensor_copy(Vg[:, :, :, 0:D], M.V[:, :, bass.ds(s * GH, GH), :]).then_inc(s_vg, 1)

        with nc.Block() as block:
            @block.tensor
            def _(pe):
                tensor_step(pe, 0, None, 0)
                with pe.Fori(1, NG) as s:
                    tensor_step(pe, s, s - 1, base_of(s))
                tensor_step(pe, None, NG - 1, base_of(NG))

            @block.scalar
            def _(act):
                act.wait_ge(s_zero, 1)
                scalar_step(act, 0, None, 0)
                act.wait_ge(s_zero, 2)
                with act.Fori(1, NG) as s:
                    scalar_step(act, s, s - 1, base_of(s))
                scalar_step(act, None, NG - 1, base_of(NG))

            @block.vector
            def _(dve):
                dve.memset(mx[:, :, :, :], -3.0e38).then_inc(own_dve, 1)
                dve.sem_inc(s_y, 1)
                dve.wait_ge(own_dve, 1)
                n = 1 + vector_step(dve, 0, None, 0, 1)
                PER = OWN + NB
                with dve.Fori(1, NG) as s:
                    assert vector_step(dve, s, s - 1, base_of(s), n + (s - 1) * PER) == PER
                vector_step(dve, None, NG - 1, base_of(NG), n + (NG - 1) * PER)

            @block.gpsimd
            def _(pool):
                pool.memset(QTn[:, :, :, :, :], 0.0).then_inc(s_zero, 1)
                pool.memset(Vg[:, :, :, :], 0.0).then_inc(own_pool, 1)
                pool.wait_ge(own_pool, 1)
                pool.memset(Vg[:, :, :, D:D + 1], 1.0).then_inc(own_pool, 1)
                pool.wait_ge(own_pool, 2)
                pool.memset(QTf[:, :, :, :], 0.0).then_inc(s_zero, 1)
                pool_step(pool, 0, None)
                with pool.Fori(1, NG) as s:
                    pool_step(pool, s, s - 1)


def project(nc, M):
    with ExitStack() as ctx:
        S = Scratch(nc, ctx, "l1c")
        tP = [S.ps(f"tP{k}", [P, BL]) for k in range(2)]
        yP = [S.ps(f"yP{k}", [P, TB, P]) for k in range(2)]
        hT = S.sb("headsT", [P, BL])
        hS = S.sb("heads", [P, TB, P])
        s_h = S.sem("heads_copied")
        s_t = S.sem("heads_turned")
        s_hT = S.sem("headsT_ready")
        s_y = S.sem("product_in_psum")
        s_u = S.sem("u_updated")
        s_e = S.sem("expert_weights_loaded")
        with nc.Block() as block:
            @block.sync
            def _(sp):
                sp.dma_start(M.E[:, 0:WV], M.experts_w[:, 0:WV]).then_inc(s_e, 16)
                sp.dma_start(M.E[:, WV:WV + EPROJ], M.experts_w[:, WV:WV + EPROJ]).then_inc(s_e, 16)
                sp.wait_ge(s_e, 32)

            @block.gpsimd
            def _(pool):
                with pool.Fori(0, NB) as i:
                    pool.tensor_copy(hS[:, :, :], M.Y[:, bass.ts(i, TB), :, :].rearrange("p t h d -> p t (h d)")).then_inc(s_h, 1)
                    pool.wait_ge(s_t, i + 1)

            @block.tensor
            def _(pe):
                with pe.Fori(0, NB) as i:
                    pe.wait_ge(s_h, i + 1)
                    turn(pe, M, tP[0], hS).then_inc(s_t, 1)
                    pe.wait_ge(s_hT, i + 1)
                    for j in range(TB):
                        last = pe.matmul(yP[0][:, j, :], hT[:, j * P:(j + 1) * P], M.w("m_proj"), start=True, stop=True)
                    last.then_inc(s_y, 1)
                    pe.wait_ge(s_u, i + 1)

            @block.scalar
            def _(act):
                with act.Fori(0, NB) as i:
                    act.wait_ge(s_t, i + 1)
                    act.copy(hT[:, :], tP[0][:, :]).then_inc(s_hT, 1)

            @block.vector
            def _(dve):
                with dve.Fori(0, NB) as i:
                    dve.wait_ge(s_y, i + 1)
                    u = M.U[:, bass.ts(i, TB), :]
                    dve.tensor_tensor(u, u, yP[0][:, :, :], ALU.add).then_inc(s_u, 1)


def experts(nc, M):
    with ExitStack() as ctx:
        S = Scratch(nc, ctx, "l1d")
        inner, tail = Norm(S, "inner"), Tail(S)
        turnP = S.ps("turnP", [P, BL])
        gP = [S.ps(f"gP{k}", [P, BL]) for k in range(2)]
        vP = [S.ps(f"vP{k}", [P, BL]) for k in range(2)]
        yP = [S.ps(f"yP{k}", [P, TB, P]) for k in range(2)]
        hT = S.sb("hT", [P, BL])
        lg = S.sb("logits", [P, TB, NE])
        best = S.sb("best", [P, TB, 1])
        hit = S.sb("hit", [P, TB, NE])
        miss = S.sb("miss", [P, TB, NE])
        left = S.sb("left", [P, 2, TB])
        pick = S.sb("pick", [P, TB, NE])
        sg = S.sb("silu", [P, 2, BL])
        a = S.sb("act", [P, 2, FC, BL])
        s_turned = S.sem("h_turned")
        s_hT = S.sem("hT_ready")
        s_lg = S.sem("logits_in_psum")
        s_lgo = S.sem("logits_out")
        s_gP = S.sem("gate_in_psum")
        s_sg = S.sem("silu_ready")
        s_a = S.sem("act_ready")
        s_y = S.sem("expert_in_psum")
        s_acc = S.sem("expert_added")
        own_dve = S.sem("own_dve")
        N_FRONT = 13
        N_TAIL = 14
        PER = 26 + N_FRONT + N_TAIL
        ROUTE = 3 + NE
        assert ROUTE < 2 * FC
        wv = lambda n: M.E[:, n:n + P]
        u_tile = lambda i: lambda j: M.U[:, i * TB + j, :]
        with nc.Block() as block:
            @block.tensor
            def _(pe):
                def begin(i):
                    pe.wait_ge(inner.done, i + 1)
                    turn(pe, M, turnP, inner.out).then_inc(s_turned, 1)

                def logits(i):
                    pe.wait_ge(s_hT, i + 1)
                    for j in range(TB):
                        last = pe.matmul(turnP[:, j * NE:(j + 1) * NE], hT[:, j * P:(j + 1) * P], M.w("m_router"), start=True, stop=True)
                    last.then_inc(s_lg, 1)

                def body(i, first, more):
                    def down(e):
                        pe.wait_ge(s_a, (i * NE + e) * FC + FC)
                        if e >= 2 or not first:
                            pe.wait_ge(s_acc, i * NE + e - 1)
                        for j in range(TB):
                            for c in range(FC):
                                last = pe.matmul(yP[e % 2][:, j, :], a[:, e % 2, c, j * P:(j + 1) * P],
                                                 M.E[:, WV + (e * FC + c) * P:WV + (e * FC + c + 1) * P], start=(c == 0), stop=(c == FC - 1))
                        last.then_inc(s_y, 1)

                    for e in range(NE):
                        for c in range(FC):
                            n = e * FC + c
                            if n >= 2 or not first:
                                pe.wait_ge(s_a, i * NE * FC + n - 1)
                            pe.matmul(gP[n % 2][:, :], wv(e * 2 * FF + c * P), hT[:, :], start=True, stop=True)
                            pe.matmul(vP[n % 2][:, :], wv(e * 2 * FF + FF + c * P), hT[:, :], start=True, stop=True).then_inc(s_gP, 1)
                        if e >= 1:
                            down(e - 1)
                        if e == NE - 2:
                            pe.wait_ge(s_lgo, i + 1)
                    if more:
                        begin(i + 1)
                    down(NE - 1)
                    if more:
                        logits(i + 1)

                begin(0)
                logits(0)
                body(0, True, True)
                with pe.Fori(1, NB - 1) as i:
                    body(i, False, True)
                body(NB - 1, False, False)

            @block.scalar
            def _(act):
                def begin(i):
                    act.wait_ge(s_turned, i + 1)
                    act.activation(hT[:, :], turnP[:, :], ACT.Identity, scale=M.w("m_ln2w"), bias=M.w("m_ln2b")).then_inc(s_hT, 1)

                def body(i, more):
                    for n in range(NE * FC):
                        act.wait_ge(s_gP, i * NE * FC + n + 1)
                        if n >= 2:
                            act.wait_ge(s_a, i * NE * FC + n - 1)
                        act.activation(sg[:, n % 2, :], gP[n % 2][:, :], ACT.Silu).then_inc(s_sg, 1)
                    if more:
                        begin(i + 1)
                        act.wait_ge(s_a, i * NE * FC + NE * FC)

                begin(0)
                blocks(act, body)

            @block.gpsimd
            def _(pool):
                inner.pool(pool, M, 0)
                inner.pool(pool, M, 1)
                with pool.Fori(1, NB - 1) as i:
                    tail.pool(pool, M, i - 1)
                    inner.pool(pool, M, i + 1)
                tail.pool(pool, M, NB - 2)
                tail.pool(pool, M, NB - 1)

            @block.vector
            def _(dve):
                def add(own, i, e, tiles):
                    own.wait()
                    dve.wait_ge(s_y, i * NE + e + 1)
                    for j in tiles:
                        u = M.U[:, i * TB + j, :]
                        own(dve.scalar_tensor_tensor(u, yP[e % 2][:, j, :], pick[:, j, e:e + 1], u, ALU.mult, ALU.add))
                    if TB - 1 in tiles:
                        own.wait()
                        dve.sem_inc(s_acc, 1)

                def route(own, i, step):
                    own.wait()
                    if step == 0:
                        dve.wait_ge(s_lg, i + 1)
                        own(dve.tensor_copy(lg[:, :, :], turnP[:, 0:TB * NE].rearrange("p (t e) -> p t e", e=NE)))
                    elif step == 1:
                        dve.sem_inc(s_lgo, 1)
                        own(dve.tensor_reduce(best[:, :, 0], lg[:, :, :], AX.X, ALU.max))
                    elif step == 2:
                        own(dve.tensor_tensor(hit[:, :, :], lg[:, :, :], best[:, :, :].broadcast_to([P, TB, NE]), ALU.is_equal))
                    elif step == 3:
                        own(dve.tensor_copy(pick[:, :, 0], hit[:, :, 0]))
                        own(dve.tensor_scalar(miss[:, :, :], hit[:, :, :], -1.0, 1.0, ALU.mult, ALU.add))
                    else:
                        e = step - 3
                        former = miss[:, :, 0] if e == 1 else left[:, (e - 1) % 2, :]
                        own(dve.tensor_tensor(pick[:, :, e], hit[:, :, e], former, ALU.mult))
                        if e + 1 < NE:
                            own(dve.tensor_tensor(left[:, e % 2, :], miss[:, :, e], former, ALU.mult))

                def body(i, first, more, base):
                    own = Chain(dve, own_dve, base)
                    for e in range(NE):
                        for c in range(FC):
                            n = e * FC + c
                            if e == 1 and c == 2 and not first:
                                tail.stats(dve, M, own, u_tile(i - 1), i - 1)
                            if e == 2 and c == 0 and not first:
                                tail.apply(dve, M, own, u_tile(i - 1), i - 1)
                            if e == 2 and c == 2 and more:
                                inner.stats(dve, M, own, u_tile(i + 1))
                            if e == 3 and c == 0 and more:
                                dve.wait_ge(s_turned, i + 1)
                                inner.apply(dve, own, u_tile(i + 1), i + 1)
                                dve.sem_inc(inner.done, 1)
                            dve.wait_ge(s_sg, i * NE * FC + n + 1)
                            if e >= 2 and c == 0:
                                dve.wait_ge(s_y, i * NE + e - 1)
                            dve.tensor_tensor(a[:, e % 2, c, :], sg[:, n % 2, :], vP[n % 2][:, :], ALU.mult).then_inc(s_a, 1)
                            if 1 <= n < 1 + ROUTE:
                                route(own, i, n - 1)
                            if e >= 2 and c < 2:
                                add(own, i, e - 2, (2 * c, 2 * c + 1))
                    add(own, i, NE - 2, range(TB))
                    add(own, i, NE - 1, range(TB))
                    dve.sem_inc(tail.y, 1)
                    return own.n

                own = Chain(dve, own_dve)
                inner.dve(dve, M, own, u_tile(0), 0)
                dve.sem_inc(inner.done, 1)
                n = own.n
                n += body(0, True, True, n)
                with dve.Fori(1, NB - 1) as i:
                    assert body(i, False, True, n + (i - 1) * PER) == PER
                n += (NB - 2) * PER
                n += body(NB - 1, False, False, n)
                tail.dve(dve, M, Chain(dve, own_dve, n), u_tile(NB - 1), NB - 1)



def long_conv(nc, M):
    G = 8
    PADW = CK - 4
    with ExitStack() as ctx:
        S = Scratch(nc, ctx, "l2")
        front, tail = Front(S, pad=3), Tail(S)
        zP = [S.ps(f"zP{k}", [P, BL]) for k in range(2)]
        cP = [S.ps(f"cP{k}", [P, BL]) for k in range(2)]
        yP = S.ps("yP", [P, TB, P])
        taps = S.sb("taps", [P, 2 * 4 * 8, 32])
        z = S.sb("z", [P, G, PADW + BL])
        hb = S.sb("half_bias", [P, 2])
        th = S.sb("tanh", [P, 2, BL])
        sg = S.sb("sigmoid", [P, 2, BL])
        ga = S.sb("gated", [P, 2, BL])
        s_zP = S.sem("z_in_psum")
        s_z = S.sem("z_ready")
        edge = S.sb("edge", [P, 1, 3])
        s_edge = S.sem("edge_cleared")
        s_keep = S.sem("history_kept")
        s_cP = S.sem("conv_in_psum")
        s_th = S.sem("tanh_ready")
        s_ga = S.sem("gated_ready")
        s_set = S.sem("set_up")
        s_hist = S.sem("hT_history")
        s_pool = S.sem("own_pool")
        own_dve = S.sem("own_dve")
        FRONT = 13
        PER = 29
        with nc.Block() as block:
            @block.tensor
            def _(pe):
                pe.wait_ge(s_set, 5)
                front.pe(pe, M, 0)

                def inputs(i, groups):
                    pe.wait_ge(front.ready, i + 1)
                    for n in groups:
                        if n >= 2:
                            pe.wait_ge(s_z, i * G + n - 1)
                        for a in range(4):
                            last = pe.matmul(zP[n % 2][32 * a:32 * a + 32, :], M.w("c_in", 32 * n, 32),
                                             front.hT[:, 3 - a:3 - a + BL], start=True, stop=True)
                        last.then_inc(s_zP, 1)

                def body(i, more):
                    inputs(i, range(2, G))
                    for half in range(2):
                        pe.wait_ge(s_edge, i * 2 + half + 1)
                        for m in range(8):
                            for n in range(4):
                                last = pe.matmul(cP[half][32 * n:32 * n + 32, :], taps[:, (half * 4 + n) * 8 + m, :],
                                                 z[:, half * 4 + n, PADW - 4 * m:PADW - 4 * m + BL],
                                                 start=(m == 0), stop=(m == 7), skip_group_check=True)
                        last.then_inc(s_cP, 1)
                    if more:
                        front.pe(pe, M, i + 1)
                        inputs(i + 1, (0, 1))
                    pe.wait_ge(s_ga, i * 2 + 2)
                    for j in range(TB):
                        for half in range(2):
                            pe.matmul(yP[:, j, :], ga[:, half, j * P:(j + 1) * P], M.w("c_out", half * P, P),
                                      start=(half == 0), stop=False)
                        last = pe.matmul(yP[:, j, :], M.ones[0:1, :], M.row("c_bout"), start=False, stop=True)
                    last.then_inc(tail.y, 1)

                inputs(0, (0, 1))
                blocks(pe, body)

            @block.scalar
            def _(act):
                act.activation(hb[:, 0:1], M.w("c_ba"), ACT.Copy, scale=0.5).then_inc(s_set, 1)
                act.activation(hb[:, 1:2], M.w("c_bb"), ACT.Copy, scale=0.5).then_inc(s_set, 1)
                act.wait_ge(s_set, 5)
                front.act(act, 0)

                def body(i, more):
                    for n in range(G):
                        act.wait_ge(s_zP, i * G + n + 1)
                        act.activation(z[:, n, PADW:PADW + BL], zP[n % 2][:, :], ACT.Identity,
                                       bias=M.w("c_inb", n, 1)).then_inc(s_z, 1)
                    for half in range(2):
                        act.wait_ge(s_cP, i * 2 + half + 1)
                        act.activation(th[:, half, :], cP[half][:, :], ACT.Tanh, scale=0.5, bias=hb[:, half:half + 1]).then_inc(s_th, 1)
                    if more:
                        act.wait_ge(s_hist, i + 1)
                        front.act(act, i + 1)
                        act.wait_ge(s_keep, i + 2)

                blocks(act, body)

            @block.gpsimd
            def _(pool):
                pool.memset(z[:, :, 0:PADW], 0.0).then_inc(s_set, 1)
                pool.memset(front.hT[:, 0:3], 0.0).then_inc(s_set, 1)
                pool.memset(edge[:, :, :], 1.0).then_inc(s_pool, 1)
                pool.wait_ge(s_pool, 1)
                for a in range(1, 4):
                    pool.memset(edge[32 * a:32 * a + 32, :, 0:a], 0.0).then_inc(s_pool, 1)
                pool.wait_ge(s_pool, 4)
                pool.sem_inc(s_keep, 1)
                front.pool(pool, M, 0)

                def body(i, more):
                    pool.wait_ge(s_z, i * G + 4)
                    pool.tensor_tensor(z[:, 0:4, PADW:PADW + 3], z[:, 0:4, PADW:PADW + 3],
                                       edge[:, :, :].broadcast_to([P, 4, 3]), ALU.mult).then_inc(s_edge, 1)
                    pool.wait_ge(s_zP, i * G + G)
                    alone(pool, M)
                    pool.tensor_copy(front.hT[:, 0:3], front.hT[:, BL:BL + 3]).then_inc(s_hist, 1)
                    pool.wait_ge(s_z, i * G + G)
                    pool.tensor_tensor(z[:, 4:8, PADW:PADW + 3], z[:, 4:8, PADW:PADW + 3],
                                       edge[:, :, :].broadcast_to([P, 4, 3]), ALU.mult).then_inc(s_edge, 1)
                    if more:
                        front.pool(pool, M, i + 1)
                    pool.wait_ge(s_edge, i * 2 + 2)
                    alone(pool, M)
                    pool.memset(edge[:, :, :], 1.0).then_inc(s_pool, 1)
                    pool.wait_ge(s_pool, i + 5)
                    pool.wait_ge(s_cP, i * 2 + 2)
                    alone(pool, M)
                    pool.tensor_copy(z[:, :, 0:PADW], z[:, :, BL:BL + PADW]).then_inc(s_keep, 1)
                    tail.pool(pool, M, i)

                blocks(pool, body)

            @block.vector
            def _(dve):
                diag = M.w("c_diag").rearrange("p (a c) -> p a c", a=1).broadcast_to([P, 64, 32])
                dve.tensor_tensor(taps[:, :, :], M.w("c_taps").rearrange("p (n a) -> p n a", a=1).broadcast_to([P, 64, 32]),
                                  diag, ALU.mult).then_inc(s_set, 1)
                own = Chain(dve, own_dve)
                front.dve(dve, M, own, 0)
                assert own.n == FRONT

                def body(i, more):
                    own = Chain(dve, own_dve, FRONT + i * PER)
                    if more:
                        front.stats(dve, M, own, i + 1)
                        front.apply(dve, M, own, i + 1, after=i + 1)
                    for half in range(2):
                        dve.wait_ge(s_th, i * 2 + half + 1)
                        own(dve.tensor_scalar(sg[:, half, :], th[:, half, :], 0.5, 0.5, ALU.mult, ALU.add))
                    own.wait()
                    for half, b in ((0, "c_ba"), (1, "c_bb")):
                        dve.scalar_tensor_tensor(ga[:, half, :], cP[half][:, :], M.w(b), sg[:, 1 - half, :],
                                                 ALU.add, ALU.mult).then_inc(s_ga, 1)
                    tail.dve(dve, M, own, lambda j: yP[:, j, :], i)
                    assert own.n == PER - (0 if more else FRONT), own.n

                blocks(dve, body)



STEPS = 5


def spiking_layer(nc, M):
    with ExitStack() as ctx:
        S = Scratch(nc, ctx, "l3")
        front, tail = Front(S), Tail(S, EPS * STEPS ** 2)
        hP = [S.ps(f"hP{k}", [P, BL]) for k in range(FC)]
        yP = S.ps("yP", [P, TB, P])
        r = S.sb("relu", [P, FC, BL])
        a = S.sb("act", [P, FC, BL])
        mem = S.sb("membrane", [P, 2, BL])
        spk = S.sb("spike", [P, 2, BL])
        cnt = S.sb("count", [P, TB, P])
        cur = S.sb("current", [P, BL])
        s_cur = S.sem("current_ready")
        s_used = S.sem("current_used")
        s_spk = S.sem("spike_ready")
        s_cnt = S.sem("spike_counted")
        s_hP = S.sem("hidden_in_psum")
        s_r = S.sem("relu_ready")
        s_a = S.sem("act_ready")
        s_y = S.sem("product_in_psum")
        own_dve = S.sem("own_dve")
        FRONT = 13
        PER = 41

        def ahead(eng, body):
            with eng.Fori(0, NB - 2) as i:
                body(i, True, True)
            body(NB - 2, True, False)
            body(NB - 1, False, False)

        with nc.Block() as block:
            @block.tensor
            def _(pe):
                def hidden(i):
                    pe.wait_ge(front.ready, i + 1)
                    for c in range(FC):
                        pe.matmul(hP[c][:, :], M.w("s_fc", c * P, P), front.hT[:, :], start=True, stop=True).then_inc(s_hP, 1)

                def body(i, more):
                    if not (isinstance(i, int) and i == 0):
                        pe.wait_ge(s_cur, i)
                    for c in range(FC):
                        pe.wait_ge(s_a, i * FC + c + 1)
                        for j in range(TB):
                            last = pe.matmul(yP[:, j, :], a[:, c, j * P:(j + 1) * P], M.w("s_proj", c * P, P),
                                             start=(c == 0 and j == 0), stop=(c == FC - 1), skip_group_check=True)
                    last.then_inc(s_y, 1)
                    if more:
                        front.pe(pe, M, i + 1)
                        hidden(i + 1)

                front.pe(pe, M, 0)
                hidden(0)
                body(0, True)
                with pe.Fori(1, NB - 1) as i:
                    body(i, True)
                body(NB - 1, False)

            @block.scalar
            def _(act):
                def relus(i):
                    for c in range(FC):
                        act.wait_ge(s_hP, i * FC + c + 1)
                        act.activation(r[:, c, :], hP[c][:, :], ACT.Relu).then_inc(s_r, 1)

                def body(i, more):
                    if not (isinstance(i, int) and i == 0):
                        act.wait_ge(s_used, i)
                    act.wait_ge(s_y, i + 1)
                    act.copy(cur[:, :], yP[:, :, :].rearrange("p j f -> p (j f)")).then_inc(s_cur, 1)
                    if more:
                        front.act(act, i + 1)
                        relus(i + 1)

                front.act(act, 0)
                relus(0)
                body(0, True)
                with act.Fori(1, NB - 1) as i:
                    body(i, True)
                body(NB - 1, False)

            @block.gpsimd
            def _(pool):
                def body(i, more, more2):
                    c = cnt[:, :, :].rearrange("p j f -> p (j f)")
                    for n in range(1, STEPS - 1):
                        pool.wait_ge(s_spk, i * (STEPS - 1) + n + 1)
                        if n >= 2:
                            pool.wait_ge(s_cnt, i * (STEPS - 2) + n - 1)
                        pool.tensor_tensor(c, c, spk[:, n % 2, :], ALU.add).then_inc(s_cnt, 1)
                    tail.pool(pool, M, i)
                    if more2:
                        front.pool(pool, M, i + 2)

                front.pool(pool, M, 0)
                front.pool(pool, M, 1)
                ahead(pool, body)

            @block.vector
            def _(dve):
                def squares(i):
                    for c in range(FC):
                        dve.wait_ge(s_r, i * FC + c + 1)
                        dve.tensor_tensor(a[:, c, :], r[:, c, :], hP[c][:, :], ALU.mult).then_inc(s_a, 1)

                def neurons(own, i):
                    dve.wait_ge(s_cur, i + 1)
                    c = cnt[:, :, :].rearrange("p j f -> p (j f)")
                    m0, m1 = mem[:, 0, :], mem[:, 1, :]
                    own(dve.tensor_scalar(c, cur[:, :], 1.0, None, ALU.is_gt))
                    own(dve.scalar_tensor_tensor(m1, cur[:, :], 0.9, cur[:, :], ALU.mult, ALU.add))
                    own.wait()
                    dve.sem_inc(s_spk, 1)
                    for n in range(1, STEPS):
                        former = c if n == 1 else spk[:, (n - 1) % 2, :]
                        if n > 1:
                            own(dve.scalar_tensor_tensor(m1, m0, 0.9, cur[:, :], ALU.mult, ALU.add))
                            own.wait()
                        own(dve.tensor_tensor(m0, m1, former, ALU.subtract))
                        own.wait()
                        if n == STEPS - 1:
                            dve.sem_inc(s_used, 1)
                        if n > 2:
                            dve.wait_ge(s_cnt, i * (STEPS - 2) + n - 2)
                        own(dve.tensor_scalar(spk[:, n % 2, :], m0, 1.0, None, ALU.is_gt))
                        own.wait()
                        if n < STEPS - 1:
                            dve.sem_inc(s_spk, 1)
                    dve.wait_ge(s_cnt, i * (STEPS - 2) + STEPS - 2)
                    own(dve.tensor_tensor(c, c, spk[:, (STEPS - 1) % 2, :], ALU.add))
                    own.wait()
                    dve.sem_inc(tail.y, 1)

                def body(i, more, more2):
                    own = Chain(dve, own_dve, 2 * FRONT + i * PER if not isinstance(i, int) or i < NB - 1
                                else 2 * FRONT + i * PER - FRONT)
                    neurons(own, i)
                    tail.stats(dve, M, own, lambda j: cnt[:, j, :], i)
                    if more:
                        squares(i + 1)
                    tail.apply(dve, M, own, lambda j: cnt[:, j, :], i)
                    if more2:
                        front.stats(dve, M, own, i + 2)
                        front.apply(dve, M, own, i + 2, after=i + 2)
                    assert own.n == PER - (0 if more2 else FRONT), own.n

                own = Chain(dve, own_dve)
                front.dve(dve, M, own, 0)
                squares(0)
                front.stats(dve, M, own, 1)
                front.apply(dve, M, own, 1, after=1)
                assert own.n == 2 * FRONT
                ahead(dve, body)



def last_layer(nc, M):
    with ExitStack() as ctx:
        S = Scratch(nc, ctx, "l7")
        front, tail = Front(S), Tail(S)
        hP = [S.ps(f"hP{k}", [P, BL]) for k in range(FC)]
        yP = S.ps("yP", [P, TB, P])
        a = S.sb("act", [P, FC, BL])
        s_hP = S.sem("hidden_in_psum")
        s_a = S.sem("act_ready")
        own_dve = S.sem("own_dve")
        s_yfree = S.sem("product_used")
        FRONT = 13
        PER = 27
        with nc.Block() as block:
            @block.tensor
            def _(pe):
                def body(i, more):
                    pe.wait_ge(front.ready, i + 1)
                    for c in range(FC):
                        pe.matmul(hP[c][:, :], M.w("f_w1", c * P, P), front.hT[:, :], start=True, stop=True).then_inc(s_hP, 1)
                    pe.wait_ge(s_yfree, i + 1)
                    for j in range(TB):
                        pe.matmul(yP[:, j, :], M.ones[0:1, :], M.row("f_b2"), start=(j == 0), stop=False, skip_group_check=True)
                    for c in range(FC):
                        pe.wait_ge(s_a, i * FC + c + 1)
                        for j in range(TB):
                            last = pe.matmul(yP[:, j, :], a[:, c, j * P:(j + 1) * P], M.w("f_w2", c * P, P),
                                             start=False, stop=(c == FC - 1), skip_group_check=True)
                    last.then_inc(tail.y, 1)
                    if more:
                        front.pe(pe, M, i + 1)

                front.pe(pe, M, 0)
                blocks(pe, body)

            @block.scalar
            def _(act):
                def body(i, more):
                    for c in range(FC):
                        act.wait_ge(s_hP, i * FC + c + 1)
                        act.activation(a[:, c, :], hP[c][:, :], ACT.Relu, bias=M.w("f_b1", c, 1)).then_inc(s_a, 1)
                    if more:
                        front.act(act, i + 1)

                front.act(act, 0)
                blocks(act, body)

            @block.gpsimd
            def _(pool):
                norms(pool, M, front, tail)

            @block.vector
            def _(dve):
                def body(i, more):
                    own = Chain(dve, own_dve, FRONT + i * PER)
                    if more:
                        front.stats(dve, M, own, i + 1)
                        front.apply(dve, M, own, i + 1, after=i + 1)
                    tail.dve(dve, M, own, lambda j: yP[:, j, :], i)
                    dve.sem_inc(s_yfree, 1)
                    assert own.n == PER - (0 if more else FRONT), own.n

                dve.sem_inc(s_yfree, 1)
                own = Chain(dve, own_dve)
                front.dve(dve, M, own, 0)
                assert own.n == FRONT
                blocks(dve, body)



def surprise_memory(nc, M):
    with ExitStack() as ctx:
        S = Scratch(nc, ctx, "l4")
        front, tail = Front(S), Tail(S)
        bank = [S.ps(f"bank{k}", [P, BL]) for k in range(3)]
        yP = S.ps("yP", [P, TB, P])
        fcP = [S.ps(f"fcP{k}", [P, BL]) for k in range(2)]
        turnP = S.ps("turnP", [P, TB, P])
        q, k_, g, dec = (S.sb(n, [P, BL]) for n in ("q", "k", "surprise", "decay"))
        half = S.sb("tanh_half", [P, BL])
        m1 = S.sb("m1", [32, BL])
        hb = S.sb("half_bias", [P, 1])
        u = S.sb("u", [P, 3, BL])
        st = S.sb("state", [P, 2, BL])
        last_state = S.sb("last_state", [P, D])
        prod = S.sb("prod", [P, D, BL])
        y = S.sb("y", [P, TB, P])
        sq = S.sb("squares", [P, TB, P])
        ms = S.sb("mean_square", [P, 2, TB])
        rms = S.sb("rms", [P, TB])
        yn = S.sb("yn", [P, TB, P])
        ynT = S.sb("ynT", [P, BL])
        r = S.sb("relu", [P, 2, BL])
        a = S.sb("act", [P, FC, BL])
        out = S.sb("out", [P, TB, P])
        s_m1P = S.sem("m1_in_psum")
        s_m1 = S.sem("m1_ready")
        s_gP = S.sem("surprise_in_psum")
        s_g = S.sem("tanh_ready")
        s_qP = S.sem("q_in_psum")
        s_q = S.sem("q_ready")
        s_kP = S.sem("k_in_psum")
        s_k = S.sem("gated_k_ready")
        s_vP = S.sem("v_in_psum")
        s_u = S.sem("v_bank_used")
        s_st = S.sem("state_ready")
        s_prod = S.sem("q_times_state")
        s_yP = S.sem("y_in_psum")
        s_y = S.sem("y_in_sbuf")
        s_ms = S.sem("mean_square_ready")
        s_rms = S.sem("rms_ready")
        s_yn = S.sem("yn_ready")
        s_ynP = S.sem("yn_turned")
        s_ynT = S.sem("ynT_ready")
        s_hP = S.sem("hidden_in_psum")
        s_r = S.sem("relu_ready")
        s_a = S.sem("act_ready")
        s_mlp = S.sem("mlp_in_psum")
        s_out = S.sem("out_ready")
        own_dve = S.sem("own_dve")
        own_act = S.sem("own_act")
        PER = 48
        with nc.Block() as block:
            @block.tensor
            def _(pe):
                def turn_yn(i):
                    pe.wait_ge(s_yn, i + 1)
                    for t in range(TB):
                        last = pe.transpose(turnP[:, t, :], yn[:, t, :], M.eye)
                    last.then_inc(s_ynP, 1)

                def hidden(i, chunks):
                    pe.wait_ge(s_ynT, i + 1)
                    for c in chunks:
                        if c >= 2:
                            pe.wait_ge(s_a, i * FC + c - 1)
                        pe.matmul(fcP[c % 2][:, :], M.w("g_fc", c * P, P), ynT[:, :], start=True, stop=True).then_inc(s_hP, 1)

                def down(i):
                    pe.wait_ge(s_a, i * FC + FC)
                    for t in range(TB):
                        for c in range(FC):
                            last = pe.matmul(turnP[:, t, :], a[:, c, t * P:(t + 1) * P], M.w("g_cp", c * P, P),
                                             start=(c == 0), stop=(c == FC - 1))
                    last.then_inc(s_mlp, 1)

                hT = front.hT[:, :]

                def gates(i):
                    pe.wait_ge(front.ready, i + 1)
                    pe.matmul(bank[0][0:32, :], M.w("g_m1"), hT, start=True, stop=True).then_inc(s_m1P, 1)
                    if not (isinstance(i, int) and i == 0):
                        pe.wait_ge(s_u, i * D)
                    pe.matmul(bank[1][:, :], M.w("g_k"), hT, start=True, stop=True).then_inc(s_kP, 1)
                    pe.matmul(bank[2][:, :], M.w("g_q"), hT, start=True, stop=True).then_inc(s_qP, 1)
                    pe.wait_ge(s_m1, i + 1)
                    pe.matmul(bank[0][:, :], M.w("g_m2")[0:32, :], m1[:, :], start=True, stop=True).then_inc(s_gP, 1)

                def project(i, j, first):
                    if j == 0 and not first:
                        pe.wait_ge(s_y, i)
                    pe.wait_ge(s_prod, i * D + j + 1)
                    for t in range(TB):
                        last = pe.matmul(yP[:, t, :], prod[:, j, t * P:(t + 1) * P], M.w("g_proj", j * P, P),
                                         start=(j == 0 and t == 0),
                                         stop=(j == D - 1), skip_group_check=True)
                    if j == D - 1:
                        last.then_inc(s_yP, 1)

                def body(i, first, more):
                    pe.wait_ge(s_k, i + 1)
                    for j in range(D):
                        if j == 1:
                            pe.wait_ge(s_q, i + 1)
                        if j >= 2:
                            pe.wait_ge(s_u, i * D + j - 1)
                        pe.matmul(bank[1 + j % 2][:, :], M.w("g_v", j * P, P), hT, start=True, stop=True).then_inc(s_vP, 1)
                        if j >= 3:
                            project(i, j - 3, first)
                        if not first:
                            if j == 3:
                                turn_yn(i - 1)
                            if j == 4:
                                hidden(i - 1, (0, 1))
                            if j == 6:
                                hidden(i - 1, (2, 3))
                    if more:
                        front.pe(pe, M, i + 1)
                    project(i, D - 3, first)
                    if more:
                        gates(i + 1)
                    project(i, D - 2, first)
                    if not first:
                        down(i - 1)
                    project(i, D - 1, first)

                front.pe(pe, M, 0)
                gates(0)
                body(0, True, True)
                with pe.Fori(1, NB - 1) as i:
                    body(i, False, True)
                body(NB - 1, False, False)
                turn_yn(NB - 1)
                hidden(NB - 1, range(FC))
                down(NB - 1)

            @block.scalar
            def _(act):
                def part_b(i):
                    act.wait_ge(s_ynP, i + 1)
                    act.copy(ynT[:, :], turnP[:, :, :].rearrange("p t f -> p (t f)")).then_inc(s_ynT, 1)
                    for c in range(FC):
                        act.wait_ge(s_hP, i * FC + c + 1)
                        if c >= 2:
                            act.wait_ge(s_a, i * FC + c - 1)
                        act.activation(r[:, c % 2, :], fcP[c % 2][:, :], ACT.Relu).then_inc(s_r, 1)

                def gates(i):
                    act.wait_ge(s_m1P, i + 1)
                    act.activation(m1[:, :], bank[0][0:32, :], ACT.Relu, bias=M.w("g_bm1")[0:32, :]).then_inc(s_m1, 1)
                    if not (isinstance(i, int) and i == 0):
                        act.wait_ge(s_prod, i * D)
                    act.wait_ge(s_qP, i + 1)
                    act.copy(q[:, :], bank[2][:, :]).then_inc(s_q, 1)
                    act.wait_ge(s_gP, i + 1)
                    act.activation(half[:, :], bank[0][:, :], ACT.Tanh, scale=0.5, bias=hb[:, :]).then_inc(s_g, 1)

                def body(i, first, more):
                    if not first:
                        part_b(i - 1)
                    if more:
                        front.act(act, i + 1)
                        gates(i + 1)
                    act.wait_ge(s_out, i + 1)
                    act.wait_ge(s_yP, i + 1)
                    act.copy(y[:, :, :], yP[:, :, :]).then_inc(s_y, 1)

                act.activation(hb[:, :], M.w("g_bm2"), ACT.Copy, scale=0.5).then_inc(own_act, 1)
                act.wait_ge(own_act, 1)
                front.act(act, 0)
                gates(0)
                body(0, True, True)
                with act.Fori(1, NB - 1) as i:
                    body(i, False, True)
                body(NB - 1, False, False)
                part_b(NB - 1)

            @block.gpsimd
            def _(pool):
                def root(i):
                    pool.wait_ge(s_ms, i + 1)
                    pool.tensor_tensor(rms[:, :], ms[:, 1, :], M.mhalf[:, 0:TB], ALU.pow).then_inc(s_rms, 1)

                def body(i, first, more):
                    pool.wait_ge(s_q, i + 1)
                    for j in range(D):
                        pool.wait_ge(s_st, i * D + j + 1)
                        pool.tensor_tensor(prod[:, j, :], q[:, :], st[:, j % 2, :], ALU.mult).then_inc(s_prod, 1)
                        if j == 0 and not first:
                            root(i - 1)
                        if j == 3 and more:
                            front.pool(pool, M, i + 1)
                    if not first:
                        tail.pool(pool, M, i - 1)

                front.pool(pool, M, 0)
                body(0, True, True)
                with pool.Fori(1, NB - 1) as i:
                    body(i, False, True)
                body(NB - 1, False, False)
                root(NB - 1)
                tail.pool(pool, M, NB - 1)

            @block.vector
            def _(dve):
                def mean_square(own, i):
                    dve.wait_ge(s_y, i + 1)
                    for t in range(TB):
                        own(dve.tensor_tensor_reduce(out=sq[:, t, :], in0=y[:, t, :], in1=y[:, t, :], scale=1.0, scalar=0.0,
                                                     op0=ALU.mult, op1=ALU.add, accum_out=ms[:, 0, t:t + 1]))
                    own.wait()
                    own(dve.tensor_scalar(ms[:, 1, :], ms[:, 0, :], 1.0 / P, float(np.finfo(np.float32).eps), ALU.mult, ALU.add))
                    own.wait()
                    dve.sem_inc(s_ms, 1)

                def scaled(own, i):
                    dve.wait_ge(s_rms, i + 1)
                    for t in range(TB):
                        own(dve.tensor_scalar(yn[:, t, :], y[:, t, :], rms[:, t:t + 1], None, ALU.mult))
                    own.wait()
                    dve.sem_inc(s_yn, 1)

                def squares(i, chunks):
                    for c in chunks:
                        dve.wait_ge(s_r, i * FC + c + 1)
                        dve.tensor_tensor(a[:, c, :], r[:, c % 2, :], fcP[c % 2][:, :], ALU.mult).then_inc(s_a, 1)

                def finish(own, i):
                    dve.wait_ge(s_mlp, i + 1)
                    own(dve.tensor_tensor(out[:, :, :], y[:, :, :], turnP[:, :, :], ALU.add))
                    own.wait()
                    dve.sem_inc(s_out, 1)
                    dve.sem_inc(tail.y, 1)
                    tail.dve(dve, M, own, lambda j: out[:, j, :], i)

                def gates(own, i):
                    dve.wait_ge(s_g, i + 1)
                    own(dve.tensor_scalar(g[:, :], half[:, :], 0.5, 0.5, ALU.mult, ALU.add))
                    own.wait()
                    own(dve.tensor_scalar(dec[:, :], g[:, :], -1.0, 1.0, ALU.mult, ALU.add))
                    dve.wait_ge(s_kP, i + 1)
                    own(dve.tensor_tensor(k_[:, :], g[:, :], bank[1][:, :], ALU.mult))
                    own.wait()
                    dve.sem_inc(s_k, 1)

                def body(i, first, more, base):
                    own = Chain(dve, own_dve, base)

                    def weigh(j):
                        dve.wait_ge(s_vP, i * D + j + 1)
                        dve.tensor_tensor(u[:, j % 3, :], k_[:, :], bank[1 + j % 2][:, :], ALU.mult).then_inc(s_u, 1)

                    def keep(j):
                        dve.wait_ge(s_st, i * D + j + 1)
                        own(dve.tensor_copy(last_state[:, j:j + 1], st[:, j % 2, BL - 1:BL]))

                    weigh(0)
                    for j in range(D):
                        if j + 1 < D:
                            weigh(j + 1)
                        if j >= 2:
                            dve.wait_ge(s_prod, i * D + j - 1)
                        own.wait()
                        dve.wait_ge(s_u, i * D + j + 1)
                        dve.tensor_tensor_scan(st[:, j % 2, :], dec[:, :], u[:, j % 3, :], last_state[:, j:j + 1],
                                               ALU.mult, ALU.add).then_inc(s_st, 1)
                        if j >= 1:
                            keep(j - 1)
                        if not first:
                            if j == 0:
                                mean_square(own, i - 1)
                            if j == 1:
                                scaled(own, i - 1)
                            if j == 4:
                                squares(i - 1, (0, 1))
                            if j == 6:
                                squares(i - 1, (2, 3))
                        if more:
                            if j == 3:
                                front.stats(dve, M, own, i + 1)
                            if j == 5:
                                front.apply(dve, M, own, i + 1, after=i + 1)
                    keep(D - 1)
                    if more:
                        gates(own, i + 1)
                    if not first:
                        finish(own, i - 1)
                    return own.n

                own = Chain(dve, own_dve)
                own(dve.memset(last_state[:, :], 0.0))
                own(dve.memset(ms[:, :, :], 0.0))
                own.wait()
                dve.sem_inc(s_out, 1)
                front.dve(dve, M, own, 0)
                gates(own, 0)
                n = own.n
                n += body(0, True, True, n)
                with dve.Fori(1, NB - 1) as i:
                    assert body(i, False, True, n + (i - 1) * PER) == PER
                n += (NB - 2) * PER
                n += body(NB - 1, False, False, n)
                own = Chain(dve, own_dve, n)
                mean_square(own, NB - 1)
                scaled(own, NB - 1)
                squares(NB - 1, range(FC))
                finish(own, NB - 1)



def channel_mix(nc, M):
    with ExitStack() as ctx:
        S = Scratch(nc, ctx, "l5")
        front, tail = Front(S, pad=1), Tail(S)
        kP = S.ps("kP", [P, BL])
        rP = S.ps("rP", [P, TB, P])
        vP = S.ps("vP", [P, TB, P])
        rest = S.sb("one_minus_mu", [P, 2])
        now = S.sb("now", [P, 2, BL])
        xr = S.sb("xr", [P, BL])
        xk = S.sb("xk", [P, BL])
        relu = S.sb("relu", [P, BL])
        ka = S.sb("k_act", [P, BL])
        half = S.sb("tanh_half", [P, TB, P])
        r = S.sb("r", [P, TB, P])
        y = S.sb("y", [P, TB, P])
        s_mix = S.sem("mixed")
        s_kP = S.sem("k_in_psum")
        s_rP = S.sem("r_in_psum")
        s_relu = S.sem("relu_ready")
        s_ka = S.sem("k_act_ready")
        s_r = S.sem("tanh_ready")
        s_vP = S.sem("v_in_psum")
        own_dve = S.sem("own_dve")
        s_keep = S.sem("history_kept")
        FRONT = 13
        MIX = 4
        FIRST, PER = 3 + FRONT, 33
        with nc.Block() as block:
            @block.tensor
            def _(pe):
                def body(i, more):
                    pe.wait_ge(s_mix, i + 1)
                    pe.matmul(kP[:, :], M.w("r_k"), xk[:, :], start=True, stop=True).then_inc(s_kP, 1)
                    for j in range(TB):
                        last = pe.matmul(rP[:, j, :], xr[:, j * P:(j + 1) * P], M.w("r_r"), start=True, stop=True)
                    last.then_inc(s_rP, 1)
                    if more:
                        front.pe(pe, M, i + 1)
                    pe.wait_ge(s_ka, i + 1)
                    for j in range(TB):
                        last = pe.matmul(vP[:, j, :], ka[:, j * P:(j + 1) * P], M.w("r_v"), start=True, stop=True)
                    last.then_inc(s_vP, 1)

                front.pe(pe, M, 0)
                blocks(pe, body)

            @block.scalar
            def _(act):
                def body(i, more):
                    act.wait_ge(s_kP, i + 1)
                    act.activation(relu[:, :], kP[:, :], ACT.Relu).then_inc(s_relu, 1)
                    act.wait_ge(s_rP, i + 1)
                    act.activation(half[:, :, :], rP[:, :, :], ACT.Tanh, scale=0.5).then_inc(s_r, 1)
                    if more:
                        act.wait_ge(s_keep, i + 2)
                        front.act(act, i + 1)

                front.act(act, 0)
                blocks(act, body)

            @block.gpsimd
            def _(pool):
                norms(pool, M, front, tail)

            @block.vector
            def _(dve):
                first = Chain(dve, own_dve)
                mu = [M.w("r_mur"), M.w("r_muk")]
                for k in range(2):
                    first(dve.tensor_scalar(rest[:, k:k + 1], mu[k], -1.0, 1.0, ALU.mult, ALU.add))
                first(dve.memset(front.hT[:, 0:1], 0.0))
                first.wait()
                dve.sem_inc(s_keep, 1)
                front.dve(dve, M, first, 0)
                assert first.n == FIRST

                def mix(own, i):
                    dve.wait_ge(front.ready, i + 1)
                    for k in range(2):
                        own(dve.tensor_scalar(now[:, k, :], front.hT[:, 1:1 + BL], mu[k], None, ALU.mult))
                    own.wait()
                    for k, dst in ((0, xr), (1, xk)):
                        own(dve.scalar_tensor_tensor(dst[:, :], front.hT[:, 0:BL], rest[:, k:k + 1], now[:, k, :], ALU.mult, ALU.add))
                    own.wait()
                    dve.sem_inc(s_mix, 1)
                    dve.tensor_copy(front.hT[:, 0:1], front.hT[:, BL:BL + 1]).then_inc(s_keep, 1)

                def body(i, more):
                    own = Chain(dve, own_dve, i * PER + FIRST + MIX)
                    if more:
                        front.stats(dve, M, own, i + 1)
                    dve.wait_ge(s_relu, i + 1)
                    dve.tensor_tensor(ka[:, :], relu[:, :], kP[:, :], ALU.mult).then_inc(s_ka, 1)
                    if more:
                        front.apply(dve, M, own, i + 1, after=i + 1)
                    dve.wait_ge(s_r, i + 1)
                    own(dve.tensor_scalar(r[:, :, :], half[:, :, :], 0.5, 0.5, ALU.mult, ALU.add))
                    own.wait()
                    dve.wait_ge(s_vP, i + 1)
                    own(dve.tensor_tensor(y[:, :, :], r[:, :, :], vP[:, :, :], ALU.mult))
                    own.wait()
                    dve.sem_inc(tail.y, 1)
                    tail.stats(dve, M, own, lambda j: y[:, j, :], i)
                    if more:
                        mix(own, i + 1)
                    tail.apply(dve, M, own, lambda j: y[:, j, :], i)
                    assert own.n == PER - (0 if more else FRONT + MIX), own.n

                mix(first, 0)
                assert first.n == FIRST + MIX
                blocks(dve, body)



LR = 1e-3
NCH = NT
GS = 2.0 / P
QUICK, FULL = 5, 3 * P + 1
TOLS = [(2.0 ** -20, 2.0 ** -19), (2.0 ** -18, 2.0 ** -18)]
SHRINK = 8


def test_time_mlp(nc, M):
    with ExitStack() as ctx:
        S = Scratch(nc, ctx, "l6")
        M.hT = S.sb("hT_all", [P, T])
        M.kT = S.sb("kT_all", [P, T])
        M.vT = S.sb("vT_all", [P, T])
        M.M1 = S.sb("M1_all", [P, T])
        M.Kt = S.sb("K_all", [P, T])
        M.W1, M.W2h, M.W2T = (S.sb(n, [P, P]) for n in ("W1", "W2_half", "W2T"))
        M.before4, M.before2 = S.sb("before4", [P, P]), S.sb("before2", [P, P])
        M.b1, M.b2 = S.sb("b1", [P, 1]), S.sb("b2", [P, 1])
        keys_and_values(nc, M)
        learn(nc, M)
        answer(nc, M)


def keys_and_values(nc, M):
    with ExitStack() as ctx:
        S = Scratch(nc, ctx, "l6a")
        front = Front(S)
        kvP = [S.ps(f"kvP{k}", [P, BL]) for k in range(2)]
        gramP = S.ps("gramP", [P, TB, P])
        keyP = S.ps("keyP", [P, BL])
        k4 = S.sb("k_block", [P, BL])
        s_kvP = S.sem("kv_in_psum")
        s_k = S.sem("k_ready")
        s_gram = S.sem("gram_in_psum")
        s_m1 = S.sem("gram_masked")
        s_keyP = S.sem("keys_turned")
        s_key = S.sem("keys_ready")
        own_dve = S.sem("own_dve")
        PER = 13
        with nc.Block() as block:
            @block.tensor
            def _(pe):
                front.pe(pe, M, 0)

                def body(i, more):
                    pe.wait_ge(front.ready, i + 1)
                    for n in range(2):
                        last = pe.matmul(kvP[n][:, :], M.w("t_kv", n * P, P), front.hT[:, :], start=True, stop=True)
                    last.then_inc(s_kvP, 1)
                    if more:
                        front.pe(pe, M, i + 1)
                    pe.wait_ge(s_k, i + 1)
                    for j in range(TB):
                        kj = k4[:, j * P:(j + 1) * P]
                        last = pe.matmul(gramP[:, j, :], kj, kj, start=True, stop=True)
                    last.then_inc(s_gram, 1)
                    for j in range(TB):
                        last = pe.transpose(keyP[:, j * P:(j + 1) * P], k4[:, j * P:(j + 1) * P], M.eye)
                    last.then_inc(s_keyP, 1)
                    if more:
                        pe.wait_ge(s_key, i + 1)
                        pe.wait_ge(s_m1, i + 1)

                blocks(pe, body)

            @block.scalar
            def _(act):
                block_of = lambda x, i: x[:, i * BL:(i + 1) * BL] if isinstance(i, int) else x[:, bass.ds(i * BL, BL)]

                def begin(i):
                    act.wait_ge(front.turned, i + 1)
                    act.copy(block_of(M.hT, i), front.bank[:, :])
                    front.act(act, i)

                def body(i, more):
                    act.wait_ge(s_kvP, i + 1)
                    act.copy(k4[:, :], kvP[0][:, :]).then_inc(s_k, 1)
                    act.copy(block_of(M.kT, i), kvP[0][:, :])
                    if more:
                        begin(i + 1)
                    act.copy(block_of(M.vT, i), kvP[1][:, :])
                    act.wait_ge(s_keyP, i + 1)
                    act.copy(block_of(M.Kt, i), keyP[:, :]).then_inc(s_key, 1)

                begin(0)
                blocks(act, body)

            @block.gpsimd
            def _(pool):
                with pool.Fori(0, NB) as i:
                    front.pool(pool, M, i)

            @block.vector
            def _(dve):
                own = Chain(dve, own_dve)
                front.dve(dve, M, own, 0)
                own(dve.tensor_scalar(M.before4[:, :], M.w("t_before"), -LR / 4, None, ALU.mult))
                own(dve.tensor_scalar(M.before2[:, :], M.w("t_before"), -LR / 2, None, ALU.mult))
                own.wait()
                n = own.n

                def body(i, more):
                    own = Chain(dve, own_dve, i * PER + n)
                    if more:
                        front.stats(dve, M, own, i + 1)
                        front.apply(dve, M, own, i + 1, after=i + 1)
                        assert own.n == PER, own.n
                    dve.wait_ge(s_gram, i + 1)
                    M1 = M.M1[:, i * BL:(i + 1) * BL] if isinstance(i, int) else M.M1[:, bass.ds(i * BL, BL)]
                    dve.scalar_tensor_tensor(M1.rearrange("p (t q) -> p t q", t=TB), gramP[:, :, :], 1.0,
                                             M.before4[:, :].rearrange("p (a q) -> p a q", a=1).broadcast_to([P, TB, P]),
                                             ALU.add, ALU.mult).then_inc(s_m1, 1)

                blocks(dve, body)


def learn(nc, M):
    with ExitStack() as ctx:
        S = Scratch(nc, ctx, "l6b")
        hTP, hP, oP, gP, aaP, eeP, etP, dP = (S.ps(n, [P, BL]) for n in ("hTP", "hP", "oP", "gP", "aaP", "eeP", "etP", "dP"))
        b_ = lambda x: x[:, 0:P]
        names = ("M1", "Kt", "hb", "tT", "tt", "w", "z", "bv", "M2", "M3", "E", "G4")
        M1, Kt, hb, tT, tt, w, z, bv, M2, M3, E, G4 = (S.sb(n, [P, P]) for n in names)
        A2 = S.sb("A2", [P, 2, P])
        ae = [S.sb(n, [P, 2, P]) for n in ("ae", "ae_before", "ae_last")]
        names = ("diff", "diff_before", "square", "changes", "changes_before", "sizes")
        diff, diff0, square, changes, changes0, sizes = (S.sb(n, [P, 2, P]) for n in names)
        red = S.sb("reduced", [P, 6, 2])
        bad = S.sb("not_settled", [P, 2])
        total = S.sb("total", [P, 1])
        allones = S.sb("all_ones", [P, P])
        flag = S.sb("flag", [P, 1], I32)
        sem = lambda n: S.sem(n)
        s_hT = sem("hT_in_psum")
        s_tT = sem("tanhT_ready")
        s_aT = sem("aT_ready")
        s_hP = sem("h_in_psum")
        s_tt = sem("tanh_ready")
        s_A = sem("A_ready")
        s_w = sem("w_ready")
        s_z = sem("derivative_ready")
        s_o = sem("o_in_psum")
        s_aa = sem("aa_in_psum")
        s_M2 = sem("M2_ready")
        s_e = sem("eT_ready")
        s_g = sem("g_in_psum")
        s_G = sem("G_ready")
        s_ee = sem("ee_in_psum")
        s_M3 = sem("M3_ready")
        s_et = sem("e_turned")
        s_E = sem("E_ready")
        own_pool = sem("own_pool")
        s_h0 = sem("start_h_in_psum")
        s_hb = sem("start_h_ready")
        s_bv = sem("bv_ready")
        s_m1 = sem("gram_copied")
        s_d1 = sem("w1_update_in_psum")
        s_d2 = sem("w2_update_in_psum")
        s_w1 = sem("w1_updated")
        s_w2 = sem("w2_updated")
        s_diff = sem("change_taken")
        own_w = sem("own_dve_updates")
        s_set = sem("pass_set_up")
        s_all = sem("pass_checked")
        s_bad = sem("not_settled_ready")
        s_sum = sem("not_settled_summed")
        s_flag = sem("flag_ready")
        own_set = sem("own_dve_set_up")
        N_SET, N_CHECK, POOL_CH = 9, 14, 8

        def set_up(dve, first):
            own = Chain(dve, own_set, 1 if first else 1 + N_SET + N_CHECK)
            own(dve.tensor_copy(M.W1[:, :], M.w("t_w1")))
            own(dve.tensor_scalar(M.W2h[:, :], M.w("t_w2"), 0.5, None, ALU.mult))
            own(dve.tensor_copy(M.W2T[:, :], M.w("t_w2t")))
            own(dve.tensor_copy(M.b1[:, :], M.w("t_b1")))
            own(dve.tensor_copy(M.b2[:, :], M.w("t_b2")))
            own(dve.memset(changes[:, :, :], 0.0))
            own(dve.memset(changes0[:, :, :], 0.0))
            own(dve.memset(sizes[:, :, :], 0.0))
            own.wait()
            own(dve.memset(bad[:, :], 0.0))
            own.wait()
            assert own.n == N_SET
            dve.sem_inc(s_set, 1)

        class Step:

            def __init__(self, c, it, NI, n0, k0, q0, p, buf=0, first=False, last=False):
                self.n = n0 + c * NI + it
                self.k = k0 + c * (NI - 1) + it
                self.q = q0 + c * (NI - 1) + it - 1
                self.p, self.first, self.last = p, first, last
                self.ae = ae[buf]

        def steps(eng, c, NI, n0, k0, q0, body):
            body(Step(c, 0, NI, n0, k0, q0, 0, first=True))
            with eng.Fori(0, (NI - 3) // 2) as m:
                for r in range(2):
                    body(Step(c, m * 2 + (r + 1), NI, n0, k0, q0, (r + 1) % 2))
            body(Step(c, NI - 2, NI, n0, k0, q0, 1, buf=1))
            body(Step(c, NI - 1, NI, n0, k0, q0, 0, buf=2, last=True))

        def tensor_pass(pe, NI, n0, k0, q0, c0):
            def body(s, c=None):
                if s.first:
                    pe.transpose(b_(hP), hb[:, :], M.eye).then_inc(s_hP, 1)
                else:
                    pe.wait_ge(s_G, s.n)
                    pe.matmul(b_(hTP), G4[:, :], M1[:, :], start=False, stop=True).then_inc(s_hT, 1)
                    pe.matmul(b_(hP), M1[:, :], G4[:, :], start=False, stop=True).then_inc(s_hP, 1)
                    pe.wait_ge(s_E, s.n)
                    pe.wait_ge(s_M2, s.k)
                    pe.matmul(b_(oP), E[:, :], M2[:, :], start=True, stop=False)
                pe.wait_ge(s_aT, s.n + 1)
                pe.matmul(b_(oP), M.W2h[:, :], s.ae[:, 0, :], start=s.first, stop=True).then_inc(s_o, 1)
                if not s.last:
                    pe.matmul(b_(aaP), s.ae[:, 0, :], s.ae[:, 0, :], start=True, stop=True).then_inc(s_aa, 1)
                    pe.matmul(b_(hTP), M.eye, hb[:, :], start=True, stop=False)
                if not s.first:
                    pe.wait_ge(s_M3, s.k)
                    pe.matmul(b_(gP), M3[:, :], A2[:, 1 - s.p, :], start=True, stop=False)
                if not s.last:
                    pe.wait_ge(s_A, s.n + 1)
                    pe.matmul(b_(hP), hb[:, :], M.eye, start=True, stop=False)
                pe.wait_ge(s_e, s.n + 1)
                pe.matmul(b_(gP), s.ae[:, 1, :], M.W2T[:, :], start=s.first, stop=True).then_inc(s_g, 1)
                pe.transpose(b_(etP), s.ae[:, 1, :], M.eye).then_inc(s_et, 1)
                if not s.last:
                    pe.matmul(b_(eeP), s.ae[:, 1, :], s.ae[:, 1, :], start=True, stop=True).then_inc(s_ee, 1)
                if s.first:
                    pe.wait_ge(s_m1, c0 + c + 1)
                    alone(pe, M)

            pe.wait_ge(s_set, 1 if n0 == 0 else 2)
            with pe.Fori(0, NCH) as c:
                pe.wait_ge(s_w1, c0 + c + 1)
                pe.matmul(b_(hTP), M.W1[:, :], M.kT[:, bass.ts(c, P)], start=True, stop=True).then_inc(s_h0, 1)
                pe.wait_ge(s_w2, c0 + c + 1)
                pe.wait_ge(s_hb, c0 + c + 1)
                steps(pe, c, NI, n0, k0, q0, lambda s: body(s, c))
                pe.wait_ge(s_G, n0 + c * NI + NI)
                pe.matmul(b_(hTP), Kt[:, :], G4[:, :], start=True, stop=True)
                pe.matmul(hTP[:, P:P + 1], G4[:, :], allones[:, 0:1], start=True, stop=True).then_inc(s_d1, 1)
                pe.wait_ge(s_E, n0 + c * NI + NI)
                AL = A2[:, (NI - 1) % 2, :]
                pe.matmul(b_(dP), AL, E[:, :], start=True, stop=True)
                pe.matmul(dP[:, P:2 * P], E[:, :], AL, start=True, stop=True)
                pe.matmul(dP[:, 2 * P:2 * P + 1], E[:, :], allones[:, 0:1], start=True, stop=True).then_inc(s_d2, 1)

        def scalar_pass(act, NI, n0, k0, q0, c0):
            def body(s, c=None):
                if s.first:
                    act.wait_ge(s_hb, c0 + c + 1)
                    act.activation(tT[:, :], hb[:, :], ACT.Tanh, scale=0.5).then_inc(s_tT, 1)
                else:
                    act.wait_ge(s_hT, s.q + 1)
                    act.activation(tT[:, :], b_(hTP), ACT.Tanh, scale=0.5).then_inc(s_tT, 1)
                act.wait_ge(s_hP, s.n + 1)
                act.activation(tt[:, :], b_(hP), ACT.Tanh, scale=0.5).then_inc(s_tt, 1)
                if s.first:
                    act.wait_ge(s_d1, c0 + c + 1)
                    act.copy(M1[:, :], M.M1[:, bass.ts(c, P)])
                    act.copy(Kt[:, :], M.Kt[:, bass.ts(c, P)]).then_inc(s_m1, 1)
                act.wait_ge(s_et, s.n + 1)
                act.copy(E[:, :], b_(etP)).then_inc(s_E, 1)

            act.wait_ge(s_set, 1 if n0 == 0 else 2)
            with act.Fori(0, NCH) as c:
                steps(act, c, NI, n0, k0, q0, lambda s: body(s, c))

        def vector_pass(dve, NI, n0, k0, q0, c0):
            def body(s, c=None):
                aT, eT = s.ae[:, 0, :], s.ae[:, 1, :]
                if s.first:
                    dve.wait_ge(s_h0, c0 + c + 1)
                    dve.tensor_scalar(hb[:, :], b_(hTP), M.b1[:, :], None, ALU.add).then_inc(s_hb, 1)
                    dve.tensor_scalar(bv[:, :], M.vT[:, bass.ts(c, P)], M.b2[:, :], -GS, ALU.subtract, ALU.mult).then_inc(s_bv, 1)
                    dve.wait_ge(s_diff, c0 + c + 1)
                dve.wait_ge(s_tT, s.n + 1)
                dve.scalar_tensor_tensor(aT, tT[:, :], 1.0, hb[:, :] if s.first else b_(hTP), ALU.add, ALU.mult).then_inc(s_aT, 1)
                dve.wait_ge(s_tt, s.n + 1)
                dve.scalar_tensor_tensor(A2[:, s.p, :], tt[:, :], 1.0, b_(hP), ALU.add, ALU.mult).then_inc(s_A, 1)
                dve.wait_ge(s_A, s.n + 1)
                dve.scalar_tensor_tensor(w[:, :], tt[:, :], 1.0, A2[:, s.p, :], ALU.subtract, ALU.mult).then_inc(s_w, 1)
                dve.wait_ge(s_o, s.n + 1)
                if s.first:
                    dve.wait_ge(s_bv, c0 + c + 1)
                dve.scalar_tensor_tensor(eT, b_(oP), GS, bv[:, :], ALU.mult, ALU.add).then_inc(s_e, 1)
                dve.wait_ge(s_w, s.n + 1)
                dve.scalar_tensor_tensor(z[:, :], tt[:, :], 2.0, w[:, :], ALU.mult, ALU.subtract).then_inc(s_z, 1)
                if not s.last:
                    dve.wait_ge(s_aa, s.k + 1)
                    dve.scalar_tensor_tensor(M2[:, :], b_(aaP), 4.0, M.before4[:, :], ALU.add, ALU.mult).then_inc(s_M2, 1)
                dve.wait_ge(s_g, s.n + 1)
                dve.wait_ge(s_z, s.n + 1)
                dve.scalar_tensor_tensor(G4[:, :], z[:, :], 2.0, b_(gP), ALU.add, ALU.mult).then_inc(s_G, 1)
                if not s.last:
                    dve.wait_ge(s_ee, s.k + 1)
                    dve.tensor_tensor(M3[:, :], b_(eeP), M.before2[:, :], ALU.mult).then_inc(s_M3, 1)

            with dve.Fori(0, NCH) as c:
                steps(dve, c, NI, n0, k0, q0, lambda s: body(s, c))
                dve.wait_ge(s_d1, c0 + c + 2)
                dve.scalar_tensor_tensor(M.W1[:, :], b_(hTP), -LR / 4, M.W1[:, :], ALU.mult, ALU.add)
                dve.scalar_tensor_tensor(M.b1[:, :], hTP[:, P:P + 1], -LR / 4, M.b1[:, :], ALU.mult, ALU.add).then_inc(s_w1, 1)
                dve.wait_ge(s_d2, c0 + c + 1)
                dve.scalar_tensor_tensor(M.b2[:, :], dP[:, 2 * P:2 * P + 1], -LR, M.b2[:, :], ALU.mult, ALU.add)
                dve.scalar_tensor_tensor(M.W2h[:, :], b_(dP), -LR / 4, M.W2h[:, :], ALU.mult, ALU.add)
                dve.scalar_tensor_tensor(M.W2T[:, :], dP[:, P:2 * P], -LR / 2, M.W2T[:, :], ALU.mult, ALU.add).then_inc(s_w2, 1)
                dve.wait_ge(s_w1, c0 + c + 2)
                dve.wait_ge(s_w2, c0 + c + 2)

        def pool_pass(pool, NI, n0, k0, q0, c0):
            pool.wait_ge(s_set, 1 if n0 == 0 else 2)
            with pool.Fori(0, NCH) as c:
                own = (c0 + c) * POOL_CH
                pool.wait_ge(s_e, n0 + c * NI + NI)
                pool.tensor_tensor(diff0[:, :, :], ae[1][:, :, :], ae[0][:, :, :], ALU.subtract).then_inc(own_pool, 1)
                pool.tensor_tensor(diff[:, :, :], ae[2][:, :, :], ae[1][:, :, :], ALU.subtract).then_inc(own_pool, 1)
                pool.tensor_tensor(square[:, :, :], ae[2][:, :, :], ae[2][:, :, :], ALU.mult).then_inc(own_pool, 1)
                pool.wait_ge(own_pool, own + 3)
                pool.sem_inc(s_diff, 1)
                pool.tensor_tensor(diff0[:, :, :], diff0[:, :, :], diff0[:, :, :], ALU.mult).then_inc(own_pool, 1)
                pool.tensor_tensor(diff[:, :, :], diff[:, :, :], diff[:, :, :], ALU.mult).then_inc(own_pool, 1)
                pool.wait_ge(own_pool, own + 5)
                pool.tensor_tensor(changes0[:, :, :], changes0[:, :, :], diff0[:, :, :], ALU.add).then_inc(own_pool, 1)
                pool.tensor_tensor(changes[:, :, :], changes[:, :, :], diff[:, :, :], ALU.add).then_inc(own_pool, 1)
                pool.tensor_tensor(sizes[:, :, :], sizes[:, :, :], square[:, :, :], ALU.add).then_inc(own_pool, 1)
                pool.wait_ge(own_pool, own + 8)
            pool.sem_inc(s_all, 1)

        NQ = NCH * QUICK
        quick = (QUICK, 0, 0, 0, 0)
        full = (FULL, NQ, NQ - NCH, NQ - NCH, NCH)
        with nc.Block() as block:
            @block.tensor
            def _(pe):
                pe.sem_inc(s_d1, 1)
                tensor_pass(pe, *quick)
                pe.wait_ge(s_bad, 1)
                pe.matmul(dP[:, 0:2], allones[:, :], bad[:, :], start=True, stop=True).then_inc(s_sum, 1)
                pe.wait_ge(s_flag, 1)
                again = pe.value_load(flag[0:1, 0:1], min_val=0, max_val=1)
                with pe.If(again > 0):
                    tensor_pass(pe, *full)
                    pe.wait_ge(s_w2, 2 * NCH + 1)
                pe.nop()

            @block.scalar
            def _(act):
                scalar_pass(act, *quick)
                act.wait_ge(s_flag, 1)
                again = act.value_load(flag[0:1, 0:1], min_val=0, max_val=1)
                with act.If(again > 0):
                    scalar_pass(act, *full)
                    act.wait_ge(s_w2, 2 * NCH + 1)
                act.nop()

            @block.gpsimd
            def _(pool):
                pool.sem_inc(s_diff, 1)
                pool_pass(pool, *quick)
                pool.wait_ge(s_flag, 1)
                again = pool.value_load(flag[0:1, 0:1], min_val=0, max_val=1)
                with pool.If(again > 0):
                    pool_pass(pool, *full)
                    pool.wait_ge(s_w2, 2 * NCH + 1)
                pool.nop()

            @block.vector
            def _(dve):
                dve.memset(allones[:, :], 1.0).then_inc(own_set, 1)
                dve.wait_ge(own_set, 1)
                set_up(dve, True)
                dve.sem_inc(s_w1, 1)
                dve.sem_inc(s_w2, 1)
                vector_pass(dve, *quick)
                own = Chain(dve, own_set, 1 + N_SET)
                dve.wait_ge(s_all, 1)
                own(dve.tensor_reduce(red[:, 0, :], changes[:, :, :], AX.X, ALU.max))
                own(dve.tensor_reduce(red[:, 1, :], changes0[:, :, :], AX.X, ALU.max))
                own(dve.tensor_reduce(red[:, 2, :], sizes[:, :, :], AX.X, ALU.max))
                own.wait()
                own(dve.tensor_scalar(red[:, 3, :], red[:, 1, :], 1.0 / SHRINK ** 2, None, ALU.mult))
                for x, (small, limit) in enumerate(TOLS):
                    own(dve.tensor_scalar(red[:, 4, x:x + 1], red[:, 2, x:x + 1], small ** 2 / NCH, None, ALU.mult))
                    own(dve.tensor_scalar(red[:, 5, x:x + 1], red[:, 2, x:x + 1], ((SHRINK - 1) * limit) ** 2 / NCH, None, ALU.mult))
                own.wait()
                own(dve.tensor_tensor(red[:, 3, :], red[:, 3, :], red[:, 4, :], ALU.max))
                own.wait()
                own(dve.tensor_tensor(red[:, 3, :], red[:, 3, :], red[:, 5, :], ALU.min))
                own.wait()
                own(dve.tensor_tensor(bad[:, :], red[:, 0, :], red[:, 3, :], ALU.is_gt))
                own.wait()
                dve.sem_inc(s_bad, 1)
                dve.wait_ge(s_sum, 1)
                own(dve.tensor_reduce(total[:, :], dP[:, 0:2], AX.X, ALU.add))
                own.wait()
                own(dve.tensor_scalar(flag[:, :], total[:, :], 0.5, None, ALU.is_gt))
                own.wait()
                own(dve.memset(M.spare[:, 0:1], 0.0))
                assert own.n == N_CHECK, own.n
                dve.sem_inc(s_flag, 1)
                again = dve.value_load(flag[0:1, 0:1], min_val=0, max_val=1)
                with dve.If(again > 0):
                    set_up(dve, False)
                    vector_pass(dve, *full)
                dve.nop()


def answer(nc, M):
    with ExitStack() as ctx:
        S = Scratch(nc, ctx, "l6c")
        tail = Tail(S)
        qP, hP, oP = (S.ps(n, [P, BL]) for n in ("qP", "hP", "oP"))
        yP = S.ps("yP", [P, TB, P])
        q, hs, yT = (S.sb(n, [P, BL]) for n in ("q", "hidden", "yT"))
        s_qP = S.sem("q_in_psum")
        s_q = S.sem("q_ready")
        s_hP = S.sem("hidden_in_psum")
        s_h = S.sem("hidden_ready")
        s_oP = S.sem("o_in_psum")
        s_yT = S.sem("yT_ready")
        s_yfree = S.sem("yP_used")
        own_dve = S.sem("own_dve")
        PER = 14
        with nc.Block() as block:
            @block.tensor
            def _(pe):
                def query(i):
                    hT = M.hT[:, i * BL:(i + 1) * BL] if isinstance(i, int) else M.hT[:, bass.ds(i * BL, BL)]
                    pe.matmul(qP[:, :], M.w("t_q"), hT, start=True, stop=True).then_inc(s_qP, 1)

                def body(i, more):
                    pe.wait_ge(s_q, i + 1)
                    pe.matmul(hP[:, :], M.W1[:, :], q[:, :], start=True, stop=True).then_inc(s_hP, 1)
                    if more:
                        query(i + 1)
                    pe.wait_ge(s_h, i + 1)
                    pe.matmul(oP[:, :], M.W2h[:, :], hs[:, :], start=True, stop=True).then_inc(s_oP, 1)
                    pe.wait_ge(s_yT, i + 1)
                    pe.wait_ge(s_yfree, i + 1)
                    for j in range(TB):
                        last = pe.transpose(yP[:, j, :], yT[:, j * P:(j + 1) * P], M.eye)
                    last.then_inc(tail.y, 1)

                query(0)
                blocks(pe, body)

            @block.scalar
            def _(act):
                def query(i):
                    act.wait_ge(s_qP, i + 1)
                    act.copy(q[:, :], qP[:, :]).then_inc(s_q, 1)

                def body(i, more):
                    act.wait_ge(s_hP, i + 1)
                    act.activation(hs[:, :], hP[:, :], ACT.Silu, bias=M.b1[:, :]).then_inc(s_h, 1)
                    if more:
                        query(i + 1)
                    act.wait_ge(s_oP, i + 1)
                    act.activation(yT[:, :], oP[:, :], ACT.Identity, scale=2.0, bias=M.b2[:, :]).then_inc(s_yT, 1)

                query(0)
                blocks(act, body)

            @block.gpsimd
            def _(pool):
                with pool.Fori(0, NB) as i:
                    tail.pool(pool, M, i)

            @block.vector
            def _(dve):
                dve.sem_inc(s_yfree, 1)
                with dve.Fori(0, NB) as i:
                    own = Chain(dve, own_dve, i * PER)
                    tail.dve(dve, M, own, lambda j: yP[:, j, :], i)
                    dve.sem_inc(s_yfree, 1)
                    assert own.n == PER, own.n


def build(nc, x, w, experts_w, rows, causal, out, layers=range(8)):
    with ExitStack() as ctx:
        M = Mem()
        M.ctx = ctx
        M.experts_w = experts_w
        load(nc, M, x, w, rows, causal)
        for n in layers:
            LAYERS[n](nc, M)
        store(nc, M, out)


LAYERS = [head_mix, causal_moe, long_conv, spiking_layer, surprise_memory, channel_mix, test_time_mlp, last_layer]


def host_layout(i):
    f = np.float32
    a = {k: np.asarray(v) for k, v in i.items()}
    part = {}
    part["eye"] = np.eye(P, dtype=f)
    part["l0_qkv"] = a["L0_attn_Wqkv"].T
    part["l0_proj"] = a["L0_attn_Wproj"].T
    for k, n in (("m_ln1w", "L0_ffn_ln1_w"), ("m_ln1b", "L0_ffn_ln1_b"), ("m_ln2w", "L0_ffn_ln2_w"),
                 ("m_ln2b", "L0_ffn_ln2_b"), ("c_ba", "L1_attn_b_a"), ("c_bb", "L1_attn_b_b"),
                 ("r_mur", "L2_ffn_mu_r"), ("r_muk", "L2_ffn_mu_k"), ("t_b1", "L3_attn_b1"), ("t_b2", "L3_attn_b2")):
        part[k] = a[n].reshape(P, 1)
    part["m_conv"] = a["L0_ffn_conv_w"].reshape(P, 3)
    part["m_qkv"] = a["L0_ffn_attn_w"]
    part["m_proj"] = a["L0_ffn_proj_w"]
    part["m_router"] = a["L0_ffn_router_w"]
    inv = (f(1.0) / np.power(f(10000.0), np.arange(0, D, 2, dtype=f) / f(D))).astype(f)
    ang = np.arange(T, dtype=f)[:, None] * inv[None, :]
    for k, fn in (("cos", np.cos), ("sin", np.sin)):
        part[k] = fn(ang).astype(f).reshape(NT, P, D // 2).transpose(1, 0, 2).reshape(P, -1)
    wv = a["L0_ffn_expert_wv"].transpose(1, 0, 2).reshape(P, -1)
    ep = a["L0_ffn_expert_proj"].reshape(NE, FC, P, P).transpose(2, 0, 1, 3).reshape(P, -1)
    experts_w = np.concatenate([wv, ep], axis=1)
    part["c_in"] = a["L1_attn_w_in"].T
    bi = a["L1_attn_b_in"].reshape(8, 1, 32)
    part["c_inb"] = np.concatenate([bi] * 4, axis=1).reshape(8, P).T
    taps = np.stack([a["L1_attn_w_a"].reshape(P, CK), a["L1_attn_w_b"].reshape(P, CK)])[:, :, ::-1]
    part["c_taps"] = taps.reshape(2, 4, 32, 8, 4).transpose(4, 2, 0, 1, 3).reshape(P, 64)
    part["c_diag"] = np.concatenate([np.eye(32, dtype=f)] * 4, axis=0)
    part["c_out"] = a["L1_attn_w_out"].T.reshape(2, P, P).transpose(1, 0, 2).reshape(P, -1)
    part["s_fc"] = a["L1_ffn_W_fc"].T
    part["s_proj"] = a["L1_ffn_W_proj"].T.reshape(FC, P, P).transpose(1, 0, 2).reshape(P, -1)
    part["g_q"], part["g_k"] = a["L2_attn_Wq"].T, a["L2_attn_Wk"].T
    wv = a["L2_attn_Wv"].T.reshape(P, H, D)
    part["g_v"] = np.stack([np.stack([wv[:, :, j]] * D, axis=2) for j in range(D)], axis=1).reshape(P, -1)
    part["g_m1"] = a["L2_attn_Wm1"].T
    z = lambda m: np.concatenate([m, np.zeros((P - m.shape[0], m.shape[1]), f)], axis=0)
    part["g_bm1"] = z(a["L2_attn_bm1"].reshape(32, 1))
    part["g_m2"] = z(np.stack([a["L2_attn_Wm2"].T] * D, axis=2).reshape(32, P))
    part["g_bm2"] = np.stack([a["L2_attn_bm2"]] * D, axis=1).reshape(P, 1)
    wp = a["L2_attn_Wproj"].T.reshape(H, D, P)
    part["g_proj"] = np.stack([np.stack([wp[:, j]] * D, axis=1).reshape(P, P) for j in range(D)], axis=1).reshape(P, -1)
    part["g_fc"] = a["L2_attn_Wfc"].T
    part["g_cp"] = a["L2_attn_Wcp"].T.reshape(FC, P, P).transpose(1, 0, 2).reshape(P, -1)
    part["r_r"], part["r_k"], part["r_v"] = a["L2_ffn_W_r"].T, a["L2_ffn_W_k"].T, a["L2_ffn_W_v"].T
    part["t_q"], part["t_kv"] = a["L3_attn_W_Q"], a["L3_attn_W_KV"]
    part["t_w1"], part["t_w2"], part["t_w2t"] = a["L3_attn_W1"], a["L3_attn_W2"], a["L3_attn_W2"].T
    part["t_before"] = np.triu(np.ones((P, P), f), 1)
    part["f_w1"] = a["L3_ffn_w1"]
    part["f_b1"] = a["L3_ffn_b1"].reshape(FC, P).T
    part["f_w2"] = a["L3_ffn_w2"].reshape(FC, P, P).transpose(1, 0, 2).reshape(P, -1)
    w = np.concatenate([part[n] for n, _ in PACK], axis=1)
    rows = np.concatenate([a["L0_attn_bproj"], a["L1_attn_b_out"], a["L3_ffn_b2"]]).reshape(1, -1)
    x = a["L0_attn_x"].reshape(T, P)
    return {"x": x, "w": w, "experts_w": experts_w, "rows": rows}


def kernel(**inputs):
    import concourse.bacc as _bacc
    from concourse.bass_utils import run_bass_kernel_spmd as _run

    arrays = host_layout(inputs)
    arrays["causal"] = np.triu(np.full((P, P), NEG, np.float32), 1).astype(mybir.dt.np(BF16))
    nc = _bacc.Bacc("TRN2", target_bir_lowering=False, num_devices=1)
    arrays = {f"in_{k}_dram": np.ascontiguousarray(v) for k, v in arrays.items()}
    args = [nc.dram_tensor(k, v.shape, mybir.dt.from_np(v.dtype), kind="ExternalInput").ap() for k, v in arrays.items()]
    out = nc.dram_tensor("out_0_dram", (T, P), F32, kind="ExternalOutput").ap()
    build(nc, *args, out)
    r = _run(nc, [arrays], core_ids=[0])
    return r.results[0]["out_0_dram"].reshape(1, T, P)
```
